# Optimizing a Trainium2 kernel written in Bass

```python
import numpy as np
import jax
import jax.numpy as jnp

def _softmax(x, axis=-1):
    return jax.nn.softmax(x, axis=axis)

def _gelu(x):
    return jax.nn.gelu(x, approximate=True)

def _silu(x):
    return jax.nn.silu(x)

def _sigmoid(x):
    return jax.nn.sigmoid(x)

def _layernorm(x, axis=-1, eps=1e-05):
    m = jnp.mean(x, axis=axis, keepdims=True)
    v = jnp.var(x, axis=axis, keepdims=True)
    return (x - m) / jnp.sqrt(v + eps)

def _scatter_add(tgt, idx, src, axis=0):
    return tgt.at[idx].add(src)

def _segment_sum(src, seg, n):
    return jax.ops.segment_sum(src, seg, n)
kernel_name = 'mk_decoder_preln_d2_seqx_r8_218dac'

def setup_inputs(seed: int=0):
    np.random.seed(seed)
    _w = jnp.asarray

    def _rec_inputs():
        import jax
        import jax.numpy as jnp
        _rk = jax.random.key(seed)
        x = -0.0003929 + 0.9999 * jax.random.normal(jax.random.fold_in(_rk, 1), (8, 256, 128), jnp.float32)
        _lenS = 256 - jax.random.randint(jax.random.fold_in(_rk, 7), (8,), 0, max(1, 256 // 4) + 1, jnp.int32)
        _lenS2 = 256 - jax.random.randint(jax.random.fold_in(_rk, 8), (8,), 0, max(1, 256 // 4) + 1, jnp.int32)
        _ctx_2048P = jax.random.normal(jax.random.fold_in(_rk, 11), (8, 16, 256), jnp.float32)
        _ctx_2048c = jax.random.dirichlet(jax.random.fold_in(_rk, 511), 0.3 * jnp.ones((16,), jnp.float32), (8, 256))
        _ctx_2048t = jnp.einsum('bsk,bkd->bsd', _ctx_2048c, _ctx_2048P)
        _ctx_2048t = _ctx_2048t * jax.lax.rsqrt(jnp.mean(jnp.square(_ctx_2048t)) + 1e-12) * 0.953939
        ctx_2048 = 4.13588e-05 + 0.999923 * (_ctx_2048t + 0.3 * jax.random.normal(jax.random.fold_in(_rk, 611), (8, 256, 256), jnp.float32))
        _validS = jnp.arange(256)[None, :] < _lenS[:, None]
        _validS2 = jnp.arange(256)[None, :] < _lenS2[:, None]
        _causal = jnp.tril(jnp.ones((256, 256), dtype=bool))
        mask_BxS2_if0 = jnp.where(jnp.ones((8, 256), dtype=bool), 4, 0).astype(jnp.int32)
        mask_BxS2_fk1 = jnp.where(jnp.broadcast_to(_validS2[:, :], (8, 256)), 1.0, 0.0).astype(jnp.float32)
        return (x, ctx_2048, mask_BxS2_if0, mask_BxS2_fk1)
    x, ctx_2048, mask_BxS2_if0, mask_BxS2_fk1 = _rec_inputs()

    def _L0_attn_setup():
        import jax, jax.numpy as jnp
        import numpy as np
        D_MODEL = 128
        NUM_HEADS = 4
        HEAD_QK = 32
        HEAD_V = 64
        EPS = 1e-05
        ROPE_BASE = 10000.0

        def _apply_rotary(q, k):
            T, d = (q.shape[1], q.shape[-1])
            half = d // 2
            inv_freq = 1.0 / ROPE_BASE ** (jnp.arange(0, d, 2, dtype=jnp.float32) / d)
            freqs = jnp.arange(T, dtype=jnp.float32)[:, None] * inv_freq[None, :]
            cos = jnp.cos(freqs)[None, :, None, :]
            sin = jnp.sin(freqs)[None, :, None, :]

            def rot(x):
                x1, x2 = (x[..., :half], x[..., half:])
                return jnp.concatenate([x1 * cos - x2 * sin, x1 * sin + x2 * cos], axis=-1)
            return (rot(q), rot(k))
        key = jax.random.key(seed)
        ks = jax.random.split(key, 7)
        B, T = (2, 256)
        key_dim = NUM_HEADS * HEAD_QK
        value_dim = NUM_HEADS * HEAD_V
        s = 0.02
        return {'x': jax.random.normal(ks[0], (B, T, D_MODEL), jnp.float32), 'Wq': jax.random.normal(ks[1], (key_dim, D_MODEL), jnp.float32) * s, 'Wk': jax.random.normal(ks[2], (key_dim, D_MODEL), jnp.float32) * s, 'Wv': jax.random.normal(ks[3], (value_dim, D_MODEL), jnp.float32) * s, 'Wg': jax.random.normal(ks[4], (value_dim, D_MODEL), jnp.float32) * s, 'Wo': jax.random.normal(ks[5], (D_MODEL, value_dim), jnp.float32) * s, 'g_norm_w': jnp.ones((HEAD_V,), jnp.float32)}
    _L0_attn_all = _L0_attn_setup()
    _L0_attn_in = {k: v for k, v in _L0_attn_all.items() if k in ('Wq', 'Wk', 'Wv', 'Wg', 'Wo', 'g_norm_w')}
    del _L0_attn_all

    def _L0_xattn_setup():
        import jax, jax.numpy as jnp
        import numpy as np
        B, L, P = (4, 512, 128)
        D_MODEL = 128
        D_GLOBAL = 256
        HEADDIM = 32
        EPSILON = 0.001
        RMS_EPS = 1e-05

        def rmsnorm(x, g, eps=RMS_EPS):
            var = jnp.mean(jnp.square(x), axis=-1, keepdims=True)
            return x * jax.lax.rsqrt(var + eps) * g

        def _hnet_depool(h, h_patch_full, patch_lens):
            h_patch = h_patch_full[..., :D_MODEL]
            bsz, plen = (h_patch.shape[0], h_patch.shape[1])
            seqlen = h.shape[1]
            logp = jnp.full((bsz, plen), -EPSILON, dtype=jnp.float32)
            bidx = jnp.cumsum(patch_lens, axis=1) - 1
            boundary_mask = jnp.zeros((bsz, seqlen), dtype=jnp.int32)
            boundary_mask = boundary_mask.at[jnp.arange(bsz)[:, None], bidx].set(1)
            dt = (-jnp.log(-jnp.expm1(logp))).astype(h_patch.dtype)
            x = h_patch / dt[..., None]
            n_heads = D_MODEL // HEADDIM
            A = -jnp.ones((n_heads,), dtype=jnp.float32)
            bcoef = jnp.exp(logp).astype(h_patch.dtype)
            x4 = x.reshape(bsz, plen, n_heads, HEADDIM)
            a = jnp.exp(dt[:, :, None] * A[None, None, :])
            u = (dt * bcoef)[:, :, None, None] * x4
            a_b = jnp.broadcast_to(a[..., None], u.shape)

            def comb(lft, rgt):
                aL, uL = lft
                aR, uR = rgt
                return (aL * aR, uL * aR + uR)
            _, s = jax.lax.associative_scan(comb, (a_b, u), axis=1)
            depool = s.reshape(bsz, plen, D_MODEL)
            plug = jnp.clip(jnp.cumsum(boundary_mask, axis=1) - 1, 0, plen - 1)
            depool_out = depool[jnp.arange(bsz)[:, None], plug]
            return depool_out + h
        key = jax.random.key(seed)
        k1, k2, k3, k4 = jax.random.split(key, 4)
        embeds = jax.random.normal(k1, (B, L, D_MODEL), dtype=jnp.float32)
        patch_embeds = jax.random.normal(k2, (B, P, D_GLOBAL), dtype=jnp.float32)
        patch_lens = jnp.full((B, P), L // P, dtype=jnp.int64)
        W_in = jax.random.normal(k3, (D_MODEL, D_MODEL), dtype=jnp.float32) * 0.02
        b_in = jnp.zeros((D_MODEL,), dtype=jnp.float32)
        g_res = jnp.ones((D_MODEL,), dtype=jnp.float32)
        g_init = jnp.ones((D_GLOBAL,), dtype=jnp.float32)
        return {'embeds': embeds, 'patch_embeds': patch_embeds, 'patch_lens': patch_lens, 'W_in': W_in, 'b_in': b_in, 'g_res': g_res, 'g_init': g_init}
    _L0_xattn_all = _L0_xattn_setup()
    _L0_xattn_in = {k: v for k, v in _L0_xattn_all.items() if k in ('W_in', 'b_in', 'g_res', 'g_init')}
    del _L0_xattn_all

    def _L0_ffn_setup():
        import jax, jax.numpy as jnp
        import numpy as np
        S, B, H = (256, 1, 128)
        E, K, F = (8, 2, 176)
        key = jax.random.key(seed)
        k1, k2, k3, k4 = jax.random.split(key, 4)
        return {'hidden_states': jax.random.normal(k1, (S, B, H), jnp.float32), 'router_weight': jax.random.normal(k2, (H, E), jnp.float32) * 0.02, 'w1': jax.random.normal(k3, (E, H, 2 * F), jnp.float32) * 0.02, 'w2': jax.random.normal(k4, (E, F, H), jnp.float32) * 0.02}
    _L0_ffn_all = _L0_ffn_setup()
    _L0_ffn_in = {k: v for k, v in _L0_ffn_all.items() if k in ('router_weight', 'w1', 'w2')}
    del _L0_ffn_all

    def _L1_attn_setup():
        import jax, jax.numpy as jnp
        import numpy as np
        import math
        D_MODEL = 128
        D_STATE = 64
        DT_MIN, DT_MAX = (0.001, 0.1)
        key = jax.random.key(seed)
        ks = jax.random.split(key, 8)
        x = jax.random.normal(ks[0], (2, 512, D_MODEL), dtype=jnp.float32)
        lim = 1.0 / math.sqrt(D_MODEL)
        Win = jax.random.uniform(ks[1], (D_MODEL, D_MODEL), minval=-lim, maxval=lim, dtype=jnp.float32)
        bin_ = jax.random.uniform(ks[2], (D_MODEL,), minval=-lim, maxval=lim, dtype=jnp.float32)
        Wout = jax.random.uniform(ks[3], (D_MODEL, D_MODEL), minval=-lim, maxval=lim, dtype=jnp.float32)
        bout = jax.random.uniform(ks[4], (D_MODEL,), minval=-lim, maxval=lim, dtype=jnp.float32)
        A_log = jnp.broadcast_to(jnp.log(jnp.arange(1, D_STATE + 1, dtype=jnp.float32)), (D_MODEL, D_STATE))
        B = 0.1 * jax.random.normal(ks[5], (D_MODEL, D_STATE), dtype=jnp.float32)
        C = 0.1 * jax.random.normal(ks[6], (D_MODEL, D_STATE), dtype=jnp.float32)
        Dp = jnp.ones((D_MODEL,), dtype=jnp.float32)
        log_dt = jax.random.uniform(ks[7], (D_MODEL,), dtype=jnp.float32) * (math.log(DT_MAX) - math.log(DT_MIN)) + math.log(DT_MIN)
        dt = jnp.exp(log_dt)
        return {'x': x, 'Win': Win, 'bin_': bin_, 'A_log': A_log, 'B': B, 'C': C, 'Dp': Dp, 'dt': dt, 'Wout': Wout, 'bout': bout}
    _L1_attn_all = _L1_attn_setup()
    _L1_attn_in = {k: v for k, v in _L1_attn_all.items() if k in ('Win', 'bin_', 'A_log', 'B', 'C', 'Dp', 'dt', 'Wout', 'bout')}
    del _L1_attn_all

    def _L1_xattn_setup():
        import jax, jax.numpy as jnp
        import numpy as np
        B, S, T = (32, 64, 64)
        SRC_SIZE, TGT_SIZE, OUT_SIZE, NUM_HEAD = (256, 128, 128, 8)
        HEAD_DIM = OUT_SIZE // NUM_HEAD
        key = jax.random.key(seed)
        ks = jax.random.split(key, 12)
        src = jax.random.normal(ks[0], (B, S, SRC_SIZE), dtype=jnp.float32)
        tgt = jax.random.normal(ks[1], (B, T, TGT_SIZE), dtype=jnp.float32)
        src_mask = (jax.random.uniform(ks[2], (B, S)) > 0.3).astype(jnp.float32)
        src_mask = src_mask.at[:, 0].set(1.0)
        tgt_mask = (jax.random.uniform(ks[3], (B, T)) > 0.3).astype(jnp.float32)
        tgt_mask = tgt_mask.at[:, 0].set(1.0)

        def lin(k, out_f, in_f):
            return jax.random.normal(k, (out_f, in_f), dtype=jnp.float32) / np.sqrt(in_f)
        W_src = lin(ks[4], 2 * OUT_SIZE, SRC_SIZE)
        b_src = jnp.zeros((2 * OUT_SIZE,), jnp.float32)
        W_tgt = lin(ks[5], OUT_SIZE, TGT_SIZE)
        b_tgt = jnp.zeros((OUT_SIZE,), jnp.float32)
        W_out = lin(ks[6], OUT_SIZE, OUT_SIZE + TGT_SIZE)
        b_out = jnp.zeros((OUT_SIZE,), jnp.float32)
        return {'src': src, 'tgt': tgt, 'src_mask': src_mask, 'tgt_mask': tgt_mask, 'W_src': W_src, 'b_src': b_src, 'W_tgt': W_tgt, 'b_tgt': b_tgt, 'W_out': W_out, 'b_out': b_out}
    _L1_xattn_all = _L1_xattn_setup()
    _L1_xattn_in = {k: v for k, v in _L1_xattn_all.items() if k in ('W_src', 'b_src', 'W_tgt', 'b_tgt', 'W_out', 'b_out')}
    del _L1_xattn_all

    def _L1_ffn_setup():
        import jax, jax.numpy as jnp
        import numpy as np
        B, S, D, F, E, K = (4, 256, 128, 512, 8, 2)
        FS = 128
        LN_EPS = 1e-05

        def _swiglu(x, gu_w, dn_w):
            gate, up = jnp.split(x @ gu_w, 2, axis=-1)
            gate = jnp.clip(gate, -10.0, 10.0)
            return jax.nn.silu(gate) * up @ dn_w
        key = jax.random.key(seed)
        ks = jax.random.split(key, 6)
        s = 0.02
        return {'x': jax.random.normal(ks[0], (B, S, D), jnp.float32), 'ln_gamma': jnp.ones((D,), jnp.float32), 'ln_beta': jnp.zeros((D,), jnp.float32), 'router_w': jax.random.normal(ks[1], (D, E), jnp.float32) * s, 'gate_up_w': jax.random.normal(ks[2], (E, D, 2 * F), jnp.float32) * s, 'down_w': jax.random.normal(ks[3], (E, F, D), jnp.float32) * s, 'shared_gate_up_w': jax.random.normal(ks[4], (D, 2 * FS), jnp.float32) * s, 'shared_down_w': jax.random.normal(ks[5], (FS, D), jnp.float32) * s}
    _L1_ffn_all = _L1_ffn_setup()
    _L1_ffn_in = {k: v for k, v in _L1_ffn_all.items() if k in ('ln_gamma', 'ln_beta', 'router_w', 'gate_up_w', 'down_w', 'shared_gate_up_w', 'shared_down_w')}
    del _L1_ffn_all
    return {'x': x, 'ctx_2048': ctx_2048, 'mask_BxS2_if0': mask_BxS2_if0, 'mask_BxS2_fk1': mask_BxS2_fk1, 'L0_attn_Wq': _L0_attn_in['Wq'], 'L0_attn_Wk': _L0_attn_in['Wk'], 'L0_attn_Wv': _L0_attn_in['Wv'], 'L0_attn_Wg': _L0_attn_in['Wg'], 'L0_attn_Wo': _L0_attn_in['Wo'], 'L0_attn_g_norm_w': _L0_attn_in['g_norm_w'], 'L0_xattn_W_in': _L0_xattn_in['W_in'], 'L0_xattn_b_in': _L0_xattn_in['b_in'], 'L0_xattn_g_res': _L0_xattn_in['g_res'], 'L0_xattn_g_init': _L0_xattn_in['g_init'], 'L0_ffn_router_weight': _L0_ffn_in['router_weight'], 'L0_ffn_w1': _L0_ffn_in['w1'], 'L0_ffn_w2': _L0_ffn_in['w2'], 'L1_attn_Win': _L1_attn_in['Win'], 'L1_attn_bin_': _L1_attn_in['bin_'], 'L1_attn_A_log': _L1_attn_in['A_log'], 'L1_attn_B': _L1_attn_in['B'], 'L1_attn_C': _L1_attn_in['C'], 'L1_attn_Dp': _L1_attn_in['Dp'], 'L1_attn_dt': _L1_attn_in['dt'], 'L1_attn_Wout': _L1_attn_in['Wout'], 'L1_attn_bout': _L1_attn_in['bout'], 'L1_xattn_W_src': _L1_xattn_in['W_src'], 'L1_xattn_b_src': _L1_xattn_in['b_src'], 'L1_xattn_W_tgt': _L1_xattn_in['W_tgt'], 'L1_xattn_b_tgt': _L1_xattn_in['b_tgt'], 'L1_xattn_W_out': _L1_xattn_in['W_out'], 'L1_xattn_b_out': _L1_xattn_in['b_out'], 'L1_ffn_ln_gamma': _L1_ffn_in['ln_gamma'], 'L1_ffn_ln_beta': _L1_ffn_in['ln_beta'], 'L1_ffn_router_w': _L1_ffn_in['router_w'], 'L1_ffn_gate_up_w': _L1_ffn_in['gate_up_w'], 'L1_ffn_down_w': _L1_ffn_in['down_w'], 'L1_ffn_shared_gate_up_w': _L1_ffn_in['shared_gate_up_w'], 'L1_ffn_shared_down_w': _L1_ffn_in['shared_down_w']}

def reference(x, ctx_2048, mask_BxS2_if0, mask_BxS2_fk1, L0_attn_Wq, L0_attn_Wk, L0_attn_Wv, L0_attn_Wg, L0_attn_Wo, L0_attn_g_norm_w, L0_xattn_W_in, L0_xattn_b_in, L0_xattn_g_res, L0_xattn_g_init, L0_ffn_router_weight, L0_ffn_w1, L0_ffn_w2, L1_attn_Win, L1_attn_bin_, L1_attn_A_log, L1_attn_B, L1_attn_C, L1_attn_Dp, L1_attn_dt, L1_attn_Wout, L1_attn_bout, L1_xattn_W_src, L1_xattn_b_src, L1_xattn_W_tgt, L1_xattn_b_tgt, L1_xattn_W_out, L1_xattn_b_out, L1_ffn_ln_gamma, L1_ffn_ln_beta, L1_ffn_router_w, L1_ffn_gate_up_w, L1_ffn_down_w, L1_ffn_shared_gate_up_w, L1_ffn_shared_down_w):
    import jax
    import jax.numpy as jnp

    def _L0_attn_ref(x, Wq, Wk, Wv, Wg, Wo, g_norm_w):
        import jax, jax.numpy as jnp
        import numpy as np
        D_MODEL = 128
        NUM_HEADS = 4
        HEAD_QK = 32
        HEAD_V = 64
        EPS = 1e-05
        ROPE_BASE = 10000.0

        def _apply_rotary(q, k):
            T, d = (q.shape[1], q.shape[-1])
            half = d // 2
            inv_freq = 1.0 / ROPE_BASE ** (jnp.arange(0, d, 2, dtype=jnp.float32) / d)
            freqs = jnp.arange(T, dtype=jnp.float32)[:, None] * inv_freq[None, :]
            cos = jnp.cos(freqs)[None, :, None, :]
            sin = jnp.sin(freqs)[None, :, None, :]

            def rot(x):
                x1, x2 = (x[..., :half], x[..., half:])
                return jnp.concatenate([x1 * cos - x2 * sin, x1 * sin + x2 * cos], axis=-1)
            return (rot(q), rot(k))
        B, T, _ = x.shape
        H, dk, dv = (NUM_HEADS, HEAD_QK, HEAD_V)
        q = (x @ Wq.T).reshape(B, T, H, dk)
        k = (x @ Wk.T).reshape(B, T, H, dk)
        q, k = _apply_rotary(q, k)
        q = jnp.transpose(q, (0, 2, 1, 3))
        k = jnp.transpose(k, (0, 2, 1, 3))
        v = jnp.transpose((x @ Wv.T).reshape(B, T, H, dv), (0, 2, 1, 3))
        q = q * dk ** (-0.5)
        log_decay = jnp.log1p(-jnp.exp2(-5.0 - jnp.arange(H, dtype=jnp.float32)))
        t = jnp.arange(T, dtype=jnp.float32)
        diff = t[:, None] - t[None, :]
        decay_mask = jnp.where(diff >= 0, jnp.exp(log_decay[:, None, None] * diff[None]), 0.0)
        scores = jnp.einsum('bhtd,bhsd->bhts', q, k) * decay_mask[None]
        o = jnp.einsum('bhts,bhsd->bhtd', scores, v)
        o = jnp.transpose(o, (0, 2, 1, 3))
        rms = jax.lax.rsqrt(jnp.mean(o * o, axis=-1, keepdims=True) + EPS)
        o_n = o * rms * g_norm_w
        g = (x @ Wg.T).reshape(B, T, H, dv)
        o_g = o_n * (g * jax.nn.sigmoid(g))
        return o_g.reshape(B, T, H * dv) @ Wo.T

    def _L0_xattn_ref(embeds, patch_embeds, patch_lens, W_in, b_in, g_res, g_init):
        import jax, jax.numpy as jnp
        import numpy as np
        B, L, P = (4, 512, 128)
        D_MODEL = 128
        D_GLOBAL = 256
        HEADDIM = 32
        EPSILON = 0.001
        RMS_EPS = 1e-05

        def rmsnorm(x, g, eps=RMS_EPS):
            var = jnp.mean(jnp.square(x), axis=-1, keepdims=True)
            return x * jax.lax.rsqrt(var + eps) * g

        def _hnet_depool(h, h_patch_full, patch_lens):
            h_patch = h_patch_full[..., :D_MODEL]
            bsz, plen = (h_patch.shape[0], h_patch.shape[1])
            seqlen = h.shape[1]
            logp = jnp.full((bsz, plen), -EPSILON, dtype=jnp.float32)
            bidx = jnp.cumsum(patch_lens, axis=1) - 1
            boundary_mask = jnp.zeros((bsz, seqlen), dtype=jnp.int32)
            boundary_mask = boundary_mask.at[jnp.arange(bsz)[:, None], bidx].set(1)
            dt = (-jnp.log(-jnp.expm1(logp))).astype(h_patch.dtype)
            x = h_patch / dt[..., None]
            n_heads = D_MODEL // HEADDIM
            A = -jnp.ones((n_heads,), dtype=jnp.float32)
            bcoef = jnp.exp(logp).astype(h_patch.dtype)
            x4 = x.reshape(bsz, plen, n_heads, HEADDIM)
            a = jnp.exp(dt[:, :, None] * A[None, None, :])
            u = (dt * bcoef)[:, :, None, None] * x4
            a_b = jnp.broadcast_to(a[..., None], u.shape)

            def comb(lft, rgt):
                aL, uL = lft
                aR, uR = rgt
                return (aL * aR, uL * aR + uR)
            _, s = jax.lax.associative_scan(comb, (a_b, u), axis=1)
            depool = s.reshape(bsz, plen, D_MODEL)
            plug = jnp.clip(jnp.cumsum(boundary_mask, axis=1) - 1, 0, plen - 1)
            depool_out = depool[jnp.arange(bsz)[:, None], plug]
            return depool_out + h
        h = rmsnorm(embeds, g_res)
        h = jnp.einsum('bld,ed->ble', h, W_in) + b_in
        h_patch = rmsnorm(patch_embeds, g_init)
        return _hnet_depool(h, h_patch, patch_lens)

    def _L0_ffn_ref(hidden_states, router_weight, w1, w2):
        import jax, jax.numpy as jnp
        import numpy as np
        S, B, H = (256, 1, 128)
        E, K, F = (8, 2, 176)
        s, b, h = hidden_states.shape
        x = hidden_states.reshape(-1, h)
        logits = x @ router_weight
        probs = jax.nn.softmax(logits, axis=-1)
        _, topk_idx = jax.lax.top_k(probs, K)
        routing_map = jax.nn.one_hot(topk_idx, E, dtype=probs.dtype).sum(axis=1)
        local_probs = probs * routing_map
        y = jnp.einsum('th,ehf->tef', x, w1)
        y1, y2 = jnp.split(y, 2, axis=-1)
        g = jax.nn.silu(y1) * y2
        o = jnp.einsum('tef,efh->teh', g, w2)
        out = jnp.einsum('teh,te->th', o, local_probs)
        return out.reshape(s, b, h)

    def _L1_attn_ref(x, Win, bin_, A_log, B, C, Dp, dt, Wout, bout):
        import jax, jax.numpy as jnp
        import numpy as np
        import math
        D_MODEL = 128
        D_STATE = 64
        DT_MIN, DT_MAX = (0.001, 0.1)
        b, L, d = x.shape
        x = x @ Win.T + bin_
        u = jnp.transpose(x, (0, 2, 1))
        A = -jnp.exp(-A_log)
        logdA = A * dt[:, None]
        dB = B * dt[:, None]
        t = jnp.arange(L, dtype=x.dtype)
        powers = jnp.exp(logdA[:, :, None] * t)
        k = jnp.einsum('dn,dnl->dl', C * dB, powers)
        n_fft = 2 * L
        k_f = jnp.fft.rfft(k, n=n_fft)
        u_f = jnp.fft.rfft(u, n=n_fft)
        y = jnp.fft.irfft(u_f * k_f[None], n=n_fft)[..., :L]
        y = y + u * Dp[:, None]
        y = jnp.transpose(y, (0, 2, 1))
        return y @ Wout.T + bout

    def _L1_xattn_ref(src, tgt, src_mask, tgt_mask, W_src, b_src, W_tgt, b_tgt, W_out, b_out):
        import jax, jax.numpy as jnp
        import numpy as np
        B, S, T = (32, 64, 64)
        SRC_SIZE, TGT_SIZE, OUT_SIZE, NUM_HEAD = (256, 128, 128, 8)
        HEAD_DIM = OUT_SIZE // NUM_HEAD
        b, s, _ = src.shape
        t = tgt.shape[1]
        src_trans = jnp.einsum('bsf,of->bso', src, W_src) + b_src
        tgt_trans = jnp.einsum('btf,of->bto', tgt, W_tgt) + b_tgt
        src_trans = src_trans * src_mask[:, :, None]
        tgt_trans = tgt_trans * tgt_mask[:, :, None]
        src_key, src_val = jnp.split(src_trans, 2, axis=2)
        k = src_key.reshape(b, s, NUM_HEAD, HEAD_DIM)
        v = src_val.reshape(b, s, NUM_HEAD, HEAD_DIM)
        q = tgt_trans.reshape(b, t, NUM_HEAD, HEAD_DIM)
        scores = jnp.einsum('bthd,bshd->bhts', q, k) / np.sqrt(HEAD_DIM)
        scores = jnp.where(src_mask[:, None, None, :] == 0, -jnp.inf, scores)
        attn = jax.nn.softmax(scores, axis=-1)
        tgt_update = jnp.einsum('bhts,bshd->bthd', attn, v).reshape(b, t, OUT_SIZE)
        cat_tgt = jnp.concatenate([tgt, tgt_update], axis=2)
        return jnp.einsum('btf,of->bto', cat_tgt, W_out) + b_out

    def _L1_ffn_ref(x, ln_gamma, ln_beta, router_w, gate_up_w, down_w, shared_gate_up_w, shared_down_w):
        import jax, jax.numpy as jnp
        import numpy as np
        B, S, D, F, E, K = (4, 256, 128, 512, 8, 2)
        FS = 128
        LN_EPS = 1e-05

        def _swiglu(x, gu_w, dn_w):
            gate, up = jnp.split(x @ gu_w, 2, axis=-1)
            gate = jnp.clip(gate, -10.0, 10.0)
            return jax.nn.silu(gate) * up @ dn_w
        b, s, d = x.shape
        xf = x.reshape(-1, d)
        mu = jnp.mean(xf, axis=-1, keepdims=True)
        var = jnp.var(xf, axis=-1, keepdims=True)
        xn = (xf - mu) * jax.lax.rsqrt(var + LN_EPS) * ln_gamma + ln_beta
        logits = xn @ router_w
        probs = jax.nn.softmax(logits, axis=-1)
        topv, topi = jax.lax.top_k(probs, K)
        topv = topv / jnp.sum(topv, axis=-1, keepdims=True)
        comb = jnp.sum(jax.nn.one_hot(topi, E, dtype=xn.dtype) * topv[..., None], axis=1)
        out = jnp.zeros_like(xf)
        for e in range(E):
            out = out + comb[:, e:e + 1] * _swiglu(xn, gate_up_w[e], down_w[e])
        out = out + _swiglu(xn, shared_gate_up_w, shared_down_w)
        return out.reshape(b, s, d)
    x = x + _L0_attn_ref(_layernorm(x, axis=-1), L0_attn_Wq, L0_attn_Wk, L0_attn_Wv, L0_attn_Wg, L0_attn_Wo, L0_attn_g_norm_w)
    x = x + _L0_xattn_ref(_layernorm(x, axis=-1), ctx_2048, mask_BxS2_if0, L0_xattn_W_in, L0_xattn_b_in, L0_xattn_g_res, L0_xattn_g_init)
    x = x + _L0_ffn_ref(_layernorm(x, axis=-1), L0_ffn_router_weight, L0_ffn_w1, L0_ffn_w2)
    x = x + _L1_attn_ref(_layernorm(x, axis=-1), L1_attn_Win, L1_attn_bin_, L1_attn_A_log, L1_attn_B, L1_attn_C, L1_attn_Dp, L1_attn_dt, L1_attn_Wout, L1_attn_bout)
    x = x + _L1_xattn_ref(ctx_2048, _layernorm(x, axis=-1), mask_BxS2_fk1, mask_BxS2_fk1, L1_xattn_W_src, L1_xattn_b_src, L1_xattn_W_tgt, L1_xattn_b_tgt, L1_xattn_W_out, L1_xattn_b_out)
    x = x + _L1_ffn_ref(_layernorm(x, axis=-1), L1_ffn_ln_gamma, L1_ffn_ln_beta, L1_ffn_router_w, L1_ffn_gate_up_w, L1_ffn_down_w, L1_ffn_shared_gate_up_w, L1_ffn_shared_down_w)
    return x

_drawn_inputs = setup_inputs


def setup_inputs(seed=0):
    import zlib

    import numpy as np

    out = dict(_drawn_inputs(seed))
    spreads = {'L0_attn_g_norm_w': (1.0, 0.6),
     'L0_xattn_b_in': (0.0, 0.1),
     'L0_xattn_g_res': (1.0, 0.2),
     'L0_xattn_g_init': (1.0, 0.2),
     'L1_attn_Dp': (1.0, 0.2),
     'L1_xattn_b_src': (0.0, 0.1),
     'L1_xattn_b_tgt': (0.0, 0.8),
     'L1_xattn_b_out': (0.0, 0.1),
     'L1_ffn_ln_gamma': (1.0, 0.6),
     'L1_ffn_ln_beta': (0.0, 0.8)}
    factors = {'L0_ffn_router_weight': 8.0,
     'L0_ffn_w1': 8.0,
     'L0_ffn_w2': 8.0,
     'L1_attn_bin_': 2.827,
     'L1_attn_A_log': 8.0,
     'L1_attn_dt': 3.572,
     'L1_ffn_router_w': 8.0,
     'L1_ffn_gate_up_w': 8.0,
     'L1_ffn_down_w': 8.0,
     'L1_ffn_shared_gate_up_w': 8.0,
     'L1_ffn_shared_down_w': 8.0}
    for name, (base, spread) in spreads.items():
        noise = np.random.default_rng([zlib.crc32(name.encode()), seed]).standard_normal(out[name].shape)
        drawn = base * np.exp(spread * noise) if base else spread * noise
        out[name] = jnp.asarray(drawn.astype(out[name].dtype))
    for name, factor in factors.items():
        out[name] = (out[name] * factor).astype(out[name].dtype)
    return out
```

```python
from contextlib import ExitStack

import numpy as np

import concourse.bass as bass
from concourse import mybir

ALU = mybir.AluOpType
ACT = mybir.ActivationFunctionType
AX = mybir.AxisListType
F32 = mybir.dt.float32
BF16 = mybir.dt.bfloat16
I32 = mybir.dt.int32
U32 = mybir.dt.uint32

P = 128
B, S, D = 8, 256, 128
DC = 256
NT = B * S // P
PAIR = 4
PAIRS = NT // PAIR
WIDE = PAIR * P
LN_EPS = 1e-5
RSQRT_MAGIC = float(0x5F3759DF)

RH, RQK, RV = 4, 32, 64
CAUSAL = 384
DEPOOL_DT = float(-np.log(-np.expm1(np.float32(-0.001))))
DEPOOL_B = float(np.exp(np.float32(-0.001)))
E = 8
SLOT_TILES = 2 * NT + E
GATE_LIMIT = 10.0
SLOTS = SLOT_TILES * P
F0, F1, FS = 176, 512, 128
N_STATE = 64
FFT = 2 * S
XH, XD = 8, 16
MASKED = -1e30
HEAD_ROWS = 32
MASK_ROW, MAX_ROW = XD, XD + 1
AUX, AUX_MASK, AUX_BIAS, AUX_ONE = 65, 0, 32, 64


LOAD_ORDER = ("ret", "dep", "ffn0", "conv", "xat", "ffn1")


class Steps:

    def __init__(self, core, engine, i=0, per_body=0):
        self.core, self.engine, self.i, self.per_body, self.n = core, engine, i, per_body, 0
        self.sem, self.base = core.vector_steps, core.vector_base

    def done(self, ins):
        self.n += 1
        return ins.then_inc(self.sem, 1)

    def wait(self):
        self.engine.wait_ge(self.sem, self.i * self.per_body + (self.base + self.n))

    def close(self):
        self.core.vector_base += self.n


def rounds(engine, n, body):
    body(0)
    with engine.Fori(1, n) as i:
        body(i)


def wait_last_round(engine, sem, value):
    if not isinstance(value, int):
        engine.wait_ge(sem, value)
    else:
        assert value == 0


def rsqrt(vec, steps, out, v, tmp):
    steps.done(vec.tensor_scalar(tmp.bitcast(I32), v.bitcast(I32), 1, None, ALU.logical_shift_right))
    steps.wait()
    steps.done(vec.tensor_scalar(out.bitcast(I32), tmp.bitcast(I32), -1.0, RSQRT_MAGIC, ALU.mult, ALU.add))
    for _ in range(3):
        steps.wait()
        steps.done(vec.tensor_tensor(tmp, out, out, ALU.mult))
        steps.wait()
        steps.done(vec.scalar_tensor_tensor(out=tmp, in0=tmp, scalar=-0.5, in1=v, op0=ALU.mult, op1=ALU.mult))
        steps.wait()
        steps.done(vec.scalar_tensor_tensor(out=out, in0=tmp, scalar=1.5, in1=out, op0=ALU.add, op1=ALU.mult))


def layer_norm(vec, steps, x, first_tile, st, twice, xn, before_write):
    for j in range(PAIR):
        steps.done(vec.bn_stats(st["raw"][:, j, :], x[:, bass.ds(first_tile + j, 1), :]))
    steps.wait()
    raw, mean, diff, v, r, tmp = (st[k] for k in ("raw", "mean", "diff", "v", "r", "tmp"))
    steps.done(vec.tensor_tensor(mean[:, :], raw[:, :, 1], raw[:, :, 4], ALU.add))
    steps.done(vec.tensor_tensor(diff[:, :], raw[:, :, 1], raw[:, :, 4], ALU.subtract))
    steps.done(vec.tensor_tensor(v[:, :], raw[:, :, 2], raw[:, :, 5], ALU.add))
    steps.wait()
    steps.done(vec.tensor_scalar(mean[:, :], mean[:, :], 0.5, None, ALU.mult))
    steps.done(vec.scalar_tensor_tensor(out=diff[:, :], in0=diff[:, :], scalar=0.25, in1=diff[:, :],
                                        op0=ALU.mult, op1=ALU.mult))
    steps.done(vec.tensor_scalar(v[:, :], v[:, :], 1.0 / D, None, ALU.mult))
    steps.wait()
    steps.done(vec.tensor_tensor(diff[:, :], v[:, :], diff[:, :], ALU.add))
    steps.wait()
    steps.done(vec.tensor_scalar(v[:, :], diff[:, :], LN_EPS, None, ALU.add))
    steps.wait()
    rsqrt(vec, steps, r[:, :], v[:, :], tmp[:, :])
    if twice:
        steps.wait()
        steps.done(vec.tensor_tensor(diff[:, :], diff[:, :], r[:, :], ALU.mult))
        steps.wait()
        steps.done(vec.tensor_tensor(diff[:, :], diff[:, :], r[:, :], ALU.mult))
        steps.wait()
        steps.done(vec.tensor_scalar(v[:, :], diff[:, :], LN_EPS, None, ALU.add))
        steps.wait()
        rsqrt(vec, steps, st["r2"][:, :], v[:, :], tmp[:, :])
        steps.wait()
        steps.done(vec.tensor_tensor(r[:, :], r[:, :], st["r2"][:, :], ALU.mult))
    steps.wait()
    if before_write:
        before_write()
    return [vec.tensor_scalar(xn[:, j, :], x[:, bass.ds(first_tile + j, 1), :], mean[:, j:j + 1], r[:, j:j + 1],
                              ALU.subtract, ALU.mult) for j in range(PAIR)]


LN_STEPS = PAIR + 3 + 3 + 1 + 1 + 11
LN_STEPS_TWICE = LN_STEPS + 3 + 11 + 1


class Core:

    def __init__(self, nc, ctx, arg):
        self.nc, self.ctx, self.arg = nc, ctx, arg
        self.loads = {}
        self.loaded = {}
        self.psum = ctx.enter_context(nc.psum_tensor("psum", [P, 8, 512], F32))
        self.vector_steps, self.vector_base = self.sem("vector_steps"), 0
        self.bank = [self.psum[:, i, :] for i in range(8)]

        self.x = self.preload("ret", "x", [P, NT, D], arg["x"].rearrange("(t p) d -> p t d", p=P))
        self.ident = self.preload("ret", "ident", [P, P], arg["ident"])
        self.ffn = []
        for name, width, chunk in (("ffn0", F0, F0 // 2), ("ffn1", F1, P)):
            chunks = width // chunk
            w = {
                "router": self.preload(name, "router", [P, E], arg[name + "_router"]),
                "up": self.preload(name, "up", [P, E * 2 * width], arg[name + "_up"]),
                "down": self.preload(name, "down", [chunk, E * chunks * D], arg[name + "_down"]),
            }
            if name == "ffn1":
                w["gamma"] = self.preload(name, "gamma", [P, 1], arg["ffn1_gamma"])
                w["beta"] = self.preload(name, "beta", [P, 1], arg["ffn1_beta"])
                w["shared_up"] = self.preload(name, "shared_up", [P, 2 * FS], arg["ffn1_shared_up"])
                w["shared_down"] = self.preload(name, "shared_down", [FS, D], arg["ffn1_shared_down"])
            self.ffn.append(w)
        self.moe_tables = {k: self.preload("ffn0", k, [P, n], arg[k]) for k, n in
                           (("expert", E), ("upto_tile", P), ("not_first", E * NT), ("full_at", NT), ("tile_index", SLOT_TILES))}
        self.slots = [nc.dram_tensor(f"{kind}{n}", (SLOTS, D), F32, kind="Internal").ap()
                      for n in range(2) for kind in ("slot_rows", "slot_outputs")]
        self.conv = {
            "alog": self.preload("conv", "alog", [P, D // 2], arg["conv_alog"]),
            "b": self.preload("conv", "b", [P, D // 2], arg["conv_b"]),
            "c": self.preload("conv", "c", [P, D // 2], arg["conv_c"]),
            "dt": self.preload("conv", "dt", [P, D // 2], arg["conv_dt"]),
            "skip": self.preload("conv", "skip", [1, D], arg["conv_skip"]),
            "half": self.preload("conv", "half", [P, 2], arg["half"]),
            "time": self.preload("conv", "time", [P, P], arg["time"]),
            "dft": self.preload("conv", "dft", [P, 2, FFT], arg["dft"].rearrange("(a p) n -> p a n", p=P)),
            "idft": self.preload("conv", "idft", [P, 4, S], arg["idft"].rearrange("(a p) n -> p a n", p=P)),
            "packed": self.preload("conv", "packed", [P, 2], arg["packed"]),
            "win": self.preload("conv", "win", [P, D], arg["conv_win"]),
            "bin": self.preload("conv", "bin", [1, D], arg["conv_bin"]),
            "wout": self.preload("conv", "wout", [P, D], arg["conv_wout"]),
            "bout": self.preload("conv", "bout", [1, D], arg["conv_bout"]),
        }
        self.xat = {
            "mcol": self.preload("xat", "mcol", [P, NT], arg["mcol"]),
            "wk": self.preload("xat", "wk", [P, 2, 2 * P], arg["xat_wk"].rearrange("(a p) n -> p a n", p=P)),
            "wv": self.preload("xat", "wv", [P, 2, D], arg["xat_wv"].rearrange("(a p) n -> p a n", p=P)),
            "wq": self.preload("xat", "wq", [P, 2 * P], arg["xat_wq"]),
            "kaux": self.preload("xat", "kaux", [AUX, 2 * P], arg["xat_kaux"]),
            "qaux": self.preload("xat", "qaux", [AUX, 2 * P], arg["xat_qaux"]),
            "bv": self.preload("xat", "bv", [P, D], arg["xat_bv"]),
            "wout": self.preload("xat", "wout", [P, 2, D], arg["xat_wout"].rearrange("(a p) n -> p a n", p=P)),
            "bout": self.preload("xat", "bout", [1, D], arg["xat_bout"]),
        }
        self.early = ExitStack()
        self.ret = {
            "wqk": self.preload_early("ret", "wqk", [P, 4, P], arg["wqk"].rearrange("p (a n) -> p a n", a=4)),
            "rope": self.preload_early("ret", "rope", [P, 4, S], arg["rope"].rearrange("p (a n) -> p a n", a=4)),
            "wvg": self.preload_early("ret", "wvg", [P, 2 * RH * RV], arg["wvg"]),
            "causal": self.preload_early("ret", "causal", [P, CAUSAL], arg["causal"]),
            "wo": self.preload_early("ret", "wo", [P, 2, D], arg["wo"].rearrange("(a p) n -> p a n", p=P)),
            "gnorm": self.preload_early("ret", "gnorm", [P, RH * RV], arg["gnorm"]),
        }
        self.dep = {
            "lens": self.preload_early("dep", "lens", [P, B, S], arg["lens"].rearrange("(o b) s -> o b s", o=1).to_broadcast([P, B, S]), I32),
            "ctx": self.preload_early("dep", "ctx", [P, NT, DC], arg["ctx"].rearrange("(t p) d -> p t d", p=P)),
            "ginit": self.preload_early("dep", "ginit", [P, D], arg["ginit"]),
            "index": self.preload_early("dep", "index", [P, 6], arg["index"]),
            "upto": self.preload_early("dep", "upto", [P, S], arg["upto"]),
            "gres": self.preload_early("dep", "gres", [P, 1], arg["gres"]),
            "win": self.preload_early("dep", "win", [P, D], arg["dep_win"]),
            "bin": self.preload_early("dep", "bin", [1, D], arg["dep_bin"]),
        }

    def sb(self, ctx, name, shape, dt=F32):
        return ctx.enter_context(self.nc.sbuf_tensor(name, shape, dt))

    def preload_early(self, layer, name, shape, source, dt=F32):
        return self.preload(layer, name, shape, source, dt, self.early)

    def preload(self, layer, name, shape, source, dt=F32, ctx=None):
        buffer = self.sb(ctx or self.ctx, f"{layer}_{name}", shape, dt)
        if layer not in self.loads:
            self.loads[layer], self.loaded[layer] = [], self.sem(f"{layer}_loaded")
        self.loads[layer].append((buffer[tuple(slice(None) for _ in shape)], source))
        return buffer

    def wait_loaded(self, engine, layer):
        engine.wait_ge(self.loaded[layer], 16 * len(self.loads[layer]))

    def sem(self, name):
        return self.ctx.enter_context(self.nc.semaphore(name))

    def ln_buffers(self, ctx, name):
        st = {k: self.sb(ctx, f"{name}_{k}", [P, PAIR]) for k in ("mean", "diff", "v", "r", "r2", "tmp")}
        st["raw"] = self.sb(ctx, f"{name}_raw", [P, PAIR, 6])
        return st


def transpose_tiles(pe, bank, tiles, ident, n=PAIR):
    for j in range(n):
        ins = pe.transpose(bank[:, j * P:(j + 1) * P], tiles(j), ident)
    return ins


def retention_layer(core):
    nc, arg, x, ident, bank = core.nc, core.arg, core.x, core.ident, core.bank
    with ExitStack() as ctx:
        def sb(name, shape, dt=F32):
            return core.sb(ctx, "ret_" + name, shape, dt)

        def sem(name):
            return core.sem("ret_" + name)

        wqk, rope, wvg, causal, wo, gnorm = (core.ret[k] for k in ("wqk", "rope", "wvg", "causal", "wo", "gnorm"))
        st = core.ln_buffers(ctx, "ret_ln")
        xn = sb("xn", [P, PAIR, D])
        xnT = sb("xnT", [P, WIDE])
        rot = sb("rot", [P, 4, WIDE])
        qT = sb("qT", [P, WIDE])
        kT = sb("kT", [P, WIDE])
        v = sb("v", [P, PAIR, RH * RV])
        gate = sb("gate", [P, PAIR, RH * RV])
        scores = sb("scores", [P, 2, RH, CAUSAL])
        osq = sb("osq", [P, PAIR, RH * RV])
        ms = sb("ms", [P, PAIR * RH])
        rms = sb("rms", [P, PAIR * RH])
        mtmp = sb("mtmp", [P, PAIR * RH])
        o = sb("o", [P, PAIR, RH * RV])
        oT = sb("oT", [P, 2, WIDE])

        xn_ready = sem("xn_ready")
        xn_turned = sem("xn_turned")
        xnT_ready = sem("xnT_ready")
        qk_ready = sem("qk_ready")
        rot_ready = sem("rot_ready")
        qk_rotated = sem("qk_rotated")
        vg_ready = sem("vg_ready")
        vg_read = sem("vg_read")
        scores_ready = sem("scores_ready")
        scores_masked = sem("scores_masked")
        o_ready = sem("o_ready")
        osq_ready = sem("osq_ready")
        o_scaled = sem("o_scaled")
        o_gated = sem("o_gated")
        o_turned = sem("o_turned")
        oT_ready = sem("oT_ready")
        y_ready = sem("y_ready")
        y_added = sem("y_added")
        vec_per = LN_STEPS + 1 + 1 + 11
        block = ctx.enter_context(nc.Block())

        @block.sync
        def _(sp):
            for layer in LOAD_ORDER:
                for buffer, source in core.loads[layer]:
                    sp.dma_start(buffer, source).then_inc(core.loaded[layer], 16)

        @block.tensor
        def _(pe):
            core.wait_loaded(pe, "ret")
            def body(i):
                pe.wait_ge(xn_ready, 4 * i + 4)
                transpose_tiles(pe, bank[0], lambda j: xn[:, j, :], ident[:, :]).then_inc(xn_turned, 1)
                pe.wait_ge(xnT_ready, i + 1)
                wait_last_round(pe, y_added, i)
                for a in range(4):
                    pe.matmul(bank[1 + a][:, :], wqk[:, a, :], xnT[:, :], start=True, stop=True).then_inc(qk_ready, 1)
                for j in range(PAIR):
                    pe.matmul(bank[(5 + j) % 8][:, :], xnT[:, j * P:(j + 1) * P], wvg[:, :],
                              start=True, stop=True).then_inc(vg_ready, 1)
                pe.wait_ge(qk_rotated, 2 * i + 2)
                for s in range(2):
                    if s == 0:
                        pe.wait_ge(rot_ready, 4 * i + 4)
                    for h in range(RH):
                        if s == 1:
                            pe.wait_ge(vg_read, 8 * i + 2 * h + 2)
                        rows, at = slice(h * RQK, (h + 1) * RQK), s * S
                        bk = bank[(1 + 4 * s + h) % 8]
                        pe.matmul(bk[:, 0:S], kT[rows, at:at + P], qT[rows, at:at + S], start=True, stop=True)
                        pe.matmul(bk[:, S:CAUSAL], kT[rows, at + P:at + S], qT[rows, at + P:at + S],
                                  start=True, stop=True).then_inc(scores_ready, 1)
                pe.wait_ge(vg_read, 8 * i + 8)
                for s in range(2):
                    pe.wait_ge(scores_masked, 8 * i + 4 * s + 4)
                    bk = bank[1 + 4 * s]
                    for h in range(RH):
                        vh = slice(h * RV, (h + 1) * RV)
                        out0 = bk[:, h * RV:(h + 1) * RV]
                        out1 = bk[:, S + h * RV:S + (h + 1) * RV]
                        pe.matmul(out0, scores[:, s, h, 0:P], v[:, 2 * s, vh], start=True, stop=True)
                        pe.matmul(out1, scores[:, s, h, P:S], v[:, 2 * s, vh], start=True, stop=False)
                        mm = pe.matmul(out1, scores[:, s, h, S:CAUSAL], v[:, 2 * s + 1, vh], start=False, stop=True)
                    mm.then_inc(o_ready, 1)
                pe.wait_ge(o_gated, 2 * i + 2)
                for a in range(2):
                    transpose_tiles(pe, bank[2 + a], lambda j: o[:, j, a * P:(a + 1) * P],
                                    ident[:, :]).then_inc(o_turned, 1)
                pe.wait_ge(oT_ready, 2 * i + 2)
                for j in range(PAIR):
                    for a in range(2):
                        mm = pe.matmul(bank[4][:, j * P:(j + 1) * P], oT[:, a, j * P:(j + 1) * P], wo[:, a, :],
                                       start=(a == 0), stop=(a == 1))
                mm.then_inc(y_ready, 1)
            rounds(pe, PAIRS, body)

        @block.scalar
        def _(act):
            core.wait_loaded(act, "ret")
            act.preload_act_table(ACT.Silu)
            def body(i):
                act.wait_ge(xn_turned, i + 1)
                act.activation(xnT[:, :], bank[0][:, :], ACT.Copy).then_inc(xnT_ready, 1)
                for j in range(PAIR):
                    act.wait_ge(vg_ready, 4 * i + j + 1)
                    bk = bank[(5 + j) % 8]
                    if j == 0:
                        wait_last_round(act, o_gated, 2 * i)
                    act.activation(v[:, j, :], bk[:, 0:RH * RV], ACT.Copy).then_inc(vg_read, 1)
                    act.activation(gate[:, j, :], bk[:, RH * RV:], ACT.Silu).then_inc(vg_read, 1)
                for s in range(2):
                    act.wait_ge(o_ready, 2 * i + s + 1)
                    act.activation(osq[:, 2 * s:2 * s + 2, :],
                                   bank[1 + 4 * s][:, :].rearrange("p (j n) -> p j n", j=2),
                                   ACT.Square).then_inc(osq_ready, 1)
                for a in range(2):
                    act.wait_ge(o_turned, 2 * i + a + 1)
                    act.activation(oT[:, a, :], bank[2 + a][:, :], ACT.Copy).then_inc(oT_ready, 1)
            rounds(act, PAIRS, body)

        @block.vector
        def _(vec):
            core.wait_loaded(vec, "ret")
            def body(i):
                steps = Steps(core, vec, i, vec_per)
                for ins in layer_norm(vec, steps, x, 4 * i, st, False, xn, lambda: wait_last_round(vec, xn_turned, i)):
                    ins.then_inc(xn_ready, 1)
                for a in range(4):
                    vec.wait_ge(qk_ready, 4 * i + a + 1)
                    if a == 0:
                        wait_last_round(vec, qk_rotated, 2 * i)
                    vec.tensor_tensor(rot[:, a, :].rearrange("p (s t) -> p s t", s=2),
                                      bank[1 + a][:, :].rearrange("p (s t) -> p s t", s=2),
                                      rope[:, a:a + 1, :].to_broadcast([P, 2, S]), ALU.mult).then_inc(rot_ready, 1)
                for s in range(2):
                    for h in range(RH):
                        vec.wait_ge(scores_ready, 8 * i + 4 * s + h + 1)
                        vec.tensor_tensor(scores[:, s, h, :], bank[(1 + 4 * s + h) % 8][:, 0:CAUSAL], causal[:, :],
                                          ALU.mult).then_inc(scores_masked, 1)
                vec.wait_ge(osq_ready, 2 * i + 2)
                steps.done(vec.tensor_reduce(ms[:, :], osq[:, :, :].rearrange("p j (h n) -> p (j h) n", h=RH),
                                             AX.X, ALU.add))
                steps.wait()
                steps.done(vec.tensor_scalar(ms[:, :], ms[:, :], 1.0 / RV, LN_EPS, ALU.mult, ALU.add))
                steps.wait()
                rsqrt(vec, steps, rms[:, :], ms[:, :], mtmp[:, :])
                steps.wait()
                for s in range(2):
                    if s == 0:
                        wait_last_round(vec, o_turned, 2 * i)
                    vec.tensor_tensor(
                        o[:, 2 * s:2 * s + 2, :].rearrange("p j (h n) -> p (j h) n", h=RH),
                        bank[1 + 4 * s][:, :].rearrange("p (g n) -> p g n", n=RV),
                        rms[:, 8 * s:8 * s + 8].unsqueeze(2).to_broadcast([P, 8, RV]), ALU.mult).then_inc(o_scaled, 1)
                vec.wait_ge(y_ready, i + 1)
                vec.tensor_tensor(x[:, bass.ds(4 * i, PAIR), :], x[:, bass.ds(4 * i, PAIR), :],
                                  bank[4][:, :].rearrange("p (j n) -> p j n", j=PAIR), ALU.add).then_inc(y_added, 1)
                assert steps.n == vec_per
            rounds(vec, PAIRS, body)
            core.vector_base += PAIRS * vec_per

        @block.gpsimd
        def _(pool):
            core.wait_loaded(pool, "ret")
            def body(i):
                for a, dst in enumerate((qT, kT)):
                    pool.wait_ge(rot_ready, 4 * i + 2 * a + 2)
                    if a == 0:
                        wait_last_round(pool, scores_ready, 8 * i)
                    pool.tensor_tensor(dst[:, :], rot[:, 2 * a, :], rot[:, 2 * a + 1, :],
                                       ALU.add).then_inc(qk_rotated, 1)
                pool.wait_ge(vg_read, 8 * i + 8)
                pool.tensor_tensor(gate[:, :, :], gate[:, :, :], gnorm[:, :].unsqueeze(1).to_broadcast([P, PAIR, RH * RV]),
                                   ALU.mult).then_inc(o_gated, 1)
                pool.wait_ge(o_gated, 2 * i + 1)
                pool.wait_ge(o_scaled, 2 * i + 2)
                pool.tensor_tensor(o[:, :, :], o[:, :, :], gate[:, :, :], ALU.mult).then_inc(o_gated, 1)
            rounds(pool, PAIRS, body)


def depool_layer(core):
    nc, x, ident, bank = core.nc, core.x, core.ident, core.bank
    with ExitStack() as ctx:
        def sb(name, shape, dt=F32):
            return core.sb(ctx, "dep_" + name, shape, dt)

        def sem(name):
            return core.sem("dep_" + name)

        lens, cx, ginit, index, upto, gres, win, bin_ = (core.dep[k] for k in (
            "lens", "ctx", "ginit", "index", "upto", "gres", "win", "bin"))
        st = core.ln_buffers(ctx, "dep_ln")
        zeros = sb("zeros", [P, S])
        ones = sb("ones", [1, P])
        upto_b = sb("upto_b", [P, S], BF16)
        cum = sb("cum", [P, 2, S])
        wrap = sb("wrap", [P, 2, S])
        end_at = sb("end_at", [P, 2, S])
        same = sb("same", [P, S])
        is_end = sb("is_end", [P, 4])
        is_end_b = sb("is_end_b", [P, 4, P], BF16)
        age = sb("age", [P, 2, CAUSAL])
        weight = sb("weight", [P, 2, CAUSAL])
        csq = sb("csq", [P, PAIR, DC])
        cms = sb("cms", [P, PAIR])
        crms = sb("crms", [P, PAIR])
        ctmp = sb("ctmp", [P, PAIR])
        u = sb("u", [P, PAIR, D])
        xn = sb("xn", [P, PAIR, D])
        xnT = sb("xnT", [P, WIDE])

        set_up = sem("set_up")
        xn_ready = sem("xn_ready")
        xn_turned = sem("xn_turned")
        xnT_ready = sem("xnT_ready")
        ends_ready = sem("ends_ready")
        counts_ready = sem("counts_ready")
        ages_ready = sem("ages_ready")
        decays_ready = sem("decays_ready")
        weights_ready = sem("weights_ready")
        csq_ready = sem("csq_ready")
        crms_ready = sem("crms_ready")
        u_gained = sem("u_gained")
        u_ready = sem("u_ready")
        y_ready = sem("y_ready")
        y_added = sem("y_added")
        vec_per = (2 + 1 + 1 + 4) + (1 + 1 + 11) + LN_STEPS_TWICE
        block = ctx.enter_context(nc.Block())

        @block.tensor
        def _(pe):
            core.wait_loaded(pe, "dep")
            pe.wait_ge(set_up, 3)
            def body(i):
                pe.wait_ge(ends_ready, i + 1)
                for s in range(2):
                    pe.matmul(bank[2][:, s * S:(s + 1) * S], is_end_b[:, 2 * s, :], upto_b[:, :], start=True, stop=False)
                    mm = pe.matmul(bank[2][:, s * S + P:(s + 1) * S], is_end_b[:, 2 * s + 1, :], upto_b[:, 0:P],
                                   start=False, stop=True)
                mm.then_inc(counts_ready, 1)
                pe.wait_ge(xn_ready, 4 * i + 4)
                transpose_tiles(pe, bank[0], lambda j: xn[:, j, :], ident[:, :]).then_inc(xn_turned, 1)
                wait_last_round(pe, y_added, i)
                pe.wait_ge(xnT_ready, i + 1)
                pe.wait_ge(weights_ready, i + 1)
                pe.wait_ge(u_ready, i + 1)
                for s in range(2):
                    for t in range(2):
                        j = 2 * s + t
                        y = bank[1][:, j * P:(j + 1) * P]
                        pe.matmul(y, ones[:, :], bin_[:, :], start=True, stop=False)
                        pe.matmul(y, xnT[:, j * P:(j + 1) * P], win[:, :], start=False, stop=False)
                        mm = pe.matmul(y, weight[:, s, t * P:(t + 1) * P], u[:, 2 * s, :], start=False, stop=(t == 0))
                        if t == 1:
                            mm = pe.matmul(y, weight[:, s, S:CAUSAL], u[:, 2 * s + 1, :], start=False, stop=True)
                mm.then_inc(y_ready, 1)
            rounds(pe, PAIRS, body)

        @block.scalar
        def _(act):
            core.wait_loaded(act, "dep")
            act.preload_act_table(ACT.Exp)
            def body(i):
                wait_last_round(act, crms_ready, i)
                act.activation(csq[:, :, :], cx[:, bass.ds(4 * i, PAIR), :], ACT.Square).then_inc(csq_ready, 1)
                act.wait_ge(ages_ready, 4 * i + 4)
                wait_last_round(act, y_ready, i)
                act.activation(weight[:, :, :], age[:, :, :], ACT.Exp, scale=-DEPOOL_DT).then_inc(decays_ready, 1)
                act.wait_ge(xn_turned, i + 1)
                act.activation(xnT[:, :], bank[0][:, :], ACT.Copy, scale=gres[:, 0:1]).then_inc(xnT_ready, 1)
            rounds(act, PAIRS, body)

        @block.vector
        def _(vec):
            core.wait_loaded(vec, "dep")
            vec.memset(zeros[:, :], 0.0).then_inc(set_up, 1)
            vec.memset(ones[:, :], 1.0).then_inc(set_up, 1)
            vec.tensor_copy(upto_b[:, :], upto[:, :]).then_inc(set_up, 1)
            vec.wait_ge(set_up, 3)
            def body(i):
                steps = Steps(core, vec, i, vec_per)
                for s in range(2):
                    steps.done(vec.tensor_tensor_scan(out=cum[:, s, :], data0=lens[:, bass.ds(2 * i + s, 1), :].rearrange("p o n -> p (o n)"), data1=zeros[:, :],
                                                      initial=0.0, op0=ALU.add, op1=ALU.add))
                steps.wait()
                steps.done(vec.tensor_scalar(wrap[:, :, :], cum[:, :, :], 1.0, float(S), ALU.is_lt, ALU.mult))
                steps.wait()
                steps.done(vec.scalar_tensor_tensor(out=end_at[:, :, :], in0=cum[:, :, :], scalar=-1.0,
                                                    in1=wrap[:, :, :], op0=ALU.add, op1=ALU.add))
                for s in range(2):
                    for t in range(2):
                        steps.wait()
                        steps.done(vec.tensor_scalar(same[:, :], end_at[:, s, :], index[:, t:t + 1], None, ALU.is_equal,
                                                     ALU.max, accum_out=is_end[:, 2 * s + t:2 * s + t + 1]))
                steps.wait()
                wait_last_round(vec, counts_ready, i)
                vec.tensor_copy(is_end_b[:, :, :], is_end[:, :].unsqueeze(2).to_broadcast([P, 4, P])).then_inc(ends_ready, 1)
                vec.wait_ge(csq_ready, i + 1)
                steps.done(vec.tensor_reduce(cms[:, :], csq[:, :, :], AX.X, ALU.add))
                steps.wait()
                steps.done(vec.tensor_scalar(cms[:, :], cms[:, :], 1.0 / DC, LN_EPS, ALU.mult, ALU.add))
                steps.wait()
                wait_last_round(vec, u_ready, i)
                rsqrt(vec, steps, crms[:, :], cms[:, :], ctmp[:, :])
                steps.wait()
                vec.tensor_scalar(crms[:, :], crms[:, :], DEPOOL_B, None, ALU.mult).then_inc(crms_ready, 1)
                vec.wait_ge(counts_ready, i + 1)
                wait_last_round(vec, weights_ready, i)
                for s in range(2):
                    vec.tensor_scalar(age[:, s, 0:S], bank[2][:, s * S:(s + 1) * S], index[:, 2:3], index[:, 4:5],
                                      ALU.subtract, ALU.max).then_inc(ages_ready, 1)
                    vec.tensor_scalar(age[:, s, S:CAUSAL], bank[2][:, s * S + P:(s + 1) * S], index[:, 3:4],
                                      index[:, 5:6], ALU.subtract, ALU.max).then_inc(ages_ready, 1)
                for ins in layer_norm(vec, steps, x, 4 * i, st, True, xn, lambda: wait_last_round(vec, xn_turned, i)):
                    ins.then_inc(xn_ready, 1)
                vec.wait_ge(decays_ready, i + 1)
                vec.scalar_tensor_tensor(out=weight[:, :, :], in0=age[:, :, :], scalar=0.0, in1=weight[:, :, :],
                                         op0=ALU.is_ge, op1=ALU.mult).then_inc(weights_ready, 1)
                vec.wait_ge(y_ready, i + 1)
                vec.tensor_tensor(x[:, bass.ds(4 * i, PAIR), :], x[:, bass.ds(4 * i, PAIR), :],
                                  bank[1][:, :].rearrange("p (j n) -> p j n", j=PAIR), ALU.add).then_inc(y_added, 1)
                assert steps.n == vec_per
            rounds(vec, PAIRS, body)
            core.vector_base += PAIRS * vec_per

        @block.gpsimd
        def _(pool):
            core.wait_loaded(pool, "dep")
            def body(i):
                wait_last_round(pool, y_ready, i)
                pool.tensor_tensor(u[:, :, :], cx[:, bass.ds(4 * i, PAIR), 0:D],
                                   ginit[:, :].unsqueeze(1).to_broadcast([P, PAIR, D]), ALU.mult).then_inc(u_gained, 1)
                pool.wait_ge(u_gained, i + 1)
                pool.wait_ge(crms_ready, i + 1)
                pool.tensor_tensor(u[:, :, :], u[:, :, :], crms[:, :].unsqueeze(2).to_broadcast([P, PAIR, D]),
                                   ALU.mult).then_inc(u_ready, 1)
            rounds(pool, PAIRS, body)


def conv_layer(core):
    nc, x, ident, bank = core.nc, core.x, core.ident, core.bank
    w = core.conv
    HALF = D // 2
    with ExitStack() as ctx:
        def sb(name, shape, dt=F32):
            return core.sb(ctx, "conv_" + name, shape, dt)

        def sem(name):
            return core.sem("conv_" + name)

        dft, idft, win, wout = (w[k] for k in ("dft", "idft", "win", "wout"))
        st = core.ln_buffers(ctx, "conv_ln")
        ones = sb("ones", [1, P])
        rate = sb("rate", [P, HALF])
        late = sb("late", [P, HALF])
        gain = sb("gain", [P, HALF])
        gains = sb("gains", [P, HALF, 4])
        angle = sb("angle", [P, HALF, P])
        power = sb("power", [P, HALF, P])
        kernel_t = sb("kernel_t", [P, 2, D])
        kre = sb("kre", [P, 2, D])
        kim = sb("kim", [P, 2, D])
        kre2 = sb("kre2", [P, 2, D])
        packed = sb("packed_row", [P, D])
        xn = sb("xn", [P, PAIR, D])
        xnT = sb("xnT", [P, WIDE])
        u = sb("u", [P, PAIR, D])
        prod = sb("prod", [P, 4, 4, P])
        spec = sb("spec", [P, 4, 2, D])
        yT = sb("yT", [P, WIDE])

        signed = sem("signed")
        rates_ready = sem("rates_ready")
        gains_ready = sem("gains_ready")
        angles_ready = sem("angles_ready")
        powers_ready = sem("powers_ready")
        kernel_ready = sem("kernel_ready")
        kernel_copied = sem("kernel_copied")
        kspec_ready = sem("kspec_ready")
        kspec_copied = sem("kspec_copied")
        xn_ready = sem("xn_ready")
        xn_turned = sem("xn_turned")
        xnT_ready = sem("xnT_ready")
        u_ready = sem("u_ready")
        u_copied = sem("u_copied")
        uspec_ready = sem("uspec_ready")
        products_ready = sem("products_ready")
        spec_ready = sem("spec_ready")
        yT_ready = sem("yT_ready")
        yT_copied = sem("yT_copied")
        y_ready = sem("y_ready")
        y_added = sem("y_added")
        vec_per = LN_STEPS
        CUT = 8
        PART = HALF // CUT
        block = ctx.enter_context(nc.Block())

        @block.tensor
        def _(pe):
            core.wait_loaded(pe, "conv")
            pe.wait_ge(signed, 1)
            pe.wait_ge(gains_ready, 2)
            for c in range(CUT):
                pe.wait_ge(powers_ready, c + 1)
                for j in range(c * PART, (c + 1) * PART):
                    mm = pe.matmul(bank[6][:, 4 * j:4 * j + 4], power[:, j, :], gains[:, j, :], start=True, stop=True)
            mm.then_inc(kernel_ready, 1)
            pe.wait_ge(kernel_copied, 3)
            for m in range(4):
                for j in range(2):
                    mm = pe.matmul(bank[7][:, m * D:(m + 1) * D], dft[:, j, m * P:(m + 1) * P], kernel_t[:, j, :],
                                   start=(j == 0), stop=(j == 1))
            mm.then_inc(kspec_ready, 1)
            def body(i):
                pe.wait_ge(xn_ready, 4 * i + 4)
                transpose_tiles(pe, bank[0], lambda j: xn[:, j, :], ident[:, :]).then_inc(xn_turned, 1)
                pe.wait_ge(xnT_ready, i + 1)
                for j in range(PAIR):
                    pe.matmul(bank[1][:, j * P:(j + 1) * P], ones[:, :], w["bin"][:, :], start=True, stop=False)
                    mm = pe.matmul(bank[1][:, j * P:(j + 1) * P], xnT[:, j * P:(j + 1) * P], win[:, :],
                                   start=False, stop=True)
                mm.then_inc(u_ready, 1)
                pe.wait_ge(u_copied, i + 1)
                for m in range(4):
                    for j in range(2):
                        mm = pe.matmul(bank[2 + m // 2][:, (m % 2) * S:(m % 2 + 1) * S].rearrange("p (s d) -> p s d", s=2),
                                       dft[:, j, m * P:(m + 1) * P],
                                       u[:, j:PAIR:2, :], start=(j == 0), stop=(j == 1))
                    if m % 2:
                        mm.then_inc(uspec_ready, 1)
                for s in range(2):
                    pe.wait_ge(spec_ready, 2 * i + 2)
                    for m in range(4):
                        mm = pe.matmul(bank[4][:, s * S:(s + 1) * S], spec[:, m, s, :], idft[:, m, :],
                                       start=(m == 0), stop=(m == 3))
                mm.then_inc(yT_ready, 1)
                pe.wait_ge(yT_copied, i + 1)
                for j in range(PAIR):
                    pe.matmul(bank[5][:, j * P:(j + 1) * P], ones[:, :], w["bout"][:, :], start=True, stop=False)
                    mm = pe.matmul(bank[5][:, j * P:(j + 1) * P], yT[:, j * P:(j + 1) * P], wout[:, :],
                                   start=False, stop=True)
                mm.then_inc(y_ready, 1)
            rounds(pe, PAIRS, body)

        @block.scalar
        def _(act):
            core.wait_loaded(act, "conv")
            act.activation(rate[:, :], w["alog"][:, :], ACT.Exp, scale=-1.0).then_inc(rates_ready, 1)
            act.wait_ge(signed, 2)
            act.activation(late[:, :], rate[:, :], ACT.Exp, scale=float(P)).then_inc(rates_ready, 1)
            for c in range(CUT):
                act.wait_ge(angles_ready, c + 1)
                part = slice(c * PART, (c + 1) * PART)
                act.activation(power[:, part, :], angle[:, part, :], ACT.Exp).then_inc(powers_ready, 1)
            def body(i):
                act.wait_ge(xn_turned, i + 1)
                act.activation(xnT[:, :], bank[0][:, :], ACT.Copy).then_inc(xnT_ready, 1)
                act.wait_ge(u_ready, i + 1)
                act.activation(u[:, :, :], bank[1][:, :].rearrange("p (j n) -> p j n", j=PAIR),
                               ACT.Copy).then_inc(u_copied, 1)
                act.wait_ge(yT_ready, i + 1)
                act.activation(yT[:, :], bank[4][:, :], ACT.Copy).then_inc(yT_copied, 1)
            rounds(act, PAIRS, body)

        @block.vector
        def _(vec):
            core.wait_loaded(vec, "conv")
            vec.memset(ones[:, :], 1.0).then_inc(signed, 1)
            vec.wait_ge(rates_ready, 1)
            vec.scalar_tensor_tensor(out=rate[:, :], in0=rate[:, :], scalar=-1.0, in1=w["dt"][:, :],
                                     op0=ALU.mult, op1=ALU.mult).then_inc(signed, 1)
            vec.wait_ge(signed, 2)
            setup = Steps(core, vec)
            for c in range(CUT):
                part = slice(c * PART, (c + 1) * PART)
                vec.tensor_tensor(angle[:, part, :], w["time"][:, :].unsqueeze(1).to_broadcast([P, PART, P]),
                                  rate[:, part].unsqueeze(2).to_broadcast([P, PART, P]), ALU.mult).then_inc(angles_ready, 1)
                if c == 0:
                    setup.done(vec.tensor_tensor(gain[:, :], w["b"][:, :], w["dt"][:, :], ALU.mult))
                    setup.wait()
                    setup.done(vec.tensor_tensor(gain[:, :], gain[:, :], w["c"][:, :], ALU.mult))
                    setup.wait()
                    vec.wait_ge(rates_ready, 2)
                    setup.done(vec.tensor_tensor(late[:, :], late[:, :], gain[:, :], ALU.mult))
                    setup.wait()
                    for h, g in enumerate((gain, late)):
                        vec.tensor_tensor(gains[:, :, 2 * h:2 * h + 2], g[:, :].unsqueeze(2).to_broadcast([P, HALF, 2]),
                                          w["half"][:, :].unsqueeze(1).to_broadcast([P, HALF, 2]),
                                          ALU.mult).then_inc(gains_ready, 1)
            setup.close()
            vec.wait_ge(kernel_ready, 1)
            for h in range(2):
                vec.tensor_copy(kernel_t[:, h, :].rearrange("p (j c) -> p j c", c=2),
                                bank[6][:, 0:4 * HALF].rearrange("p (j h c) -> p h j c", h=2, c=2)[:, h]
                                ).then_inc(kernel_copied, 1)
            vec.wait_ge(kernel_copied, 2)
            vec.tensor_tensor(kernel_t[0:1, 0, :], kernel_t[0:1, 0, :], w["skip"][:, :], ALU.add).then_inc(kernel_copied, 1)
            vec.wait_ge(kspec_ready, 1)
            kbank = bank[7][:, :].rearrange("p (m d) -> p m d", m=4)
            vec.tensor_copy(kre[:, :, :], kbank[:, 0:2]).then_inc(kspec_copied, 1)
            vec.tensor_scalar(packed[:, :], kbank[:, 2], w["packed"][:, 0:1], None, ALU.mult).then_inc(kspec_copied, 1)
            vec.tensor_scalar(kim[:, 0, :], kbank[:, 2], w["packed"][:, 1:2], None, ALU.mult).then_inc(kspec_copied, 1)
            vec.tensor_copy(kim[:, 1, :], kbank[:, 3]).then_inc(kspec_copied, 1)
            vec.tensor_copy(kre2[:, 1, :], kbank[:, 1]).then_inc(kspec_copied, 1)
            vec.wait_ge(kspec_copied, 5)
            vec.scalar_tensor_tensor(out=kre2[:, 0, :], in0=kre[:, 0, :], scalar=w["packed"][:, 1:2], in1=packed[:, :],
                                     op0=ALU.mult, op1=ALU.add).then_inc(kspec_copied, 1)
            vec.wait_ge(kspec_copied, 6)
            def body(i):
                steps = Steps(core, vec, i, vec_per)
                for ins in layer_norm(vec, steps, x, 4 * i, st, False, xn, lambda: wait_last_round(vec, xn_turned, i)):
                    ins.then_inc(xn_ready, 1)
                vec.wait_ge(uspec_ready, 2 * i + 2)
                wait_last_round(vec, spec_ready, 2 * i)
                for q, (half, k) in enumerate(((0, kre), (1, kim), (0, kim), (1, kre2))):
                    for m in range(2):
                        vec.tensor_tensor(prod[:, q, 2 * m:2 * m + 2, :],
                                          bank[2 + half][:, m * S:(m + 1) * S].rearrange("p (s d) -> p s d", s=2),
                                          k[:, m:m + 1, :].to_broadcast([P, 2, D]), ALU.mult).then_inc(products_ready, 1)
                vec.wait_ge(y_ready, i + 1)
                vec.tensor_tensor(x[:, bass.ds(4 * i, PAIR), :], x[:, bass.ds(4 * i, PAIR), :],
                                  bank[5][:, :].rearrange("p (j n) -> p j n", j=PAIR), ALU.add).then_inc(y_added, 1)
                assert steps.n == vec_per
            rounds(vec, PAIRS, body)
            core.vector_base += PAIRS * vec_per

        @block.gpsimd
        def _(pool):
            def body(i):
                for half, op in ((0, ALU.subtract), (1, ALU.add)):
                    pool.wait_ge(products_ready, 8 * i + 4 * half + 4)
                    if half == 0:
                        wait_last_round(pool, yT_ready, i)
                    pool.tensor_tensor(spec[:, 2 * half:2 * half + 2, :, :].rearrange("p m s d -> p (m s) d"),
                                       prod[:, 2 * half, :, :], prod[:, 2 * half + 1, :, :], op).then_inc(spec_ready, 1)
            rounds(pool, PAIRS, body)


def cross_attention_layer(core):
    nc, x, ident, bank, psum = core.nc, core.x, core.ident, core.bank, core.psum
    w = core.xat
    with ExitStack() as ctx:
        def sb(name, shape, dt=F32):
            return core.sb(ctx, "xat_" + name, shape, dt)

        def sem(name):
            return core.sem("xat_" + name)

        mcol, wk, wv, wq, bv, wout = (w[k] for k in ("mcol", "wk", "wv", "wq", "bv", "wout"))
        st = core.ln_buffers(ctx, "xat_ln")
        ones = sb("ones", [1, P])
        aux = sb("aux", [AUX, B * S])
        xn = sb("xn", [P, PAIR, D])
        xnT = sb("xnT", [P, WIDE])
        xnT_masked = sb("xnT_masked", [P, WIDE])
        ctxT = sb("ctxT", [P, 2, WIDE])
        mask = sb("mask", [P, WIDE])
        ctxT_masked = sb("ctxT_masked", [P, 2, WIDE])
        kT = sb("kT", [P, 2, WIDE])
        qT = sb("qT", [P, 2, WIDE])
        qT_less = sb("qT_less", [P, 2, WIDE])
        v = sb("v", [P, PAIR, XH, XD + 1])
        top = sb("top", [P, PAIR, 2, P])
        prob = sb("prob", [P, 2, XH, 2, S])
        total = sb("total", [P, PAIR, XH])
        upd = sb("upd", [P, PAIR, D])
        updT = sb("updT", [P, WIDE])

        set_up = sem("set_up")
        xn_ready = sem("xn_ready")
        xn_turned = sem("xn_turned")
        xnT_ready = sem("xnT_ready")
        ctx_loaded = sem("ctx_loaded")
        mask_loaded = sem("mask_loaded")
        ctx_masked = sem("ctx_masked")
        q_input_ready = sem("q_input_ready")
        kq_ready = sem("kq_ready")
        kq_copied = sem("kq_copied")
        v_ready = sem("v_ready")
        v_copied = sem("v_copied")
        scores_ready = sem("scores_ready")
        tops_ready = sem("tops_ready")
        tops_turned = sem("tops_turned")
        q_lessened = sem("q_lessened")
        shifted_ready = sem("shifted_ready")
        probs_ready = sem("probs_ready")
        upd_ready = sem("upd_ready")
        totals_ready = sem("totals_ready")
        upd_scaled = sem("upd_scaled")
        upd_turned = sem("upd_turned")
        updT_ready = sem("updT_ready")
        y_ready = sem("y_ready")
        y_added = sem("y_added")
        vec_per = LN_STEPS
        RING = (6, 7, 0, 1)
        block = ctx.enter_context(nc.Block())

        @block.sync
        def _(sp):
            sp.wait_ge(set_up, 1)
            sp.dma_start(aux[AUX_MASK:AUX_MASK + 1, :], core.arg["mask"]).then_inc(set_up, 16)
            sp.dma_start(aux[AUX_BIAS:AUX_BIAS + 1, :], core.arg["mask"]).then_inc(set_up, 16)
            def body(i):
                now = bass.ds(i * WIDE, WIDE)
                wait_last_round(sp, ctx_masked, i)
                sp.dma_start(ctxT[:, :, :], core.arg["ctxT"].rearrange("(a p) t -> p a t", p=P)[:, :, now]).then_inc(ctx_loaded, 16)
                wait_last_round(sp, q_input_ready, i)
                sp.dma_start(mask[:, :], core.arg["mask"][:, now].to_broadcast([P, WIDE])).then_inc(mask_loaded, 16)
            rounds(sp, PAIRS, body)

        @block.tensor
        def _(pe):
            core.wait_loaded(pe, "xat")
            pe.wait_ge(set_up, 1 + 32 + 5)
            def body(i):
                now = bass.ds(i * WIDE, WIDE)
                pe.wait_ge(ctx_masked, i + 1)
                for g in range(2):
                    cols = slice(g * P, (g + 1) * P)
                    pe.matmul(bank[1 + g], w["kaux"][:, cols], aux[:, now], start=True, stop=False)
                    for a in range(2):
                        mm = pe.matmul(bank[1 + g], wk[:, a, cols], ctxT_masked[:, a, :], start=False, stop=(a == 1))
                    mm.then_inc(kq_ready, 1)
                for j in range(PAIR):
                    for a in range(2):
                        mm = pe.matmul(bank[5][:, j * P:(j + 1) * P], ctxT_masked[:, a, j * P:(j + 1) * P], wv[:, a, :],
                                       start=(a == 0), stop=(a == 1))
                mm.then_inc(v_ready, 1)
                pe.wait_ge(xn_ready, 4 * i + 4)
                transpose_tiles(pe, bank[0], lambda j: xn[:, j, :], ident[:, :]).then_inc(xn_turned, 1)
                pe.wait_ge(q_input_ready, i + 1)
                wait_last_round(pe, y_added, i)
                for g in range(2):
                    cols = slice(g * P, (g + 1) * P)
                    pe.matmul(bank[3 + g], w["qaux"][:, cols], aux[:, now], start=True, stop=False)
                    pe.matmul(bank[3 + g], wq[:, cols], xnT_masked[:, :], start=False, stop=True).then_inc(kq_ready, 1)
                pe.wait_ge(kq_copied, 4 * i + 4)
                for j in range(PAIR):
                    for c in range(2):
                        n = 2 * j + c
                        if n >= 2:
                            pe.wait_ge(tops_ready, 8 * i + n - 1)
                        for h in range(2 * c, 2 * c + 2):
                            rows = slice(HEAD_ROWS * h, HEAD_ROWS * (h + 1))
                            at = (j // 2) * S
                            for g in range(2):
                                mm = pe.matmul(psum[:, (6, 0)[c] + h % 2, g * S:(g + 1) * S],
                                               qT[rows, g, j * P:(j + 1) * P], kT[rows, g, at:at + S],
                                               start=True, stop=True)
                        mm.then_inc(scores_ready, 1)
                pe.wait_ge(tops_ready, 8 * i + 8)
                for g in range(2):
                    for j in range(PAIR):
                        mm = pe.matmul(bank[2 + g][:, j * P:(j + 1) * P], top[:, j, g, :], ident[:, :],
                                       start=True, stop=True)
                    mm.then_inc(tops_turned, 1)
                pe.wait_ge(q_lessened, 2 * i + 2)
                for s in range(2):
                    for h in range(XH):
                        n = XH * s + h
                        if n >= 4:
                            pe.wait_ge(probs_ready, 16 * i + n - 3)
                        g, rows, at = h // 4, slice(HEAD_ROWS * (h % 4), HEAD_ROWS * (h % 4 + 1)), s * S
                        for t in range(2):
                            mm = pe.matmul(bank[RING[n % 4]][:, t * S:(t + 1) * S],
                                           kT[rows, g, at + t * P:at + (t + 1) * P], qT_less[rows, g, at:at + S],
                                           start=True, stop=True)
                        mm.then_inc(shifted_ready, 1)
                pe.wait_ge(v_copied, 4 * i + 4)
                for s in range(2):
                    pe.wait_ge(probs_ready, 16 * i + 8 * s + 8)
                    for t in range(2):
                        for h in range(XH):
                            at = (t * XH + h) * (XD + 1)
                            for a in range(2):
                                mm = pe.matmul(bank[5 - s][:, at:at + XD + 1], prob[:, s, h, a, t * P:(t + 1) * P],
                                               v[:, 2 * s + a, h, :], start=(a == 0), stop=(a == 1))
                    mm.then_inc(upd_ready, 1)
                pe.wait_ge(upd_scaled, 2 * i + 2)
                transpose_tiles(pe, bank[2], lambda j: upd[:, j, :], ident[:, :]).then_inc(upd_turned, 1)
                pe.wait_ge(updT_ready, i + 1)
                for j in range(PAIR):
                    y, cols = bank[3][:, j * P:(j + 1) * P], slice(j * P, (j + 1) * P)
                    pe.matmul(y, ones[:, :], w["bout"][:, :], start=True, stop=False)
                    pe.matmul(y, xnT[:, cols], wout[:, 0, :], start=False, stop=False)
                    mm = pe.matmul(y, updT[:, cols], wout[:, 1, :], start=False, stop=True)
                mm.then_inc(y_ready, 1)
            rounds(pe, PAIRS, body)

        @block.scalar
        def _(act):
            act.preload_act_table(ACT.Exp)
            def body(i):
                for g in range(2):
                    act.wait_ge(kq_ready, 4 * i + g + 1)
                    act.activation(kT[:, g, :], bank[1 + g], ACT.Copy).then_inc(kq_copied, 1)
                act.wait_ge(xn_turned, i + 1)
                act.activation(xnT[:, :], bank[0], ACT.Copy).then_inc(xnT_ready, 1)
                for g in range(2):
                    act.wait_ge(kq_ready, 4 * i + 2 + g + 1)
                    act.activation(qT[:, g, :], bank[3 + g], ACT.Copy).then_inc(kq_copied, 1)
                for s in range(2):
                    for h in range(XH):
                        n = XH * s + h
                        act.wait_ge(shifted_ready, 16 * i + n + 1)
                        act.activation(prob[:, s, h, :, :], bank[RING[n % 4]].rearrange("p (a t) -> p a t", a=2), ACT.Exp,
                                       scale=XD ** -0.5).then_inc(probs_ready, 1)
                act.wait_ge(upd_turned, i + 1)
                act.activation(updT[:, :], bank[2], ACT.Copy).then_inc(updT_ready, 1)
            rounds(act, PAIRS, body)

        @block.vector
        def _(vec):
            core.wait_loaded(vec, "xat")
            vec.memset(aux[:, :], 0.0).then_inc(set_up, 1)
            vec.memset(ones[:, :], 1.0).then_inc(set_up, 1)
            vec.memset(top[:, :, :, :], 0.0).then_inc(set_up, 1)
            vec.memset(v[:, :, :, :], 1.0).then_inc(set_up, 1)
            vec.wait_ge(set_up, 4 + 32)
            vec.tensor_scalar(aux[AUX_BIAS:AUX_BIAS + 1, :], aux[AUX_BIAS:AUX_BIAS + 1, :], 0.0, MASKED,
                              ALU.is_equal, ALU.mult).then_inc(set_up, 1)
            vec.memset(aux[AUX_ONE:AUX_ONE + 1, :], 1.0).then_inc(set_up, 1)
            vec.wait_ge(set_up, 6 + 32)
            def body(i):
                steps = Steps(core, vec, i, vec_per)
                for ins in layer_norm(vec, steps, x, 4 * i, st, False, xn, lambda: wait_last_round(vec, xn_turned, i)):
                    ins.then_inc(xn_ready, 1)
                vec.wait_ge(v_ready, i + 1)
                for j in range(PAIR):
                    vec.scalar_tensor_tensor(out=v[:, j, :, 0:XD], in0=bv[:, :].rearrange("p (h n) -> p h n", h=XH),
                                             scalar=mcol[:, bass.ds(4 * i + j, 1)],
                                             in1=bank[5][:, j * P:(j + 1) * P].rearrange("p (h n) -> p h n", h=XH),
                                             op0=ALU.mult, op1=ALU.add).then_inc(v_copied, 1)
                for j in range(PAIR):
                    for c in range(2):
                        n = 2 * j + c
                        vec.wait_ge(scores_ready, 8 * i + n + 1)
                        first = (6, 0)[c]
                        vec.tensor_reduce(top[:, j, :, MAX_ROW + 2 * c * HEAD_ROWS:MAX_ROW + (2 * c + 1) * HEAD_ROWS + 1:HEAD_ROWS]
                                          .rearrange("p g h -> p h g"),
                                          psum[:, first:first + 2, :].rearrange("p h (g n) -> p h g n", g=2),
                                          AX.X, ALU.max, negate=True).then_inc(tops_ready, 1)
                for g in range(2):
                    vec.wait_ge(tops_turned, 2 * i + g + 1)
                    vec.tensor_tensor(qT_less[:, g, :], bank[2 + g], qT[:, g, :], ALU.add).then_inc(q_lessened, 1)
                for s in range(2):
                    vec.wait_ge(upd_ready, 2 * i + s + 1)
                    got = bank[5 - s][:, 0:2 * XH * (XD + 1)].rearrange("p (t h n) -> p t h n", t=2, h=XH)
                    vec.reciprocal(total[:, 2 * s:2 * s + 2, :], got[:, :, :, XD]).then_inc(totals_ready, 1)
                    vec.wait_ge(totals_ready, 2 * i + s + 1)
                    if s == 0:
                        wait_last_round(vec, upd_turned, i)
                    vec.tensor_tensor(upd[:, 2 * s:2 * s + 2, :].rearrange("p t (h n) -> p t h n", h=XH), got[:, :, :, 0:XD],
                                      total[:, 2 * s:2 * s + 2, :].unsqueeze(3).to_broadcast([P, 2, XH, XD]),
                                      ALU.mult).then_inc(upd_scaled, 1)
                vec.wait_ge(y_ready, i + 1)
                vec.tensor_tensor(x[:, bass.ds(4 * i, PAIR), :], x[:, bass.ds(4 * i, PAIR), :],
                                  bank[3].rearrange("p (j n) -> p j n", j=PAIR), ALU.add).then_inc(y_added, 1)
                assert steps.n == vec_per
            rounds(vec, PAIRS, body)
            core.vector_base += PAIRS * vec_per

        @block.gpsimd
        def _(pool):
            def body(i):
                pool.wait_ge(ctx_loaded, 16 * i + 16)
                pool.wait_ge(mask_loaded, 16 * i + 16)
                wait_last_round(pool, v_ready, i)
                pool.tensor_tensor(ctxT_masked[:, :, :], ctxT[:, :, :],
                                   mask[:, :].unsqueeze(1).to_broadcast([P, 2, WIDE]), ALU.mult).then_inc(ctx_masked, 1)
                pool.wait_ge(xnT_ready, i + 1)
                pool.tensor_tensor(xnT_masked[:, :], xnT[:, :], mask[:, :], ALU.mult).then_inc(q_input_ready, 1)
            rounds(pool, PAIRS, body)


def expert_layer(core, number):
    nc, x, ident, bank = core.nc, core.x, core.ident, core.bank
    w, tables = core.ffn[number], core.moe_tables
    rows_d, outputs_d = core.slots[2 * number:2 * number + 2]
    last = number == 1
    name = f"ffn{number}"
    width, chunk = (F1, P) if last else (F0, F0 // 2)
    chunks = width // chunk
    K = 2
    with ExitStack() as ctx:
        def sb(n, shape, dt=F32):
            return core.sb(ctx, f"{name}_{n}", shape, dt)

        def sem(n):
            return core.sem(f"{name}_{n}")

        st = core.ln_buffers(ctx, f"{name}_ln")
        zero_row = sb("zero_row", [P, D])
        xn = sb("xn", [P, PAIR, D])
        xnT = sb("xnT", [P, WIDE])
        xn_all = sb("xn_all", [P, NT, D])
        clipped = sb("clipped", [P, 2, WIDE])
        hidden = sb("hidden", [P, 2, WIDE])
        logits = sb("logits", [P, NT, E])
        sorted_ = sb("sorted", [P, NT, E])
        order = sb("order", [P, NT, E], U32)
        choice = sb("choice", [P, NT, K])
        onehot = sb("onehot", [P, NT, K, E])
        picked = sb("picked", [P, NT, E])
        picked_b = sb("picked_b", [P, NT, E], BF16)
        upto_b = sb("upto_b", [P, P], BF16)
        ones_b = sb("ones_b", [P, P], BF16)
        soft = sb("soft", [P, NT, E])
        denom = sb("denom", [P, NT])
        weight = sb("weight", [P, NT, K])
        in_tile = sb("in_tile", [P, E, NT])
        before = sb("before", [P, E, NT])
        full = sb("full", [P, E, NT])
        tiles = sb("tiles", [P, E])
        tile_end = sb("tile_end", [P, E])
        first_slot = sb("first_slot", [P, E])
        slot = sb("slot", [P, NT, E])
        slot_sel = sb("slot_sel", [P, NT, K, E])
        slot_f = sb("slot_f", [P, NT, K])
        slot_i = sb("slot_i", [P, K, NT], U32)
        past = sb("past", [1, SLOT_TILES, E])
        owner_f = sb("owner_f", [1, SLOT_TILES])
        owner = sb("owner", [1, SLOT_TILES], I32)
        zero8 = sb("zero8", [P, E])
        row = sb("row", [P, 2, D])
        rowT = sb("rowT", [P, 2, P])
        h = sb("h", [P, 2, width])
        hT = sb("hT", [chunk, 2, chunks * P])
        y = sb("y", [P, 2, D])
        got = sb("got", [P, NT, K, D])

        set_up = sem("set_up")
        zero_filled = sem("zero_filled")
        xn_ready = sem("xn_ready")
        xn_turned = sem("xn_turned")
        xnT_ready = sem("xnT_ready")
        xn_kept = sem("xn_kept")
        logits_ready = sem("logits_ready")
        logits_kept = sem("logits_kept")
        ranks_ready = sem("ranks_ready")
        routed, GAPS, PICKS, SLOTS_KNOWN, OWNERS = sem("routed"), 1, 2, 3, 4
        soft_ready = sem("soft_ready")
        rows_placed = sem("rows_placed")
        row_loaded = [sem(f"row_loaded{s}") for s in range(2)]
        row_turned = sem("row_turned")
        rowT_ready = sem("rowT_ready")
        gate_ready = sem("gate_ready")
        up_ready = sem("up_ready")
        gate_active = sem("gate_active")
        h_ready = sem("h_ready")
        h_turned = sem("h_turned")
        hT_ready = sem("hT_ready")
        out_ready = sem("out_ready")
        out_copied = sem("out_copied")
        out_stored = [sem(f"out_stored{s}") for s in range(2)]
        gathered = [sem(f"gathered{q}") for q in range(PAIRS)]
        combined = sem("combined")
        if last:
            shared_ready = sem("shared_ready")
            shared_clipped = sem("shared_clipped")
            shared_gated = sem("shared_gated")
            shared_hidden = sem("shared_hidden")
            shared_y_ready = sem("shared_y_ready")
            shared_y_added = sem("shared_y_added")
            gate_clipped = sem("gate_clipped")
        vec_per = LN_STEPS_TWICE if last else LN_STEPS
        block = ctx.enter_context(nc.Block())
        STEPS = SLOT_TILES // 2

        @block.sync
        def _(sp):
            sp.wait_ge(set_up, 1)
            for t in range(SLOT_TILES):
                sp.dma_start(rows_d[t * P:(t + 1) * P, :], zero_row[:, :]).then_inc(zero_filled, 16)
            sp.wait_ge(rows_placed, 16 * NT * K)
            def body(i):
                for s in range(2):
                    wait_last_round(sp, row_turned, 2 * i)
                    sp.dma_start(row[:, s, :], rows_d[bass.ds((2 * i + s) * P, P), :]).then_inc(row_loaded[s], 16)
                for s in range(2):
                    sp.wait_ge(out_copied, 2 * i + s + 1)
                    sp.dma_start(outputs_d[bass.ds((2 * i + s) * P, P), :], y[:, s, :]).then_inc(out_stored[s], 16)
            rounds(sp, STEPS, body)

        @block.tensor
        def _(pe):
            core.wait_loaded(pe, name)
            pe.wait_ge(set_up, 5)
            def body(i):
                pe.wait_ge(xn_ready, 4 * i + 4)
                transpose_tiles(pe, bank[0], lambda j: xn[:, j, :], ident[:, :]).then_inc(xn_turned, 1)
                pe.wait_ge(xnT_ready, i + 1)
                wait_last_round(pe, logits_kept, i)
                for j in range(PAIR):
                    mm = pe.matmul(bank[1][:, j * E:(j + 1) * E], xnT[:, j * P:(j + 1) * P], w["router"][:, :],
                                   start=True, stop=True)
                mm.then_inc(logits_ready, 1)
                if last:
                    for a in range(2):
                        pe.matmul(bank[2 + a], w["shared_up"][:, a * FS:(a + 1) * FS], xnT[:, :],
                                  start=True, stop=True).then_inc(shared_ready, 1)
                    pe.wait_ge(shared_hidden, i + 1)
                    wait_last_round(pe, shared_y_added, i)
                    for j in range(PAIR):
                        mm = pe.matmul(bank[4][:, j * P:(j + 1) * P], hidden[:, 0, j * P:(j + 1) * P],
                                       w["shared_down"][:, :], start=True, stop=True)
                    mm.then_inc(shared_y_ready, 1)
            rounds(pe, PAIRS, body)
            pe.wait_ge(routed, PICKS)
            pe.matmul(bank[2][:, 0:NT * E], upto_b[:, :], picked_b[:, :, :].rearrange("p t e -> p (t e)"),
                      start=True, stop=True)
            pe.matmul(bank[3][:, 0:NT * E], ones_b[:, :], picked_b[:, :, :].rearrange("p t e -> p (t e)"),
                      start=True, stop=True).then_inc(ranks_ready, 1)
            pe.wait_ge(routed, OWNERS)
            def body(i):
                own = []
                for s in range(2):
                    own.append(pe.value_load(owner[0:1, bass.ds(2 * i + s, 1)], min_val=0, max_val=E - 1))
                for s in range(2):
                    pe.wait_ge(row_loaded[s], 16 * i + 16)
                    wait_last_round(pe, out_copied, 2 * i)
                    pe.transpose(bank[4 * s][:, 0:P], row[:, s, :], ident[:, :]).then_inc(row_turned, 1)
                for s in range(2):
                    pe.wait_ge(rowT_ready, 2 * i + s + 1)
                    wait_last_round(pe, h_ready, 2 * i)
                    pe.matmul(bank[4 * s + 1][:, 0:width], rowT[:, s, :],
                              w["up"][:, bass.ds(own[s] * (2 * width), width)], start=True, stop=True).then_inc(gate_ready, 1)
                    pe.matmul(bank[4 * s + 2][:, 0:width], rowT[:, s, :],
                              w["up"][:, bass.ds(own[s] * (2 * width) + width, width)],
                              start=True, stop=True).then_inc(up_ready, 1)
                for s in range(2):
                    pe.wait_ge(h_ready, 2 * i + s + 1)
                    for c in range(chunks):
                        mm = pe.transpose(bank[4 * s + 3][0:chunk, c * P:(c + 1) * P], h[:, s, c * chunk:(c + 1) * chunk],
                                          ident[:, :])
                    mm.then_inc(h_turned, 1)
                for s in range(2):
                    pe.wait_ge(hT_ready, 2 * i + s + 1)
                    for c in range(chunks):
                        mm = pe.matmul(bank[4 * s][:, 0:D], hT[:, s, c * P:(c + 1) * P],
                                       w["down"][:, bass.ds(own[s] * (chunks * D) + c * D, D)],
                                       start=(c == 0), stop=(c == chunks - 1))
                    mm.then_inc(out_ready, 1)
            rounds(pe, STEPS, body)

        @block.scalar
        def _(act):
            core.wait_loaded(act, name)

            def turned_copy(out, in_):
                if last:
                    return act.activation(out, in_, ACT.Identity, bias=w["beta"][:, 0:1], scale=w["gamma"][:, 0:1])
                return act.activation(out, in_, ACT.Copy)

            act.preload_act_table(ACT.Silu)
            def body(i):
                act.wait_ge(xn_turned, i + 1)
                turned_copy(xnT[:, :], bank[0]).then_inc(xnT_ready, 1)
                act.activation(xn_all[:, bass.ds(4 * i, PAIR), :], xn[:, :, :], ACT.Copy).then_inc(xn_kept, 1)
                if last:
                    act.wait_ge(shared_clipped, i + 1)
                    act.activation(hidden[:, 1, :], clipped[:, 0, :], ACT.Silu).then_inc(shared_gated, 1)
            rounds(act, PAIRS, body)
            act.wait_ge(routed, GAPS)
            act.activation(soft[:, :, :], soft[:, :, :], ACT.Exp).then_inc(soft_ready, 1)
            act.preload_act_table(ACT.Silu)
            def body(i):
                for s in range(2):
                    act.wait_ge(row_turned, 2 * i + s + 1)
                    turned_copy(rowT[:, s, :], bank[4 * s][:, 0:P]).then_inc(rowT_ready, 1)
                for s in range(2):
                    if last:
                        act.wait_ge(gate_clipped, 2 * i + s + 1)
                        act.activation(clipped[:, s, 0:width], clipped[:, s, 0:width], ACT.Silu).then_inc(gate_active, 1)
                    else:
                        act.wait_ge(gate_ready, 2 * i + s + 1)
                        wait_last_round(act, h_ready, 2 * i)
                        act.activation(clipped[:, s, 0:width], bank[4 * s + 1][:, 0:width], ACT.Silu).then_inc(gate_active, 1)
                for s in range(2):
                    act.wait_ge(h_turned, 2 * i + s + 1)
                    act.activation(hT[:, s, :], bank[4 * s + 3][0:chunk, 0:chunks * P], ACT.Copy).then_inc(hT_ready, 1)
                for s in range(2):
                    act.wait_ge(out_ready, 2 * i + s + 1)
                    wait_last_round(act, out_stored[s], 16 * i)
                    act.activation(y[:, s, :], bank[4 * s][:, 0:D], ACT.Copy).then_inc(out_copied, 1)
            rounds(act, STEPS, body)

        @block.vector
        def _(vec):
            core.wait_loaded(vec, name)
            vec.memset(zero_row[:, :], 0.0).then_inc(set_up, 1)
            vec.tensor_copy(upto_b[:, :], tables["upto_tile"][:, :]).then_inc(set_up, 1)
            vec.memset(ones_b[:, :], 1.0).then_inc(set_up, 1)
            vec.memset(zero8[:, :], 0.0).then_inc(set_up, 1)
            vec.memset(clipped[:, :, :], 0.0).then_inc(set_up, 1)
            vec.wait_ge(set_up, 5)
            def body(i):
                steps = Steps(core, vec, i, vec_per)

                def before_write():
                    wait_last_round(vec, xn_turned, i)
                    wait_last_round(vec, xn_kept, i)

                for ins in layer_norm(vec, steps, x, 4 * i, st, last, xn, before_write):
                    ins.then_inc(xn_ready, 1)
                vec.wait_ge(logits_ready, i + 1)
                vec.tensor_copy(logits[:, bass.ds(4 * i, PAIR), :],
                                bank[1][:, 0:PAIR * E].rearrange("p (j e) -> p j e", e=E)).then_inc(logits_kept, 1)
                if last:
                    vec.wait_ge(shared_ready, 2 * i + 2)
                    vec.tensor_scalar(clipped[:, 0, :], bank[2], -GATE_LIMIT, GATE_LIMIT, ALU.max,
                                      ALU.min).then_inc(shared_clipped, 1)
                    vec.wait_ge(shared_gated, i + 1)
                    vec.tensor_tensor(hidden[:, 0, :], hidden[:, 1, :], bank[3], ALU.mult).then_inc(shared_hidden, 1)
                    vec.wait_ge(shared_y_ready, i + 1)
                    vec.tensor_tensor(x[:, bass.ds(4 * i, PAIR), :], x[:, bass.ds(4 * i, PAIR), :],
                                      bank[4].rearrange("p (j n) -> p j n", j=PAIR), ALU.add).then_inc(shared_y_added, 1)
                assert steps.n == vec_per
            rounds(vec, PAIRS, body)
            core.vector_base += PAIRS * vec_per

            sort = Steps(core, vec)

            def do(ins):
                sort.done(ins)
                sort.wait()

            vec.wait_ge(logits_kept, PAIRS)
            for t in range(NT):
                sort.done(vec.max(sorted_[:, t, :], logits[:, t, :]))
            sort.wait()
            for t in range(NT):
                sort.done(vec.max_index(order[:, t, :], sorted_[:, t, :], logits[:, t, :]))
            vec.tensor_tensor(soft[:, :, :], sorted_[:, :, :], sorted_[:, :, 0:1].to_broadcast([P, NT, E]),
                              ALU.subtract).then_inc(routed, 1)
            sort.wait()
            do(vec.tensor_copy(choice[:, :, :], order[:, :, 0:K]))
            experts = tables["expert"][:, :].unsqueeze(1)
            for k in range(K):
                sort.done(vec.tensor_tensor(onehot[:, :, k, :], experts.to_broadcast([P, NT, E]),
                                            choice[:, :, k:k + 1].to_broadcast([P, NT, E]), ALU.is_equal))
            sort.wait()
            vec.tensor_tensor(picked_b[:, :, :], onehot[:, :, 0, :], onehot[:, :, 1, :], ALU.add).then_inc(routed, 1)
            vec.wait_ge(soft_ready, 1)
            do(vec.tensor_reduce(denom[:, :], soft[:, :, 0:K] if last else soft[:, :, :], AX.X, ALU.add))
            do(vec.reciprocal(denom[:, :], denom[:, :]))
            do(vec.tensor_tensor(weight[:, :, :], soft[:, :, 0:K], denom[:, :].unsqueeze(2).to_broadcast([P, NT, K]), ALU.mult))
            vec.wait_ge(ranks_ready, 1)
            do(vec.tensor_copy(in_tile[:, :, :], bank[3][:, 0:NT * E].rearrange("p (t e) -> p e t", e=E)))
            do(vec.tensor_tensor_scan(out=before[:, :, :].rearrange("p e t -> p (e t)"), data0=tables["not_first"][:, :],
                                      data1=in_tile[:, :, :].rearrange("p e t -> p (e t)"), initial=0.0,
                                      op0=ALU.mult, op1=ALU.add))
            do(vec.tensor_tensor(full[:, :, :], before[:, :, NT - 1:NT].to_broadcast([P, E, NT]),
                                 tables["full_at"][:, :].unsqueeze(1).to_broadcast([P, E, NT]), ALU.is_gt))
            do(vec.tensor_reduce(tiles[:, :], full[:, :, :], AX.X, ALU.add))
            do(vec.tensor_tensor_scan(out=tile_end[:, :], data0=tiles[:, :], data1=zero8[:, :], initial=0.0,
                                      op0=ALU.add, op1=ALU.add))
            do(vec.tensor_tensor(first_slot[:, :], tile_end[:, :], tiles[:, :], ALU.subtract))
            do(vec.tensor_scalar(first_slot[:, :], first_slot[:, :], float(P), -1.0, ALU.mult, ALU.add))
            do(vec.tensor_tensor(before[:, :, :], before[:, :, :], in_tile[:, :, :], ALU.subtract))
            do(vec.tensor_tensor(before[:, :, :], before[:, :, :], first_slot[:, :].unsqueeze(2).to_broadcast([P, E, NT]), ALU.add))
            do(vec.tensor_tensor(slot[:, :, :], bank[2][:, 0:NT * E].rearrange("p (t e) -> p t e", e=E),
                                 before[:, :, :].rearrange("p e t -> p t e"), ALU.add))
            for k in range(K):
                sort.done(vec.tensor_tensor(slot_sel[:, :, k, :], onehot[:, :, k, :], slot[:, :, :], ALU.mult))
            sort.wait()
            do(vec.tensor_reduce(slot_f[:, :, :], slot_sel[:, :, :, :], AX.X, ALU.add))
            vec.tensor_copy(slot_i[:, :, :], slot_f[:, :, :].rearrange("p t k -> p k t")).then_inc(routed, 1)
            do(vec.tensor_tensor(past[:, :, :], tile_end[0:1, :].unsqueeze(1).to_broadcast([1, SLOT_TILES, E]),
                                 tables["tile_index"][0:1, :].unsqueeze(2).to_broadcast([1, SLOT_TILES, E]), ALU.is_le))
            do(vec.tensor_reduce(owner_f[:, :], past[:, :, :], AX.X, ALU.add))
            vec.tensor_scalar(owner[:, :], owner_f[:, :], float(E - 1), None, ALU.min).then_inc(routed, 1)
            sort.close()
            def body(i):
                if last:
                    for s in range(2):
                        vec.wait_ge(gate_ready, 2 * i + s + 1)
                        vec.tensor_scalar(clipped[:, s, :], bank[4 * s + 1], -GATE_LIMIT, GATE_LIMIT, ALU.max,
                                          ALU.min).then_inc(gate_clipped, 1)
                for s in range(2):
                    vec.wait_ge(gate_active, 2 * i + s + 1)
                    vec.wait_ge(up_ready, 2 * i + s + 1)
                    wait_last_round(vec, h_turned, 2 * i)
                    vec.tensor_tensor(h[:, s, :], clipped[:, s, 0:width], bank[4 * s + 2][:, 0:width],
                                      ALU.mult).then_inc(h_ready, 1)
            rounds(vec, STEPS, body)
            for t in range(NT):
                if t % PAIR == 0:
                    vec.wait_ge(gathered[t // PAIR], 16 * K * PAIR)
                for k in range(K):
                    if k:
                        vec.wait_ge(combined, K * t + k)
                    vec.scalar_tensor_tensor(out=x[:, t, :], in0=got[:, t, k, :], scalar=weight[:, t, k:k + 1],
                                             in1=x[:, t, :], op0=ALU.mult, op1=ALU.add).then_inc(combined, 1)

        @block.gpsimd
        def _(pool):
            pool.wait_ge(zero_filled, 16 * SLOT_TILES)
            pool.wait_ge(xn_kept, PAIRS)
            pool.wait_ge(routed, SLOTS_KNOWN)
            for t in range(NT):
                for k in range(K):
                    pool.indirect_dma_start(out=rows_d, out_offset=bass.IndirectOffsetOnAxis(ap=slot_i[:, k, t:t + 1], axis=0),
                                            in_=xn_all[:, t, :], in_offset=None).then_inc(rows_placed, 16)
            for s in range(2):
                pool.wait_ge(out_stored[s], 16 * STEPS)
            for t in range(NT):
                for k in range(K):
                    pool.indirect_dma_start(out=got[:, t, k, :], out_offset=None, in_=outputs_d,
                                            in_offset=bass.IndirectOffsetOnAxis(ap=slot_i[:, k, t:t + 1], axis=0)
                                            ).then_inc(gathered[t // PAIR], 16)


def first_expert_layer(core):
    expert_layer(core, 0)


def second_expert_layer(core):
    expert_layer(core, 1)


def load_x(core):
    with ExitStack() as ctx:
        block = ctx.enter_context(core.nc.Block())

        @block.sync
        def _(sp):
            for layer in LOAD_ORDER:
                for buffer, source in core.loads[layer]:
                    sp.dma_start(buffer, source).then_inc(core.loaded[layer], 16)
            for layer in core.loads:
                core.wait_loaded(sp, layer)


def store_x(core, out):
    with ExitStack() as ctx:
        stored = core.sem("stored")
        block = ctx.enter_context(core.nc.Block())

        @block.sync
        def _(sp):
            sp.dma_start(out.rearrange("(t p) d -> p t d", p=P), core.x[:, :, :]).then_inc(stored, 16)
            sp.wait_ge(stored, 16)


LAYERS = [retention_layer, depool_layer, first_expert_layer, conv_layer, cross_attention_layer,
          second_expert_layer]


def decoder_kernel(nc, arg, out, layers=6):
    with ExitStack() as ctx:
        core = Core(nc, ctx, arg)
        for n, layer in enumerate(LAYERS[:layers]):
            layer(core)
            if layer in (depool_layer, load_x):
                core.early.close()
        store_x(core, out)


def half_swapped(w):
    return w.reshape(RH, 2, RQK // 2, D)[:, ::-1].reshape(RH * RQK, D)


def constants():
    f64 = np.float64
    c = {"ident": np.eye(P, dtype=np.float32)}
    inv = 1.0 / 10000.0 ** (np.arange(0, RQK, 2, dtype=f64) / RQK)
    ang = (np.arange(S, dtype=np.float32)[None, :] * inv.astype(np.float32)[:, None]).astype(np.float32).astype(f64)
    decay = np.log1p(-np.exp2(-5.0 - np.arange(RH)))
    t = np.arange(S)
    rope = np.zeros((P, 4, S))
    for h in range(RH):
        r = slice(h * RQK, (h + 1) * RQK)
        cos, sin = np.tile(np.cos(ang), (2, 1)), np.concatenate([-np.sin(ang), np.sin(ang)])
        up, down = np.exp(decay[h] * t) * RQK ** -0.5, np.exp(-decay[h] * t)
        rope[r, 0], rope[r, 1], rope[r, 2], rope[r, 3] = cos * up, sin * up, cos * down, sin * down
    c["rope"] = rope.reshape(P, -1).astype(np.float32)
    tri = np.triu(np.ones((P, P)))
    c["causal"] = np.concatenate([tri, np.ones((P, P)), tri], 1).astype(np.float32)
    p = np.arange(P)
    c["index"] = np.stack([p, p + P, p + 1, p + 1 + P, np.where(p > 0, -1.0, 0.0), -np.ones(P)], 1).astype(np.float32)
    c["upto"] = np.concatenate([tri, np.ones((P, P))], 1).astype(np.float32)
    k, t = np.arange(S), np.arange(S)
    phase = 2 * np.pi * np.outer(t, k) / FFT
    dft = np.concatenate([np.cos(phase), -np.sin(phase)], 1)
    dft[:, S] = np.where(t % 2, -1.0, 1.0)
    idft = np.concatenate([2 * np.cos(phase).T, -2 * np.sin(phase).T], 0) / FFT
    idft[0] = 1.0 / FFT
    idft[S] = np.where(t % 2, -1.0, 1.0) / FFT
    c["dft"], c["idft"] = dft.astype(np.float32), idft.astype(np.float32)
    c["time"] = np.tile(np.arange(P, dtype=np.float32), (P, 1))
    c["half"] = np.stack([p < N_STATE, p >= N_STATE], 1).astype(np.float32)
    c["upto_tile"] = c["upto"][:, :P]
    c["expert"] = np.tile(np.arange(E, dtype=np.float32), (P, 1))
    c["not_first"] = np.tile((np.arange(E * NT) % NT > 0).astype(np.float32), (P, 1))
    c["full_at"] = np.tile(np.arange(NT, dtype=np.float32) * P, (P, 1))
    c["tile_index"] = np.tile(np.arange(SLOT_TILES, dtype=np.float32), (P, 1))
    c["packed"] = np.stack([p == 0, p > 0], 1).astype(np.float32)
    return c


def by_pair(w):
    return w.reshape(D // 2, 2 * N_STATE).T


def head_padded(w):
    out = np.zeros((w.shape[0], XH, HEAD_ROWS), w.dtype)
    out[:, :, :XD] = w.reshape(-1, XH, XD)
    return out.reshape(w.shape[0], XH * HEAD_ROWS)


def aux_rows(bias, one_row):
    out = np.zeros((AUX, XH, HEAD_ROWS), bias.dtype)
    out[AUX_MASK] = head_padded(bias[None]).reshape(XH, HEAD_ROWS)
    out[AUX_ONE, :, one_row] = 1.0
    return out


def laid_out(inp):
    def cat(*a):
        return np.concatenate(a, 1)
    a = constants()
    a["x"] = inp["x"].reshape(B * S, D)
    wq, wk = inp["L0_attn_Wq"], inp["L0_attn_Wk"]
    a["wqk"] = cat(wq.T, half_swapped(wq).T, wk.T, half_swapped(wk).T)
    a["wvg"] = cat(inp["L0_attn_Wv"].T, inp["L0_attn_Wg"].T)
    a["wo"] = inp["L0_attn_Wo"].T
    a["gnorm"] = np.tile(inp["L0_attn_g_norm_w"], (P, RH))
    a["lens"] = inp["mask_BxS2_if0"]
    a["ctx"] = inp["ctx_2048"].reshape(B * S, DC)
    a["ginit"] = np.tile(inp["L0_xattn_g_init"][:D], (P, 1))
    a["gres"] = inp["L0_xattn_g_res"][:, None]
    a["dep_win"] = inp["L0_xattn_W_in"].T
    a["dep_bin"] = inp["L0_xattn_b_in"][None]
    for name, key in (("alog", "A_log"), ("b", "B"), ("c", "C")):
        a["conv_" + name] = by_pair(inp["L1_attn_" + key])
    a["conv_dt"] = by_pair(np.repeat(inp["L1_attn_dt"][:, None], N_STATE, 1))
    a["conv_skip"] = inp["L1_attn_Dp"][None]
    a["conv_win"], a["conv_wout"] = inp["L1_attn_Win"].T, inp["L1_attn_Wout"].T
    a["conv_bin"], a["conv_bout"] = inp["L1_attn_bin_"][None], inp["L1_attn_bout"][None]
    for name, layer, router, up, down, width, chunk in (
            ("ffn0", "L0_ffn_", "router_weight", "w1", "w2", F0, F0 // 2),
            ("ffn1", "L1_ffn_", "router_w", "gate_up_w", "down_w", F1, P)):
        a[name + "_router"] = inp[layer + router]
        a[name + "_up"] = inp[layer + up].transpose(1, 0, 2).reshape(D, E * 2 * width)
        a[name + "_down"] = inp[layer + down].reshape(E, width // chunk, chunk, D).transpose(2, 0, 1, 3).reshape(chunk, -1)
    a["ffn1_gamma"], a["ffn1_beta"] = inp["L1_ffn_ln_gamma"][:, None], inp["L1_ffn_ln_beta"][:, None]
    a["ffn1_shared_up"], a["ffn1_shared_down"] = inp["L1_ffn_shared_gate_up_w"], inp["L1_ffn_shared_down_w"]
    a["ctxT"] = inp["ctx_2048"].reshape(B * S, DC).T
    a["mask"] = inp["mask_BxS2_fk1"].reshape(1, B * S)
    a["mcol"] = inp["mask_BxS2_fk1"].reshape(NT, P).T
    wsrc, bsrc = inp["L1_xattn_W_src"].T, inp["L1_xattn_b_src"]
    a["xat_wk"], a["xat_wv"] = head_padded(wsrc[:, :D]), wsrc[:, D:]
    a["xat_wq"] = head_padded(inp["L1_xattn_W_tgt"].T)
    kaux = aux_rows(bsrc[:D], MAX_ROW)
    kaux[AUX_BIAS, :, MASK_ROW] = 1.0
    a["xat_kaux"] = kaux.reshape(AUX, -1)
    a["xat_qaux"] = aux_rows(inp["L1_xattn_b_tgt"], MASK_ROW).reshape(AUX, -1)
    a["xat_bv"] = np.tile(bsrc[D:], (P, 1))
    a["xat_wout"] = inp["L1_xattn_W_out"].T
    a["xat_bout"] = inp["L1_xattn_b_out"][None]
    return {k: np.ascontiguousarray(v) for k, v in a.items()}


def build(nc, arrays, layers=6):
    arg = {k: nc.dram_tensor(f"in_{k}", v.shape, mybir.dt.from_np(v.dtype), kind="ExternalInput").ap()
           for k, v in arrays.items()}
    out = nc.dram_tensor("out_x", (B * S, D), F32, kind="ExternalOutput").ap()
    decoder_kernel(nc, arg, out, layers)


def kernel(**inputs):
    import concourse.bacc as bacc
    from concourse.bass_utils import run_bass_kernel_spmd

    arrays = laid_out({k: np.asarray(v) for k, v in inputs.items()})
    nc = bacc.Bacc("TRN2", target_bir_lowering=False, num_devices=1)
    build(nc, arrays)
    r = run_bass_kernel_spmd(nc, [{f"in_{k}": v for k, v in arrays.items()}], core_ids=[0])
    return r.results[0]["out_x"].reshape(B, S, D)
```

```python
from contextlib import ExitStack

import numpy as np

import concourse.bass as bass
from concourse import mybir

ALU = mybir.AluOpType
ACT = mybir.ActivationFunctionType
AX = mybir.AxisListType
F32 = mybir.dt.float32
BF16 = mybir.dt.bfloat16
I32 = mybir.dt.int32
U32 = mybir.dt.uint32

P = 128
B, S, D = 8, 256, 128
DC = 256
NT = B * S // P
PAIR = 4
PAIRS = NT // PAIR
WIDE = PAIR * P
LN_EPS = 1e-5
RSQRT_MAGIC = float(0x5F3759DF)

RH, RQK, RV = 4, 32, 64
CAUSAL = 384
DEPOOL_DT = float(-np.log(-np.expm1(np.float32(-0.001))))
DEPOOL_B = float(np.exp(np.float32(-0.001)))
E = 8
SLOT_TILES = 2 * NT + E
GATE_LIMIT = 10.0
SLOTS = SLOT_TILES * P
F0, F1, FS = 176, 512, 128
N_STATE = 64
FFT = 2 * S
XH, XD = 8, 16
MASKED = -1e30
HEAD_ROWS = 32
MASK_ROW, MAX_ROW = XD, XD + 1


LOAD_ORDER = ("ret", "dep", "ffn0", "conv", "xat", "ffn1")


class Steps:

    def __init__(self, core, engine, i=0, per_body=0):
        self.core, self.engine, self.i, self.per_body, self.n = core, engine, i, per_body, 0
        self.sem, self.base = core.vector_steps, core.vector_base

    def done(self, ins):
        self.n += 1
        return ins.then_inc(self.sem, 1)

    def wait(self):
        self.engine.wait_ge(self.sem, self.i * self.per_body + (self.base + self.n))

    def close(self):
        self.core.vector_base += self.n


def rounds(engine, n, body):
    body(0)
    with engine.Fori(1, n) as i:
        body(i)


def turns(engine, n, body):
    body(0, True)
    with engine.Fori(1, n - 1) as i:
        body(i, True)
    body(n - 1, False)


def stream_tiles(engine, n_tiles, step):
    for n in range(2):
        step(n, n)
    with engine.Fori(1, n_tiles // 2 - 1) as i:
        for s in range(2):
            step(2 * i + s, s)
    for n in range(n_tiles - 2, n_tiles + 2):
        step(n, n % 2)


def is_tile(n, n_tiles=SLOT_TILES):
    return not isinstance(n, int) or 0 <= n < n_tiles


def wait_tiles(engine, sem, count):
    if not isinstance(count, int) or count > 0:
        engine.wait_ge(sem, count)


def wait_last_round(engine, sem, value):
    if not isinstance(value, int) or value > 0:
        engine.wait_ge(sem, value)


def rsqrt(vec, steps, out, v, tmp):
    steps.done(vec.tensor_scalar(tmp.bitcast(I32), v.bitcast(I32), 1, None, ALU.logical_shift_right))
    steps.wait()
    steps.done(vec.tensor_scalar(out.bitcast(I32), tmp.bitcast(I32), -1.0, RSQRT_MAGIC, ALU.mult, ALU.add))
    for _ in range(3):
        steps.wait()
        steps.done(vec.tensor_tensor(tmp, out, out, ALU.mult))
        steps.wait()
        steps.done(vec.scalar_tensor_tensor(out=tmp, in0=tmp, scalar=-0.5, in1=v, op0=ALU.mult, op1=ALU.mult))
        steps.wait()
        steps.done(vec.scalar_tensor_tensor(out=out, in0=tmp, scalar=1.5, in1=out, op0=ALU.add, op1=ALU.mult))


def moments(core, vec, st, twice):
    steps = Steps(core, vec)
    raw, mean, diff, v, r, tmp = (st[k] for k in ("raw", "mean", "diff", "v", "r", "tmp"))

    def do(ins):
        steps.done(ins)
        steps.wait()

    for t in range(NT):
        steps.done(vec.bn_stats(raw[:, t, :], core.x[:, t, :]))
    steps.wait()
    steps.done(vec.tensor_tensor(mean[:, :], raw[:, :, 1], raw[:, :, 4], ALU.add))
    steps.done(vec.tensor_tensor(diff[:, :], raw[:, :, 1], raw[:, :, 4], ALU.subtract))
    do(vec.tensor_tensor(v[:, :], raw[:, :, 2], raw[:, :, 5], ALU.add))
    steps.done(vec.tensor_scalar(mean[:, :], mean[:, :], 0.5, None, ALU.mult))
    steps.done(vec.tensor_scalar(v[:, :], v[:, :], 1.0 / D, None, ALU.mult))
    do(vec.scalar_tensor_tensor(out=diff[:, :], in0=diff[:, :], scalar=0.25, in1=diff[:, :],
                                op0=ALU.mult, op1=ALU.mult))
    do(vec.tensor_tensor(diff[:, :], v[:, :], diff[:, :], ALU.add))
    do(vec.tensor_scalar(v[:, :], diff[:, :], LN_EPS, None, ALU.add))
    rsqrt(vec, steps, r[:, :], v[:, :], tmp[:, :])
    steps.wait()
    if twice:
        do(vec.tensor_tensor(diff[:, :], diff[:, :], r[:, :], ALU.mult))
        do(vec.tensor_tensor(diff[:, :], diff[:, :], r[:, :], ALU.mult))
        do(vec.tensor_scalar(v[:, :], diff[:, :], LN_EPS, None, ALU.add))
        rsqrt(vec, steps, st["r2"][:, :], v[:, :], tmp[:, :])
        steps.wait()
        do(vec.tensor_tensor(r[:, :], r[:, :], st["r2"][:, :], ALU.mult))
    steps.close()


def normalize(core, vec, st, i, xn):
    return [vec.tensor_scalar(xn[:, j, :], core.x[:, bass.ds(4 * i + j, 1), :], st["mean"][:, bass.ds(4 * i + j, 1)],
                              st["r"][:, bass.ds(4 * i + j, 1)], ALU.subtract, ALU.mult) for j in range(PAIR)]


class Core:

    def __init__(self, nc, ctx, arg):
        self.nc, self.ctx, self.arg = nc, ctx, arg
        self.loads = {}
        self.loaded = {}
        self.psum = ctx.enter_context(nc.psum_tensor("psum", [P, 8, 512], F32))
        self.vector_steps, self.vector_base = self.sem("vector_steps"), 0
        self.bank = [self.psum[:, i, :] for i in range(8)]

        self.x = self.preload("ret", "x", [P, NT, D], arg["x"].rearrange("(t p) d -> p t d", p=P))
        self.ident = self.preload("ret", "ident", [P, P], arg["ident"])
        self.ffn = []
        for name, width, chunk in (("ffn0", F0, F0 // 2), ("ffn1", F1, P)):
            chunks = width // chunk
            w = {
                "router": self.preload(name, "router", [P, E], arg[name + "_router"]),
                "up": self.preload(name, "up", [P, E * 2 * width], arg[name + "_up"]),
                "down": self.preload(name, "down", [chunk, E * chunks * D], arg[name + "_down"]),
            }
            if name == "ffn1":
                w["gamma"] = self.preload(name, "gamma", [P, 1], arg["ffn1_gamma"])
                w["beta"] = self.preload(name, "beta", [P, 1], arg["ffn1_beta"])
                w["shared_up"] = self.preload(name, "shared_up", [P, 2 * FS], arg["ffn1_shared_up"])
                w["shared_down"] = self.preload(name, "shared_down", [FS, D], arg["ffn1_shared_down"])
            self.ffn.append(w)
        self.moe_tables = {k: self.preload("ffn0", k, [P, n], arg[k]) for k, n in
                           (("expert", E), ("upto_tile", P), ("not_first", E * NT), ("full_at", NT), ("tile_index", SLOT_TILES))}
        self.slots = [nc.dram_tensor(f"{kind}{n}", (SLOTS, D), F32, kind="Internal").ap()
                      for n in range(2) for kind in ("slot_rows", "slot_outputs")]
        self.conv = {
            "alog": self.preload("conv", "alog", [P, D // 2], arg["conv_alog"]),
            "b": self.preload("conv", "b", [P, D // 2], arg["conv_b"]),
            "c": self.preload("conv", "c", [P, D // 2], arg["conv_c"]),
            "dt": self.preload("conv", "dt", [P, D // 2], arg["conv_dt"]),
            "skip": self.preload("conv", "skip", [1, D], arg["conv_skip"]),
            "half": self.preload("conv", "half", [P, 2], arg["half"]),
            "time": self.preload("conv", "time", [P, P], arg["time"]),
            "dft": self.preload("conv", "dft", [P, 2, FFT], arg["dft"].rearrange("(a p) n -> p a n", p=P)),
            "idft": self.preload("conv", "idft", [P, 4, S], arg["idft"].rearrange("(a p) n -> p a n", p=P)),
            "packed": self.preload("conv", "packed", [P, 2], arg["packed"]),
            "win": self.preload("conv", "win", [P, D], arg["conv_win"]),
            "bin": self.preload("conv", "bin", [1, D], arg["conv_bin"]),
            "wout": self.preload("conv", "wout", [P, D], arg["conv_wout"]),
            "bout": self.preload("conv", "bout", [1, D], arg["conv_bout"]),
        }
        self.xat = {
            "qmask": self.preload("xat", "qmask", [P, B * S], arg["mask"].to_broadcast([P, B * S])),
            "rows": self.preload("xat", "rows", [P, 3], arg["xat_rows"]),
            "spread": self.preload("xat", "spread", [P, P], arg["spread"]),
            "wk": self.preload("xat", "wk", [P, 2, 2 * P], arg["xat_wk"].rearrange("(a p) n -> p a n", p=P)),
            "wv": self.preload("xat", "wv", [P, 2, D], arg["xat_wv"].rearrange("(a p) n -> p a n", p=P)),
            "wq": self.preload("xat", "wq", [P, 2 * P], arg["xat_wq"]),
            "kbias": self.preload("xat", "kbias", [P, 2], arg["xat_kbias"]),
            "qbias": self.preload("xat", "qbias", [P, 2], arg["xat_qbias"]),
            "bv": self.preload("xat", "bv", [P, D], arg["xat_bv"]),
            "wout": self.preload("xat", "wout", [P, 3, D], arg["xat_wout"].rearrange("(a p) n -> p a n", p=P)),
            "bout": self.preload("xat", "bout", [P, D], arg["xat_bout"]),
        }
        self.early = ExitStack()
        self.ret = {
            "wqk": self.preload_early("ret", "wqk", [P, 4, P], arg["wqk"].rearrange("p (a n) -> p a n", a=4)),
            "rope": self.preload_early("ret", "rope", [P, 4, S], arg["rope"].rearrange("p (a n) -> p a n", a=4)),
            "wvg": self.preload_early("ret", "wvg", [P, 2 * RH * RV], arg["wvg"]),
            "causal": self.preload_early("ret", "causal", [P, CAUSAL], arg["causal"]),
            "wo": self.preload_early("ret", "wo", [P, 2, D], arg["wo"].rearrange("(a p) n -> p a n", p=P)),
            "gnorm": self.preload_early("ret", "gnorm", [P, RH * RV], arg["gnorm"]),
        }
        self.dep = {
            "lens": self.preload_early("dep", "lens", [P, B, S], arg["lens"].rearrange("(o b) s -> o b s", o=1).to_broadcast([P, B, S]), I32),
            "ctx": self.preload_early("dep", "ctx", [P, NT, DC], arg["ctx"].rearrange("(t p) d -> p t d", p=P)),
            "ginit": self.preload_early("dep", "ginit", [P, D], arg["ginit"]),
            "index": self.preload_early("dep", "index", [P, 6], arg["index"]),
            "upto": self.preload_early("dep", "upto", [P, S], arg["upto"]),
            "gres": self.preload_early("dep", "gres", [P, 1], arg["gres"]),
            "win": self.preload_early("dep", "win", [P, D], arg["dep_win"]),
            "bin": self.preload_early("dep", "bin", [1, D], arg["dep_bin"]),
        }

    def sb(self, ctx, name, shape, dt=F32):
        return ctx.enter_context(self.nc.sbuf_tensor(name, shape, dt))

    def preload_early(self, layer, name, shape, source, dt=F32):
        return self.preload(layer, name, shape, source, dt, self.early)

    def preload(self, layer, name, shape, source, dt=F32, ctx=None):
        buffer = self.sb(ctx or self.ctx, f"{layer}_{name}", shape, dt)
        if layer not in self.loads:
            self.loads[layer], self.loaded[layer] = [], self.sem(f"{layer}_loaded")
        self.loads[layer].append((buffer[tuple(slice(None) for _ in shape)], source))
        return buffer

    def wait_loaded(self, engine, layer):
        engine.wait_ge(self.loaded[layer], 16 * len(self.loads[layer]))

    def sem(self, name):
        return self.ctx.enter_context(self.nc.semaphore(name))

    def ln_buffers(self, ctx, name):
        st = {k: self.sb(ctx, f"{name}_{k}", [P, NT]) for k in ("mean", "diff", "v", "r", "r2", "tmp")}
        st["raw"] = self.sb(ctx, f"{name}_raw", [P, NT, 6])
        return st


def transpose_tiles(pe, bank, tiles, ident, n=PAIR):
    for j in range(n):
        ins = pe.transpose(bank[:, j * P:(j + 1) * P], tiles(j), ident)
    return ins


def retention_layer(core):
    nc, arg, x, ident, bank = core.nc, core.arg, core.x, core.ident, core.bank
    with ExitStack() as ctx:
        def sb(name, shape, dt=F32):
            return core.sb(ctx, "ret_" + name, shape, dt)

        def sem(name):
            return core.sem("ret_" + name)

        wqk, rope, wvg, causal, wo, gnorm = (core.ret[k] for k in ("wqk", "rope", "wvg", "causal", "wo", "gnorm"))
        st = core.ln_buffers(ctx, "ret_ln")
        xn = sb("xn", [P, PAIR, D])
        xnT = sb("xnT", [P, WIDE])
        rot = sb("rot", [P, 4, WIDE])
        qT = sb("qT", [P, WIDE])
        kT = sb("kT", [P, WIDE])
        v = sb("v", [P, PAIR, RH * RV])
        gate = sb("gate", [P, PAIR, RH * RV])
        scores = sb("scores", [P, 2, RH, CAUSAL])
        osq = sb("osq", [P, PAIR, RH * RV])
        ms = sb("ms", [P, PAIR * RH])
        rms = sb("rms", [P, PAIR * RH])
        mtmp = sb("mtmp", [P, PAIR * RH])
        o = sb("o", [P, PAIR, RH * RV])
        oT = sb("oT", [P, 2, WIDE])

        xn_ready = sem("xn_ready")
        xn_turned = sem("xn_turned")
        xnT_ready = sem("xnT_ready")
        qk_ready = sem("qk_ready")
        rot_ready = sem("rot_ready")
        qk_rotated = sem("qk_rotated")
        vg_ready = sem("vg_ready")
        vg_read = sem("vg_read")
        scores_ready = sem("scores_ready")
        scores_masked = sem("scores_masked")
        o_ready = sem("o_ready")
        osq_ready = sem("osq_ready")
        o_scaled = sem("o_scaled")
        o_gated = sem("o_gated")
        o_turned = sem("o_turned")
        oT_ready = sem("oT_ready")
        y_ready = sem("y_ready")
        y_added = sem("y_added")
        vec_per = 1 + 1 + 11
        block = ctx.enter_context(nc.Block())

        @block.sync
        def _(sp):
            for layer in LOAD_ORDER:
                for buffer, source in core.loads[layer]:
                    sp.dma_start(buffer, source).then_inc(core.loaded[layer], 16)

        @block.tensor
        def _(pe):
            core.wait_loaded(pe, "ret")
            def body(i):
                pe.wait_ge(xn_ready, 4 * i + 4)
                transpose_tiles(pe, bank[0], lambda j: xn[:, j, :], ident[:, :]).then_inc(xn_turned, 1)
                pe.wait_ge(xnT_ready, i + 1)
                wait_last_round(pe, y_added, i)
                for a in range(4):
                    pe.matmul(bank[1 + a][:, :], wqk[:, a, :], xnT[:, :], start=True, stop=True).then_inc(qk_ready, 1)
                for j in range(PAIR):
                    pe.matmul(bank[(5 + j) % 8][:, :], xnT[:, j * P:(j + 1) * P], wvg[:, :],
                              start=True, stop=True).then_inc(vg_ready, 1)
                pe.wait_ge(qk_rotated, 2 * i + 2)
                for s in range(2):
                    if s == 0:
                        pe.wait_ge(rot_ready, 4 * i + 4)
                    for h in range(RH):
                        if s == 1:
                            pe.wait_ge(vg_read, 8 * i + 2 * h + 2)
                        rows, at = slice(h * RQK, (h + 1) * RQK), s * S
                        bk = bank[(1 + 4 * s + h) % 8]
                        pe.matmul(bk[:, 0:S], kT[rows, at:at + P], qT[rows, at:at + S], start=True, stop=True)
                        pe.matmul(bk[:, S:CAUSAL], kT[rows, at + P:at + S], qT[rows, at + P:at + S],
                                  start=True, stop=True).then_inc(scores_ready, 1)
                pe.wait_ge(vg_read, 8 * i + 8)
                for s in range(2):
                    pe.wait_ge(scores_masked, 8 * i + 4 * s + 4)
                    bk = bank[1 + 4 * s]
                    for h in range(RH):
                        vh = slice(h * RV, (h + 1) * RV)
                        out0 = bk[:, h * RV:(h + 1) * RV]
                        out1 = bk[:, S + h * RV:S + (h + 1) * RV]
                        pe.matmul(out0, scores[:, s, h, 0:P], v[:, 2 * s, vh], start=True, stop=True)
                        pe.matmul(out1, scores[:, s, h, P:S], v[:, 2 * s, vh], start=True, stop=False)
                        mm = pe.matmul(out1, scores[:, s, h, S:CAUSAL], v[:, 2 * s + 1, vh], start=False, stop=True)
                    mm.then_inc(o_ready, 1)
                pe.wait_ge(o_gated, 2 * i + 2)
                for a in range(2):
                    transpose_tiles(pe, bank[2 + a], lambda j: o[:, j, a * P:(a + 1) * P],
                                    ident[:, :]).then_inc(o_turned, 1)
                pe.wait_ge(oT_ready, 2 * i + 2)
                for j in range(PAIR):
                    for a in range(2):
                        mm = pe.matmul(bank[4][:, j * P:(j + 1) * P], oT[:, a, j * P:(j + 1) * P], wo[:, a, :],
                                       start=(a == 0), stop=(a == 1))
                mm.then_inc(y_ready, 1)
            rounds(pe, PAIRS, body)

        @block.scalar
        def _(act):
            core.wait_loaded(act, "ret")
            act.preload_act_table(ACT.Silu)
            def body(i):
                act.wait_ge(xn_turned, i + 1)
                act.activation(xnT[:, :], bank[0][:, :], ACT.Copy).then_inc(xnT_ready, 1)
                for j in range(PAIR):
                    act.wait_ge(vg_ready, 4 * i + j + 1)
                    bk = bank[(5 + j) % 8]
                    if j == 0:
                        wait_last_round(act, o_gated, 2 * i)
                    act.activation(v[:, j, :], bk[:, 0:RH * RV], ACT.Copy).then_inc(vg_read, 1)
                    act.activation(gate[:, j, :], bk[:, RH * RV:], ACT.Silu).then_inc(vg_read, 1)
                for s in range(2):
                    act.wait_ge(o_ready, 2 * i + s + 1)
                    act.activation(osq[:, 2 * s:2 * s + 2, :],
                                   bank[1 + 4 * s][:, :].rearrange("p (j n) -> p j n", j=2),
                                   ACT.Square).then_inc(osq_ready, 1)
                for a in range(2):
                    act.wait_ge(o_turned, 2 * i + a + 1)
                    act.activation(oT[:, a, :], bank[2 + a][:, :], ACT.Copy).then_inc(oT_ready, 1)
            rounds(act, PAIRS, body)

        @block.vector
        def _(vec):
            core.wait_loaded(vec, "ret")
            moments(core, vec, st, False)

            def body(i):
                steps = Steps(core, vec, i, vec_per)
                wait_last_round(vec, xn_turned, i)
                for ins in normalize(core, vec, st, i, xn):
                    ins.then_inc(xn_ready, 1)
                for a in range(4):
                    vec.wait_ge(qk_ready, 4 * i + a + 1)
                    if a == 0:
                        wait_last_round(vec, qk_rotated, 2 * i)
                    vec.tensor_tensor(rot[:, a, :].rearrange("p (s t) -> p s t", s=2),
                                      bank[1 + a][:, :].rearrange("p (s t) -> p s t", s=2),
                                      rope[:, a:a + 1, :].to_broadcast([P, 2, S]), ALU.mult).then_inc(rot_ready, 1)
                for s in range(2):
                    for h in range(RH):
                        vec.wait_ge(scores_ready, 8 * i + 4 * s + h + 1)
                        vec.tensor_tensor(scores[:, s, h, :], bank[(1 + 4 * s + h) % 8][:, 0:CAUSAL], causal[:, :],
                                          ALU.mult).then_inc(scores_masked, 1)
                vec.wait_ge(osq_ready, 2 * i + 2)
                steps.done(vec.tensor_reduce(ms[:, :], osq[:, :, :].rearrange("p j (h n) -> p (j h) n", h=RH),
                                             AX.X, ALU.add))
                steps.wait()
                steps.done(vec.tensor_scalar(ms[:, :], ms[:, :], 1.0 / RV, LN_EPS, ALU.mult, ALU.add))
                steps.wait()
                rsqrt(vec, steps, rms[:, :], ms[:, :], mtmp[:, :])
                steps.wait()
                for s in range(2):
                    if s == 0:
                        wait_last_round(vec, o_turned, 2 * i)
                    vec.tensor_tensor(
                        o[:, 2 * s:2 * s + 2, :].rearrange("p j (h n) -> p (j h) n", h=RH),
                        bank[1 + 4 * s][:, :].rearrange("p (g n) -> p g n", n=RV),
                        rms[:, 8 * s:8 * s + 8].unsqueeze(2).to_broadcast([P, 8, RV]), ALU.mult).then_inc(o_scaled, 1)
                vec.wait_ge(y_ready, i + 1)
                vec.tensor_tensor(x[:, bass.ds(4 * i, PAIR), :], x[:, bass.ds(4 * i, PAIR), :],
                                  bank[4][:, :].rearrange("p (j n) -> p j n", j=PAIR), ALU.add).then_inc(y_added, 1)
                assert steps.n == vec_per
            rounds(vec, PAIRS, body)
            core.vector_base += PAIRS * vec_per

        @block.gpsimd
        def _(pool):
            core.wait_loaded(pool, "ret")
            def body(i):
                for a, dst in enumerate((qT, kT)):
                    pool.wait_ge(rot_ready, 4 * i + 2 * a + 2)
                    if a == 0:
                        wait_last_round(pool, scores_ready, 8 * i)
                    pool.tensor_tensor(dst[:, :], rot[:, 2 * a, :], rot[:, 2 * a + 1, :],
                                       ALU.add).then_inc(qk_rotated, 1)
                pool.wait_ge(vg_read, 8 * i + 8)
                pool.tensor_tensor(gate[:, :, :], gate[:, :, :], gnorm[:, :].unsqueeze(1).to_broadcast([P, PAIR, RH * RV]),
                                   ALU.mult).then_inc(o_gated, 1)
                pool.wait_ge(o_gated, 2 * i + 1)
                pool.wait_ge(o_scaled, 2 * i + 2)
                pool.tensor_tensor(o[:, :, :], o[:, :, :], gate[:, :, :], ALU.mult).then_inc(o_gated, 1)
            rounds(pool, PAIRS, body)


def depool_layer(core):
    nc, x, ident, bank = core.nc, core.x, core.ident, core.bank
    with ExitStack() as ctx:
        def sb(name, shape, dt=F32):
            return core.sb(ctx, "dep_" + name, shape, dt)

        def sem(name):
            return core.sem("dep_" + name)

        lens, cx, ginit, index, upto, gres, win, bin_ = (core.dep[k] for k in (
            "lens", "ctx", "ginit", "index", "upto", "gres", "win", "bin"))
        st = core.ln_buffers(ctx, "dep_ln")
        zeros = sb("zeros", [P, S])
        ones = sb("ones", [1, P])
        upto_b = sb("upto_b", [P, S], BF16)
        cum = sb("cum", [P, 2, S])
        wrap = sb("wrap", [P, 2, S])
        end_at = sb("end_at", [P, 2, S])
        same = sb("same", [P, S])
        is_end = sb("is_end", [P, 4])
        is_end_b = sb("is_end_b", [P, 4, P], BF16)
        age = sb("age", [P, 2, CAUSAL])
        weight = sb("weight", [P, 2, CAUSAL])
        csq = sb("csq", [P, PAIR, DC])
        cms = sb("cms", [P, PAIR])
        crms = sb("crms", [P, PAIR])
        ctmp = sb("ctmp", [P, PAIR])
        u = sb("u", [P, PAIR, D])
        xn = sb("xn", [P, PAIR, D])
        xnT = sb("xnT", [P, WIDE])

        set_up = sem("set_up")
        xn_ready = sem("xn_ready")
        xn_turned = sem("xn_turned")
        xnT_ready = sem("xnT_ready")
        ends_ready = sem("ends_ready")
        counts_ready = sem("counts_ready")
        ages_ready = sem("ages_ready")
        decays_ready = sem("decays_ready")
        weights_ready = sem("weights_ready")
        csq_ready = sem("csq_ready")
        crms_ready = sem("crms_ready")
        u_gained = sem("u_gained")
        u_ready = sem("u_ready")
        y_ready = sem("y_ready")
        y_added = sem("y_added")
        vec_per = (2 + 1 + 1 + 4) + (1 + 1 + 11)
        block = ctx.enter_context(nc.Block())

        @block.tensor
        def _(pe):
            core.wait_loaded(pe, "dep")
            pe.wait_ge(set_up, 3)
            def body(i):
                pe.wait_ge(ends_ready, i + 1)
                for s in range(2):
                    pe.matmul(bank[2][:, s * S:(s + 1) * S], is_end_b[:, 2 * s, :], upto_b[:, :], start=True, stop=False)
                    mm = pe.matmul(bank[2][:, s * S + P:(s + 1) * S], is_end_b[:, 2 * s + 1, :], upto_b[:, 0:P],
                                   start=False, stop=True)
                mm.then_inc(counts_ready, 1)
                pe.wait_ge(xn_ready, 4 * i + 4)
                transpose_tiles(pe, bank[0], lambda j: xn[:, j, :], ident[:, :]).then_inc(xn_turned, 1)
                wait_last_round(pe, y_added, i)
                pe.wait_ge(xnT_ready, i + 1)
                pe.wait_ge(weights_ready, i + 1)
                pe.wait_ge(u_ready, i + 1)
                for s in range(2):
                    for t in range(2):
                        j = 2 * s + t
                        y = bank[1][:, j * P:(j + 1) * P]
                        pe.matmul(y, ones[:, :], bin_[:, :], start=True, stop=False)
                        pe.matmul(y, xnT[:, j * P:(j + 1) * P], win[:, :], start=False, stop=False)
                        mm = pe.matmul(y, weight[:, s, t * P:(t + 1) * P], u[:, 2 * s, :], start=False, stop=(t == 0))
                        if t == 1:
                            mm = pe.matmul(y, weight[:, s, S:CAUSAL], u[:, 2 * s + 1, :], start=False, stop=True)
                mm.then_inc(y_ready, 1)
            rounds(pe, PAIRS, body)

        @block.scalar
        def _(act):
            core.wait_loaded(act, "dep")
            act.preload_act_table(ACT.Exp)
            def body(i):
                wait_last_round(act, crms_ready, i)
                act.activation(csq[:, :, :], cx[:, bass.ds(4 * i, PAIR), :], ACT.Square).then_inc(csq_ready, 1)
                act.wait_ge(ages_ready, 4 * i + 4)
                wait_last_round(act, y_ready, i)
                act.activation(weight[:, :, :], age[:, :, :], ACT.Exp, scale=-DEPOOL_DT).then_inc(decays_ready, 1)
                act.wait_ge(xn_turned, i + 1)
                act.activation(xnT[:, :], bank[0][:, :], ACT.Copy, scale=gres[:, 0:1]).then_inc(xnT_ready, 1)
            rounds(act, PAIRS, body)

        @block.vector
        def _(vec):
            core.wait_loaded(vec, "dep")
            vec.memset(zeros[:, :], 0.0).then_inc(set_up, 1)
            vec.memset(ones[:, :], 1.0).then_inc(set_up, 1)
            vec.tensor_copy(upto_b[:, :], upto[:, :]).then_inc(set_up, 1)
            vec.wait_ge(set_up, 3)
            moments(core, vec, st, True)

            def body(i):
                steps = Steps(core, vec, i, vec_per)
                for s in range(2):
                    steps.done(vec.tensor_tensor_scan(out=cum[:, s, :], data0=lens[:, bass.ds(2 * i + s, 1), :].rearrange("p o n -> p (o n)"), data1=zeros[:, :],
                                                      initial=0.0, op0=ALU.add, op1=ALU.add))
                steps.wait()
                steps.done(vec.tensor_scalar(wrap[:, :, :], cum[:, :, :], 1.0, float(S), ALU.is_lt, ALU.mult))
                steps.wait()
                steps.done(vec.scalar_tensor_tensor(out=end_at[:, :, :], in0=cum[:, :, :], scalar=-1.0,
                                                    in1=wrap[:, :, :], op0=ALU.add, op1=ALU.add))
                for s in range(2):
                    for t in range(2):
                        steps.wait()
                        steps.done(vec.tensor_scalar(same[:, :], end_at[:, s, :], index[:, t:t + 1], None, ALU.is_equal,
                                                     ALU.max, accum_out=is_end[:, 2 * s + t:2 * s + t + 1]))
                steps.wait()
                wait_last_round(vec, counts_ready, i)
                vec.tensor_copy(is_end_b[:, :, :], is_end[:, :].unsqueeze(2).to_broadcast([P, 4, P])).then_inc(ends_ready, 1)
                vec.wait_ge(csq_ready, i + 1)
                steps.done(vec.tensor_reduce(cms[:, :], csq[:, :, :], AX.X, ALU.add))
                steps.wait()
                steps.done(vec.tensor_scalar(cms[:, :], cms[:, :], 1.0 / DC, LN_EPS, ALU.mult, ALU.add))
                steps.wait()
                wait_last_round(vec, u_ready, i)
                rsqrt(vec, steps, crms[:, :], cms[:, :], ctmp[:, :])
                steps.wait()
                vec.tensor_scalar(crms[:, :], crms[:, :], DEPOOL_B, None, ALU.mult).then_inc(crms_ready, 1)
                vec.wait_ge(counts_ready, i + 1)
                wait_last_round(vec, weights_ready, i)
                for s in range(2):
                    vec.tensor_scalar(age[:, s, 0:S], bank[2][:, s * S:(s + 1) * S], index[:, 2:3], index[:, 4:5],
                                      ALU.subtract, ALU.max).then_inc(ages_ready, 1)
                    vec.tensor_scalar(age[:, s, S:CAUSAL], bank[2][:, s * S + P:(s + 1) * S], index[:, 3:4],
                                      index[:, 5:6], ALU.subtract, ALU.max).then_inc(ages_ready, 1)
                wait_last_round(vec, xn_turned, i)
                for ins in normalize(core, vec, st, i, xn):
                    ins.then_inc(xn_ready, 1)
                vec.wait_ge(decays_ready, i + 1)
                vec.scalar_tensor_tensor(out=weight[:, :, :], in0=age[:, :, :], scalar=0.0, in1=weight[:, :, :],
                                         op0=ALU.is_ge, op1=ALU.mult).then_inc(weights_ready, 1)
                vec.wait_ge(y_ready, i + 1)
                vec.tensor_tensor(x[:, bass.ds(4 * i, PAIR), :], x[:, bass.ds(4 * i, PAIR), :],
                                  bank[1][:, :].rearrange("p (j n) -> p j n", j=PAIR), ALU.add).then_inc(y_added, 1)
                assert steps.n == vec_per
            rounds(vec, PAIRS, body)
            core.vector_base += PAIRS * vec_per

        @block.gpsimd
        def _(pool):
            core.wait_loaded(pool, "dep")
            def body(i):
                wait_last_round(pool, y_ready, i)
                pool.tensor_tensor(u[:, :, :], cx[:, bass.ds(4 * i, PAIR), 0:D],
                                   ginit[:, :].unsqueeze(1).to_broadcast([P, PAIR, D]), ALU.mult).then_inc(u_gained, 1)
                pool.wait_ge(u_gained, i + 1)
                pool.wait_ge(crms_ready, i + 1)
                pool.tensor_tensor(u[:, :, :], u[:, :, :], crms[:, :].unsqueeze(2).to_broadcast([P, PAIR, D]),
                                   ALU.mult).then_inc(u_ready, 1)
            rounds(pool, PAIRS, body)


def conv_layer(core):
    nc, x, ident, bank = core.nc, core.x, core.ident, core.bank
    w = core.conv
    HALF = D // 2
    with ExitStack() as ctx:
        def sb(name, shape, dt=F32):
            return core.sb(ctx, "conv_" + name, shape, dt)

        def sem(name):
            return core.sem("conv_" + name)

        dft, idft, win, wout = (w[k] for k in ("dft", "idft", "win", "wout"))
        st = core.ln_buffers(ctx, "conv_ln")
        ones = sb("ones", [1, P])
        rate = sb("rate", [P, HALF])
        late = sb("late", [P, HALF])
        gain = sb("gain", [P, HALF])
        gains = sb("gains", [P, HALF, 4])
        angle = sb("angle", [P, HALF, P])
        power = sb("power", [P, HALF, P])
        kernel_t = sb("kernel_t", [P, 2, D])
        kre = sb("kre", [P, 2, D])
        kim = sb("kim", [P, 2, D])
        kre2 = sb("kre2", [P, 2, D])
        packed = sb("packed_row", [P, D])
        xn = sb("xn", [P, PAIR, D])
        xnT = sb("xnT", [P, WIDE])
        u = sb("u", [P, PAIR, D])
        prod = sb("prod", [P, 4, 4, P])
        spec = sb("spec", [P, 4, 2, D])
        yT = sb("yT", [P, WIDE])

        signed = sem("signed")
        rates_ready = sem("rates_ready")
        gains_ready = sem("gains_ready")
        angles_ready = sem("angles_ready")
        powers_ready = sem("powers_ready")
        kernel_ready = sem("kernel_ready")
        kernel_copied = sem("kernel_copied")
        kspec_ready = sem("kspec_ready")
        kspec_copied = sem("kspec_copied")
        xn_ready = sem("xn_ready")
        xn_turned = sem("xn_turned")
        xnT_ready = sem("xnT_ready")
        u_ready = sem("u_ready")
        u_copied = sem("u_copied")
        uspec_ready = sem("uspec_ready")
        products_ready = sem("products_ready")
        spec_ready = sem("spec_ready")
        yT_ready = sem("yT_ready")
        yT_copied = sem("yT_copied")
        y_ready = sem("y_ready")
        y_added = sem("y_added")
        CUT = 8
        PART = HALF // CUT
        block = ctx.enter_context(nc.Block())

        @block.tensor
        def _(pe):
            core.wait_loaded(pe, "conv")
            pe.wait_ge(signed, 1)
            pe.wait_ge(gains_ready, 2)
            for c in range(CUT):
                pe.wait_ge(powers_ready, c + 1)
                for j in range(c * PART, (c + 1) * PART):
                    mm = pe.matmul(bank[6][:, 4 * j:4 * j + 4], power[:, j, :], gains[:, j, :], start=True, stop=True)
            mm.then_inc(kernel_ready, 1)
            pe.wait_ge(kernel_copied, 3)
            for m in range(4):
                for j in range(2):
                    mm = pe.matmul(bank[7][:, m * D:(m + 1) * D], dft[:, j, m * P:(m + 1) * P], kernel_t[:, j, :],
                                   start=(j == 0), stop=(j == 1))
            mm.then_inc(kspec_ready, 1)
            def body(i):
                pe.wait_ge(xn_ready, 4 * i + 4)
                transpose_tiles(pe, bank[0], lambda j: xn[:, j, :], ident[:, :]).then_inc(xn_turned, 1)
                pe.wait_ge(xnT_ready, i + 1)
                for j in range(PAIR):
                    pe.matmul(bank[1][:, j * P:(j + 1) * P], ones[:, :], w["bin"][:, :], start=True, stop=False)
                    mm = pe.matmul(bank[1][:, j * P:(j + 1) * P], xnT[:, j * P:(j + 1) * P], win[:, :],
                                   start=False, stop=True)
                mm.then_inc(u_ready, 1)
                pe.wait_ge(u_copied, i + 1)
                for m in range(4):
                    for j in range(2):
                        mm = pe.matmul(bank[2 + m // 2][:, (m % 2) * S:(m % 2 + 1) * S].rearrange("p (s d) -> p s d", s=2),
                                       dft[:, j, m * P:(m + 1) * P],
                                       u[:, j:PAIR:2, :], start=(j == 0), stop=(j == 1))
                    if m % 2:
                        mm.then_inc(uspec_ready, 1)
                for s in range(2):
                    pe.wait_ge(spec_ready, 2 * i + 2)
                    for m in range(4):
                        mm = pe.matmul(bank[4][:, s * S:(s + 1) * S], spec[:, m, s, :], idft[:, m, :],
                                       start=(m == 0), stop=(m == 3))
                mm.then_inc(yT_ready, 1)
                pe.wait_ge(yT_copied, i + 1)
                for j in range(PAIR):
                    pe.matmul(bank[5][:, j * P:(j + 1) * P], ones[:, :], w["bout"][:, :], start=True, stop=False)
                    mm = pe.matmul(bank[5][:, j * P:(j + 1) * P], yT[:, j * P:(j + 1) * P], wout[:, :],
                                   start=False, stop=True)
                mm.then_inc(y_ready, 1)
            rounds(pe, PAIRS, body)

        @block.scalar
        def _(act):
            core.wait_loaded(act, "conv")
            act.activation(rate[:, :], w["alog"][:, :], ACT.Exp, scale=-1.0).then_inc(rates_ready, 1)
            act.wait_ge(signed, 2)
            act.activation(late[:, :], rate[:, :], ACT.Exp, scale=float(P)).then_inc(rates_ready, 1)
            for c in range(CUT):
                act.wait_ge(angles_ready, c + 1)
                part = slice(c * PART, (c + 1) * PART)
                act.activation(power[:, part, :], angle[:, part, :], ACT.Exp).then_inc(powers_ready, 1)
            def body(i):
                act.wait_ge(xn_turned, i + 1)
                act.activation(xnT[:, :], bank[0][:, :], ACT.Copy).then_inc(xnT_ready, 1)
                act.wait_ge(u_ready, i + 1)
                act.activation(u[:, :, :], bank[1][:, :].rearrange("p (j n) -> p j n", j=PAIR),
                               ACT.Copy).then_inc(u_copied, 1)
                act.wait_ge(yT_ready, i + 1)
                act.activation(yT[:, :], bank[4][:, :], ACT.Copy).then_inc(yT_copied, 1)
            rounds(act, PAIRS, body)

        @block.vector
        def _(vec):
            core.wait_loaded(vec, "conv")
            vec.memset(ones[:, :], 1.0).then_inc(signed, 1)
            vec.wait_ge(rates_ready, 1)
            vec.scalar_tensor_tensor(out=rate[:, :], in0=rate[:, :], scalar=-1.0, in1=w["dt"][:, :],
                                     op0=ALU.mult, op1=ALU.mult).then_inc(signed, 1)
            vec.wait_ge(signed, 2)
            setup = Steps(core, vec)
            for c in range(CUT):
                part = slice(c * PART, (c + 1) * PART)
                vec.tensor_tensor(angle[:, part, :], w["time"][:, :].unsqueeze(1).to_broadcast([P, PART, P]),
                                  rate[:, part].unsqueeze(2).to_broadcast([P, PART, P]), ALU.mult).then_inc(angles_ready, 1)
                if c == 0:
                    setup.done(vec.tensor_tensor(gain[:, :], w["b"][:, :], w["dt"][:, :], ALU.mult))
                    setup.wait()
                    setup.done(vec.tensor_tensor(gain[:, :], gain[:, :], w["c"][:, :], ALU.mult))
                    setup.wait()
                    vec.wait_ge(rates_ready, 2)
                    setup.done(vec.tensor_tensor(late[:, :], late[:, :], gain[:, :], ALU.mult))
                    setup.wait()
                    for h, g in enumerate((gain, late)):
                        vec.tensor_tensor(gains[:, :, 2 * h:2 * h + 2], g[:, :].unsqueeze(2).to_broadcast([P, HALF, 2]),
                                          w["half"][:, :].unsqueeze(1).to_broadcast([P, HALF, 2]),
                                          ALU.mult).then_inc(gains_ready, 1)
            setup.close()
            vec.wait_ge(kernel_ready, 1)
            for h in range(2):
                vec.tensor_copy(kernel_t[:, h, :].rearrange("p (j c) -> p j c", c=2),
                                bank[6][:, 0:4 * HALF].rearrange("p (j h c) -> p h j c", h=2, c=2)[:, h]
                                ).then_inc(kernel_copied, 1)
            vec.wait_ge(kernel_copied, 2)
            vec.tensor_tensor(kernel_t[0:1, 0, :], kernel_t[0:1, 0, :], w["skip"][:, :], ALU.add).then_inc(kernel_copied, 1)
            vec.wait_ge(kspec_ready, 1)
            kbank = bank[7][:, :].rearrange("p (m d) -> p m d", m=4)
            vec.tensor_copy(kre[:, :, :], kbank[:, 0:2]).then_inc(kspec_copied, 1)
            vec.tensor_scalar(packed[:, :], kbank[:, 2], w["packed"][:, 0:1], None, ALU.mult).then_inc(kspec_copied, 1)
            vec.tensor_scalar(kim[:, 0, :], kbank[:, 2], w["packed"][:, 1:2], None, ALU.mult).then_inc(kspec_copied, 1)
            vec.tensor_copy(kim[:, 1, :], kbank[:, 3]).then_inc(kspec_copied, 1)
            vec.tensor_copy(kre2[:, 1, :], kbank[:, 1]).then_inc(kspec_copied, 1)
            vec.wait_ge(kspec_copied, 5)
            vec.scalar_tensor_tensor(out=kre2[:, 0, :], in0=kre[:, 0, :], scalar=w["packed"][:, 1:2], in1=packed[:, :],
                                     op0=ALU.mult, op1=ALU.add).then_inc(kspec_copied, 1)
            vec.wait_ge(kspec_copied, 6)
            moments(core, vec, st, False)

            def body(i):
                wait_last_round(vec, xn_turned, i)
                for ins in normalize(core, vec, st, i, xn):
                    ins.then_inc(xn_ready, 1)
                vec.wait_ge(uspec_ready, 2 * i + 2)
                wait_last_round(vec, spec_ready, 2 * i)
                for q, (half, k) in enumerate(((0, kre), (1, kim), (0, kim), (1, kre2))):
                    for m in range(2):
                        vec.tensor_tensor(prod[:, q, 2 * m:2 * m + 2, :],
                                          bank[2 + half][:, m * S:(m + 1) * S].rearrange("p (s d) -> p s d", s=2),
                                          k[:, m:m + 1, :].to_broadcast([P, 2, D]), ALU.mult).then_inc(products_ready, 1)
                vec.wait_ge(y_ready, i + 1)
                vec.tensor_tensor(x[:, bass.ds(4 * i, PAIR), :], x[:, bass.ds(4 * i, PAIR), :],
                                  bank[5][:, :].rearrange("p (j n) -> p j n", j=PAIR), ALU.add).then_inc(y_added, 1)
            rounds(vec, PAIRS, body)

        @block.gpsimd
        def _(pool):
            def body(i):
                for half, op in ((0, ALU.subtract), (1, ALU.add)):
                    pool.wait_ge(products_ready, 8 * i + 4 * half + 4)
                    if half == 0:
                        wait_last_round(pool, yT_ready, i)
                    pool.tensor_tensor(spec[:, 2 * half:2 * half + 2, :, :].rearrange("p m s d -> p (m s) d"),
                                       prod[:, 2 * half, :, :], prod[:, 2 * half + 1, :, :], op).then_inc(spec_ready, 1)
            rounds(pool, PAIRS, body)


def cross_attention_layer(core):
    nc, x, ident, bank, psum = core.nc, core.x, core.ident, core.bank, core.psum
    w = core.xat
    with ExitStack() as ctx:
        def sb(name, shape, dt=F32):
            return core.sb(ctx, "xat_" + name, shape, dt)

        def sem(name):
            return core.sem("xat_" + name)

        wk, wv, wq, bv, wout, qmask = (w[k] for k in ("wk", "wv", "wq", "bv", "wout", "qmask"))
        st = core.ln_buffers(ctx, "xat_ln")
        kmask = sb("kmask", [P, B * S])
        xn = sb("xn", [P, PAIR, D])
        xnT = sb("xnT", [P, WIDE])
        ctxT = sb("ctxT", [P, 2, WIDE])
        kT = sb("kT", [P, 2, WIDE])
        qT = sb("qT", [P, 2, WIDE])
        qT_less = sb("qT_less", [P, 2, WIDE])
        v = sb("v", [P, PAIR, XH, HEAD_ROWS])
        top = sb("top", [P, PAIR, 2, P])
        prob = sb("prob", [P, 2, XH, 2, S])
        heads = sb("heads", [P, 2, 2 * S])
        updT = sb("updT", [P, 2, 2 * S])

        set_up = sem("set_up")
        xn_ready = sem("xn_ready")
        xn_turned = sem("xn_turned")
        xnT_ready = sem("xnT_ready")
        ctx_loaded = sem("ctx_loaded")
        x_biased = sem("x_biased")
        k_ready = sem("k_ready")
        k_copied = sem("k_copied")
        q_ready = sem("q_ready")
        q_copied = sem("q_copied")
        v_ready = sem("v_ready")
        v_copied = sem("v_copied")
        scores_ready = sem("scores_ready")
        tops_ready = sem("tops_ready")
        tops_turned = sem("tops_turned")
        q_lessened = sem("q_lessened")
        shifted_ready = sem("shifted_ready")
        probs_ready = sem("probs_ready")
        heads_ready = sem("heads_ready")
        heads_copied = sem("heads_copied")
        sums_ready = sem("sums_ready")
        sums_inverted = sem("sums_inverted")
        updT_ready = sem("updT_ready")
        y_ready = sem("y_ready")
        y_added = sem("y_added")
        RING = (6, 7, 0, 1)
        block = ctx.enter_context(nc.Block())

        @block.sync
        def _(sp):
            def body(i):
                wait_last_round(sp, v_ready, i)
                sp.dma_start(ctxT[:, :, :], core.arg["ctxT"].rearrange("(a p) t -> p a t", p=P)[:, :, bass.ds(i * WIDE, WIDE)]
                             ).then_inc(ctx_loaded, 16)
            rounds(sp, PAIRS, body)

        @block.tensor
        def _(pe):
            core.wait_loaded(pe, "xat")

            def turn_x(i):
                pe.wait_ge(xn_ready, 4 * i + 4)
                transpose_tiles(pe, bank[2], lambda j: xn[:, j, :], ident[:, :]).then_inc(xn_turned, 1)

            def make_k(i):
                pe.wait_ge(ctx_loaded, 16 * i + 16)
                for g in range(2):
                    for a in range(2):
                        mm = pe.matmul(bank[6 + g], wk[:, a, g * P:(g + 1) * P], ctxT[:, a, :], start=(a == 0), stop=(a == 1))
                    mm.then_inc(k_ready, 1)

            def make_v(i):
                pe.wait_ge(xnT_ready, i + 1)
                for j in range(PAIR):
                    for a in range(2):
                        mm = pe.matmul(bank[2][:, j * P:(j + 1) * P], ctxT[:, a, j * P:(j + 1) * P], wv[:, a, :],
                                       start=(a == 0), stop=(a == 1))
                mm.then_inc(v_ready, 1)

            def make_q(i):
                for g in range(2):
                    pe.matmul(bank[4 + g], wq[:, g * P:(g + 1) * P], xnT[:, :], start=True, stop=True).then_inc(q_ready, 1)

            def turn_tops(i, s):
                pe.wait_ge(tops_ready, 8 * i + 4 * s + 4)
                for g in range(2):
                    for t in range(2):
                        mm = pe.matmul(bank[2 + 3 * s][:, g * S + t * P:g * S + (t + 1) * P], top[:, 2 * s + t, g, :],
                                       ident[:, :], start=True, stop=True)
                mm.then_inc(tops_turned, 1)

            def spread_sums(i, s):
                pe.wait_ge(heads_copied, 2 * i + s + 1)
                pe.matmul(bank[s], w["spread"][:, :], heads[:, s, :], start=True, stop=True).then_inc(sums_ready, 1)

            turn_x(0)
            make_k(0)
            make_v(0)
            make_q(0)

            def body(i, more):
                pe.wait_ge(k_copied, 2 * i + 2)
                pe.wait_ge(q_copied, 2 * i + 2)
                for j in range(PAIR):
                    for c in range(2):
                        n = 2 * j + c
                        if n >= 2:
                            pe.wait_ge(tops_ready, 8 * i + n - 1)
                        for h in range(2 * c, 2 * c + 2):
                            rows = slice(HEAD_ROWS * h, HEAD_ROWS * (h + 1))
                            at = (j // 2) * S
                            for g in range(2):
                                mm = pe.matmul(psum[:, (6, 0)[c] + h % 2, g * S:(g + 1) * S],
                                               qT[rows, g, j * P:(j + 1) * P], kT[rows, g, at:at + S],
                                               start=True, stop=True)
                        mm.then_inc(scores_ready, 1)
                pe.wait_ge(v_copied, i + 1)
                turn_tops(i, 0)
                wait_last_round(pe, y_added, i)
                for j in range(PAIR):
                    pe.matmul(bank[3][:, j * P:(j + 1) * P], xnT[:, j * P:(j + 1) * P], wout[:, 0, :], start=(j == 0),
                              stop=False)
                turn_tops(i, 1)
                for s in range(2):
                    pe.wait_ge(q_lessened, 2 * i + s + 1)
                    for h in range(XH):
                        n = XH * s + h
                        if n >= 4:
                            pe.wait_ge(probs_ready, 16 * i + n - 3)
                        g, rows, at = h // 4, slice(HEAD_ROWS * (h % 4), HEAD_ROWS * (h % 4 + 1)), s * S
                        for t in range(2):
                            mm = pe.matmul(bank[RING[n % 4]][:, t * S:(t + 1) * S],
                                           kT[rows, g, at + t * P:at + (t + 1) * P], qT_less[rows, g, at:at + S],
                                           start=True, stop=True)
                        mm.then_inc(shifted_ready, 1)
                for s in range(2):
                    pe.wait_ge(probs_ready, 16 * i + 8 * s + 8)
                    for g in range(2):
                        if (s, g) == (1, 1):
                            spread_sums(i, 0)
                        for h in range(4):
                            rows = slice(HEAD_ROWS * h, HEAD_ROWS * (h + 1))
                            for a in range(2):
                                mm = pe.matmul(bank[4 + s][rows, g * S:(g + 1) * S], v[:, 2 * s + a, 4 * g + h, :],
                                               prob[:, s, 4 * g + h, a, :], start=(a == 0), stop=(a == 1))
                    mm.then_inc(heads_ready, 1)
                if more:
                    turn_x(i + 1)
                    make_k(i + 1)
                spread_sums(i, 1)
                if more:
                    make_v(i + 1)
                    make_q(i + 1)
                pe.wait_ge(updT_ready, 2 * i + 2)
                for j in range(PAIR):
                    for g in range(2):
                        at = g * S + (j % 2) * P
                        mm = pe.matmul(bank[3][:, j * P:(j + 1) * P], updT[:, j // 2, at:at + P], wout[:, 1 + g, :],
                                       start=False, stop=(j == PAIR - 1 and g == 1))
                mm.then_inc(y_ready, 1)
            turns(pe, PAIRS, body)

        @block.scalar
        def _(act):
            act.preload_act_table(ACT.Exp)

            def front(i):
                act.wait_ge(xn_turned, i + 1)
                act.activation(xnT[:, :], bank[2], ACT.Copy).then_inc(xnT_ready, 1)
            front(0)

            def body(i, more):
                for s in range(2):
                    for h in range(XH):
                        n = XH * s + h
                        act.wait_ge(shifted_ready, 16 * i + n + 1)
                        act.activation(prob[:, s, h, :, :], bank[RING[n % 4]].rearrange("p (a t) -> p a t", a=2), ACT.Exp,
                                       scale=XD ** -0.5).then_inc(probs_ready, 1)
                for s in range(2):
                    act.wait_ge(heads_ready, 2 * i + s + 1)
                    act.activation(heads[:, s, :], bank[4 + s], ACT.Copy).then_inc(heads_copied, 1)
                if more:
                    front(i + 1)
            turns(act, PAIRS, body)

        @block.vector
        def _(vec):
            core.wait_loaded(vec, "xat")
            moments(core, vec, st, False)

            def front(i):
                for ins in normalize(core, vec, st, i, xn):
                    ins.then_inc(xn_ready, 1)
                vec.wait_ge(xn_ready, 4 * i + 4)
                vec.tensor_tensor(x[:, bass.ds(4 * i, PAIR), :], x[:, bass.ds(4 * i, PAIR), :],
                                  w["bout"][:, :].unsqueeze(1).to_broadcast([P, PAIR, D]), ALU.add).then_inc(x_biased, 1)

            def copy_k(i):
                for g in range(2):
                    vec.wait_ge(k_ready, 2 * i + g + 1)
                    vec.scalar_tensor_tensor(out=kT[:, g, :], in0=bank[6 + g], scalar=w["kbias"][:, g:g + 1],
                                             in1=kmask[:, bass.ds(i * WIDE, WIDE)], op0=ALU.add, op1=ALU.add
                                             ).then_inc(k_copied, 1)

            def copy_qv(i):
                for g in range(2):
                    vec.wait_ge(q_ready, 2 * i + g + 1)
                    vec.scalar_tensor_tensor(out=qT[:, g, :], in0=bank[4 + g], scalar=w["qbias"][:, g:g + 1],
                                             in1=qmask[:, bass.ds(i * WIDE, WIDE)], op0=ALU.add, op1=ALU.mult
                                             ).then_inc(q_copied, 1)
                vec.wait_ge(v_ready, i + 1)
                vec.tensor_tensor(v[:, :, :, 0:XD], bank[2].rearrange("p (j h n) -> p j h n", j=PAIR, h=XH),
                                  bv[:, :].rearrange("p (h n) -> p h n", h=XH).unsqueeze(1).to_broadcast([P, PAIR, XH, XD]),
                                  ALU.add).then_inc(v_copied, 1)

            front(0)
            vec.wait_ge(set_up, 4)
            copy_k(0)
            copy_qv(0)

            def body(i, more):
                for j in range(PAIR):
                    for c in range(2):
                        n = 2 * j + c
                        vec.wait_ge(scores_ready, 8 * i + n + 1)
                        first = (6, 0)[c]
                        vec.tensor_reduce(top[:, j, :, MAX_ROW + 2 * c * HEAD_ROWS:MAX_ROW + (2 * c + 1) * HEAD_ROWS + 1:HEAD_ROWS]
                                          .rearrange("p g h -> p h g"),
                                          psum[:, first:first + 2, :].rearrange("p h (g n) -> p h g n", g=2),
                                          AX.X, ALU.max, negate=True).then_inc(tops_ready, 1)
                for s in range(2):
                    vec.wait_ge(tops_turned, 2 * i + s + 1)
                    at = slice(s * S, (s + 1) * S)
                    vec.tensor_tensor(qT_less[:, :, at], bank[2 + 3 * s].rearrange("p (g t) -> p g t", g=2), qT[:, :, at],
                                      ALU.add).then_inc(q_lessened, 1)
                if more:
                    front(i + 1)
                for s in range(2):
                    vec.wait_ge(sums_ready, 2 * i + s + 1)
                    vec.reciprocal(updT[:, s, :], bank[s]).then_inc(sums_inverted, 1)
                    vec.wait_ge(sums_inverted, 2 * i + s + 1)
                    vec.tensor_tensor(updT[:, s, :], heads[:, s, :], updT[:, s, :], ALU.mult).then_inc(updT_ready, 1)
                    if s == 0 and more:
                        copy_k(i + 1)
                if more:
                    copy_qv(i + 1)
                vec.wait_ge(x_biased, i + 1)
                vec.wait_ge(y_ready, i + 1)
                vec.tensor_tensor(x[:, bass.ds(4 * i, PAIR), :], x[:, bass.ds(4 * i, PAIR), :],
                                  bank[3].rearrange("p (j n) -> p j n", j=PAIR), ALU.add).then_inc(y_added, 1)
            turns(vec, PAIRS, body)

        @block.gpsimd
        def _(pool):
            core.wait_loaded(pool, "xat")
            pool.memset(top[:, :, :, :], 0.0).then_inc(set_up, 1)
            pool.memset(v[:, :, :, :], 1.0).then_inc(set_up, 1)
            pool.tensor_scalar(kmask[:, :], qmask[:, :], 0.0, w["rows"][:, 0:1], ALU.is_equal, ALU.mult).then_inc(set_up, 1)
            pool.wait_ge(set_up, 3)
            pool.tensor_scalar(qmask[:, :], qmask[:, :], w["rows"][:, 1:2], w["rows"][:, 2:3], ALU.mult,
                              ALU.add).then_inc(set_up, 1)
            pool.wait_ge(set_up, 4)


def expert_layer(core, number):
    nc, x, ident, bank = core.nc, core.x, core.ident, core.bank
    w, tables = core.ffn[number], core.moe_tables
    rows_d, outputs_d = core.slots[2 * number:2 * number + 2]
    last = number == 1
    name = f"ffn{number}"
    width, chunk = (F1, P) if last else (F0, F0 // 2)
    chunks = width // chunk
    K = 2
    with ExitStack() as ctx:
        def sb(n, shape, dt=F32):
            return core.sb(ctx, f"{name}_{n}", shape, dt)

        def sem(n):
            return core.sem(f"{name}_{n}")

        st = core.ln_buffers(ctx, f"{name}_ln")
        zero_row = sb("zero_row", [P, D])
        xn = sb("xn", [P, PAIR, D])
        xnT = sb("xnT", [P, WIDE])
        xn_all = sb("xn_all", [P, NT, D])
        clipped = sb("clipped", [P, 2, WIDE])
        hidden = sb("hidden", [P, 2, WIDE])
        logits = sb("logits", [P, NT, E])
        sorted_ = sb("sorted", [P, NT, E])
        order = sb("order", [P, NT, E], U32)
        choice = sb("choice", [P, NT, K])
        onehot = sb("onehot", [P, NT, K, E])
        picked = sb("picked", [P, NT, E])
        picked_b = sb("picked_b", [P, NT, E], BF16)
        upto_b = sb("upto_b", [P, P], BF16)
        ones_b = sb("ones_b", [P, P], BF16)
        soft = sb("soft", [P, NT, E])
        denom = sb("denom", [P, NT])
        weight = sb("weight", [P, NT, K])
        in_tile = sb("in_tile", [P, E, NT])
        before = sb("before", [P, E, NT])
        full = sb("full", [P, E, NT])
        tiles = sb("tiles", [P, E])
        tile_end = sb("tile_end", [P, E])
        first_slot = sb("first_slot", [P, E])
        slot = sb("slot", [P, NT, E])
        slot_sel = sb("slot_sel", [P, NT, K, E])
        slot_f = sb("slot_f", [P, NT, K])
        slot_i = sb("slot_i", [P, K, NT], U32)
        past = sb("past", [1, SLOT_TILES, E])
        owner_f = sb("owner_f", [1, SLOT_TILES])
        owner = sb("owner", [1, SLOT_TILES], I32)
        zero8 = sb("zero8", [P, E])
        row = sb("row", [P, 2, D])
        rowT = sb("rowT", [P, 2, P])
        h = sb("h", [P, 2, width])
        hT = sb("hT", [chunk, 2, chunks * P])
        y = sb("y", [P, 2, D])
        got = sb("got", [P, NT, K, D])

        set_up = sem("set_up")
        zero_filled = sem("zero_filled")
        xn_ready = sem("xn_ready")
        xn_turned = sem("xn_turned")
        xnT_ready = sem("xnT_ready")
        xn_kept = sem("xn_kept")
        logits_ready = sem("logits_ready")
        logits_kept = sem("logits_kept")
        ranks_ready = sem("ranks_ready")
        routed, GAPS, PICKS, SLOTS_KNOWN, OWNERS = sem("routed"), 1, 2, 3, 4
        soft_ready = sem("soft_ready")
        rows_placed = sem("rows_placed")
        row_loaded = [sem(f"row_loaded{s}") for s in range(2)]
        row_turned = sem("row_turned")
        rowT_ready = sem("rowT_ready")
        gate_ready = sem("gate_ready")
        up_ready = sem("up_ready")
        gate_active = sem("gate_active")
        h_ready = sem("h_ready")
        h_turned = sem("h_turned")
        hT_ready = sem("hT_ready")
        out_ready = sem("out_ready")
        out_copied = sem("out_copied")
        out_stored = [sem(f"out_stored{s}") for s in range(2)]
        gathered = [sem(f"gathered{q}") for q in range(PAIRS)]
        combined = sem("combined")
        if last:
            shared_ready = sem("shared_ready")
            shared_clipped = sem("shared_clipped")
            shared_gated = sem("shared_gated")
            shared_hidden = sem("shared_hidden")
            shared_y_ready = sem("shared_y_ready")
            shared_y_added = sem("shared_y_added")
            gate_clipped = sem("gate_clipped")
        block = ctx.enter_context(nc.Block())
        GATE, UP, HT, ROW, OUT = (0, 1), (2, 3), 4, 5, 6

        @block.sync
        def _(sp):
            sp.wait_ge(set_up, 1)
            for t in range(SLOT_TILES):
                sp.dma_start(rows_d[t * P:(t + 1) * P, :], zero_row[:, :]).then_inc(zero_filled, 16)
            sp.wait_ge(rows_placed, 16 * NT * K)

            def load(n, s):
                wait_tiles(sp, row_turned, n - 1)
                sp.dma_start(row[:, s, :], rows_d[bass.ds(n * P, P), :]).then_inc(row_loaded[s], 16)

            def step(n, s):
                if is_tile(n + 2):
                    load(n + 2, s)
                if is_tile(n - 2):
                    sp.wait_ge(out_copied, n - 1)
                    sp.dma_start(outputs_d[bass.ds((n - 2) * P, P), :], y[:, s, :]).then_inc(out_stored[s], 16)

            for n in range(2):
                load(n, n)
            stream_tiles(sp, SLOT_TILES, step)

        @block.tensor
        def _(pe):
            core.wait_loaded(pe, name)
            pe.wait_ge(set_up, 5)
            def body(i):
                pe.wait_ge(xn_ready, 4 * i + 4)
                transpose_tiles(pe, bank[0], lambda j: xn[:, j, :], ident[:, :]).then_inc(xn_turned, 1)
                pe.wait_ge(xnT_ready, i + 1)
                wait_last_round(pe, logits_kept, i)
                for j in range(PAIR):
                    mm = pe.matmul(bank[1][:, j * E:(j + 1) * E], xnT[:, j * P:(j + 1) * P], w["router"][:, :],
                                   start=True, stop=True)
                mm.then_inc(logits_ready, 1)
                if last:
                    for a in range(2):
                        pe.matmul(bank[2 + a], w["shared_up"][:, a * FS:(a + 1) * FS], xnT[:, :],
                                  start=True, stop=True).then_inc(shared_ready, 1)
                    pe.wait_ge(shared_hidden, i + 1)
                    wait_last_round(pe, shared_y_added, i)
                    for j in range(PAIR):
                        mm = pe.matmul(bank[4][:, j * P:(j + 1) * P], hidden[:, 0, j * P:(j + 1) * P],
                                       w["shared_down"][:, :], start=True, stop=True)
                    mm.then_inc(shared_y_ready, 1)
            rounds(pe, PAIRS, body)
            pe.wait_ge(routed, PICKS)
            pe.matmul(bank[2][:, 0:NT * E], upto_b[:, :], picked_b[:, :, :].rearrange("p t e -> p (t e)"),
                      start=True, stop=True)
            pe.matmul(bank[3][:, 0:NT * E], ones_b[:, :], picked_b[:, :, :].rearrange("p t e -> p (t e)"),
                      start=True, stop=True).then_inc(ranks_ready, 1)
            pe.wait_ge(routed, OWNERS)

            def owner_of(n):
                return pe.value_load(owner[0:1, bass.ds(n, 1)], min_val=0, max_val=E - 1)

            def turn_row(n, s):
                pe.wait_ge(row_loaded[s], 8 * (n - s) + 16)
                wait_tiles(pe, rowT_ready, n)
                pe.transpose(bank[ROW][:, 0:P], row[:, s, :], ident[:, :]).then_inc(row_turned, 1)

            def gate_and_up(n, s):
                own = owner_of(n)
                pe.wait_ge(rowT_ready, n + 1)
                wait_tiles(pe, h_ready, n - 1)
                pe.matmul(bank[GATE[s]][:, 0:width], rowT[:, s, :], w["up"][:, bass.ds(own * (2 * width), width)],
                          start=True, stop=True).then_inc(gate_ready, 1)
                pe.matmul(bank[UP[s]][:, 0:width], rowT[:, s, :], w["up"][:, bass.ds(own * (2 * width) + width, width)],
                          start=True, stop=True).then_inc(up_ready, 1)

            def turn_h(n, s):
                pe.wait_ge(h_ready, n + 1)
                wait_tiles(pe, hT_ready, n)
                for c in range(chunks):
                    mm = pe.transpose(bank[HT][0:chunk, c * P:(c + 1) * P], h[:, s, c * chunk:(c + 1) * chunk], ident[:, :])
                mm.then_inc(h_turned, 1)

            def down(n, s):
                own = owner_of(n)
                pe.wait_ge(hT_ready, n + 1)
                wait_tiles(pe, out_copied, n)
                for c in range(chunks):
                    mm = pe.matmul(bank[OUT][:, 0:D], hT[:, s, c * P:(c + 1) * P],
                                   w["down"][:, bass.ds(own * (chunks * D) + c * D, D)],
                                   start=(c == 0), stop=(c == chunks - 1))
                mm.then_inc(out_ready, 1)

            def step(n, s):
                if is_tile(n):
                    gate_and_up(n, s)
                if is_tile(n + 1):
                    turn_row(n + 1, 1 - s)
                if is_tile(n - 2):
                    down(n - 2, s)
                if is_tile(n - 1):
                    turn_h(n - 1, 1 - s)

            turn_row(0, 0)
            stream_tiles(pe, SLOT_TILES, step)

        @block.scalar
        def _(act):
            core.wait_loaded(act, name)

            def turned_copy(out, in_):
                if last:
                    return act.activation(out, in_, ACT.Identity, bias=w["beta"][:, 0:1], scale=w["gamma"][:, 0:1])
                return act.activation(out, in_, ACT.Copy)

            act.preload_act_table(ACT.Silu)
            def body(i):
                act.wait_ge(xn_turned, i + 1)
                turned_copy(xnT[:, :], bank[0]).then_inc(xnT_ready, 1)
                act.activation(xn_all[:, bass.ds(4 * i, PAIR), :], xn[:, :, :], ACT.Copy).then_inc(xn_kept, 1)
                if last:
                    act.wait_ge(shared_clipped, i + 1)
                    act.activation(hidden[:, 1, :], clipped[:, 0, :], ACT.Silu).then_inc(shared_gated, 1)
            rounds(act, PAIRS, body)
            act.wait_ge(routed, GAPS)
            act.activation(soft[:, :, :], soft[:, :, :], ACT.Exp).then_inc(soft_ready, 1)
            act.preload_act_table(ACT.Silu)

            def copy_row(n, s):
                act.wait_ge(row_turned, n + 1)
                wait_tiles(act, up_ready, n - 1)
                turned_copy(rowT[:, s, :], bank[ROW][:, 0:P]).then_inc(rowT_ready, 1)

            def activate(n, s):
                if last:
                    act.wait_ge(gate_clipped, n + 1)
                    act.activation(clipped[:, s, 0:width], clipped[:, s, 0:width], ACT.Silu).then_inc(gate_active, 1)
                else:
                    act.wait_ge(gate_ready, n + 1)
                    wait_tiles(act, h_ready, n - 1)
                    act.activation(clipped[:, s, 0:width], bank[GATE[s]][:, 0:width], ACT.Silu).then_inc(gate_active, 1)

            def copy_h(n, s):
                act.wait_ge(h_turned, n + 1)
                wait_tiles(act, out_ready, n - 1)
                act.activation(hT[:, s, :], bank[HT][0:chunk, 0:chunks * P], ACT.Copy).then_inc(hT_ready, 1)

            def step(n, s):
                if is_tile(n):
                    activate(n, s)
                if is_tile(n + 1):
                    copy_row(n + 1, 1 - s)
                if is_tile(n - 1):
                    copy_h(n - 1, 1 - s)

            copy_row(0, 0)
            stream_tiles(act, SLOT_TILES, step)

        @block.vector
        def _(vec):
            core.wait_loaded(vec, name)
            vec.memset(zero_row[:, :], 0.0).then_inc(set_up, 1)
            vec.tensor_copy(upto_b[:, :], tables["upto_tile"][:, :]).then_inc(set_up, 1)
            vec.memset(ones_b[:, :], 1.0).then_inc(set_up, 1)
            vec.memset(zero8[:, :], 0.0).then_inc(set_up, 1)
            vec.memset(clipped[:, :, :], 0.0).then_inc(set_up, 1)
            vec.wait_ge(set_up, 5)
            moments(core, vec, st, last)

            def body(i):
                wait_last_round(vec, xn_turned, i)
                wait_last_round(vec, xn_kept, i)
                for ins in normalize(core, vec, st, i, xn):
                    ins.then_inc(xn_ready, 1)
                vec.wait_ge(logits_ready, i + 1)
                vec.tensor_copy(logits[:, bass.ds(4 * i, PAIR), :],
                                bank[1][:, 0:PAIR * E].rearrange("p (j e) -> p j e", e=E)).then_inc(logits_kept, 1)
                if last:
                    vec.wait_ge(shared_ready, 2 * i + 2)
                    vec.tensor_scalar(clipped[:, 0, :], bank[2], -GATE_LIMIT, GATE_LIMIT, ALU.max,
                                      ALU.min).then_inc(shared_clipped, 1)
                    vec.wait_ge(shared_gated, i + 1)
                    vec.tensor_tensor(hidden[:, 0, :], hidden[:, 1, :], bank[3], ALU.mult).then_inc(shared_hidden, 1)
                    vec.wait_ge(shared_y_ready, i + 1)
                    vec.tensor_tensor(x[:, bass.ds(4 * i, PAIR), :], x[:, bass.ds(4 * i, PAIR), :],
                                      bank[4].rearrange("p (j n) -> p j n", j=PAIR), ALU.add).then_inc(shared_y_added, 1)
            rounds(vec, PAIRS, body)

            sort = Steps(core, vec)

            def do(ins):
                sort.done(ins)
                sort.wait()

            vec.wait_ge(logits_kept, PAIRS)
            for t in range(NT):
                sort.done(vec.max(sorted_[:, t, :], logits[:, t, :]))
            sort.wait()
            for t in range(NT):
                sort.done(vec.max_index(order[:, t, :], sorted_[:, t, :], logits[:, t, :]))
            vec.tensor_tensor(soft[:, :, :], sorted_[:, :, :], sorted_[:, :, 0:1].to_broadcast([P, NT, E]),
                              ALU.subtract).then_inc(routed, 1)
            sort.wait()
            do(vec.tensor_copy(choice[:, :, :], order[:, :, 0:K]))
            experts = tables["expert"][:, :].unsqueeze(1)
            for k in range(K):
                sort.done(vec.tensor_tensor(onehot[:, :, k, :], experts.to_broadcast([P, NT, E]),
                                            choice[:, :, k:k + 1].to_broadcast([P, NT, E]), ALU.is_equal))
            sort.wait()
            vec.tensor_tensor(picked_b[:, :, :], onehot[:, :, 0, :], onehot[:, :, 1, :], ALU.add).then_inc(routed, 1)
            vec.wait_ge(soft_ready, 1)
            do(vec.tensor_reduce(denom[:, :], soft[:, :, 0:K] if last else soft[:, :, :], AX.X, ALU.add))
            do(vec.reciprocal(denom[:, :], denom[:, :]))
            do(vec.tensor_tensor(weight[:, :, :], soft[:, :, 0:K], denom[:, :].unsqueeze(2).to_broadcast([P, NT, K]), ALU.mult))
            vec.wait_ge(ranks_ready, 1)
            do(vec.tensor_copy(in_tile[:, :, :], bank[3][:, 0:NT * E].rearrange("p (t e) -> p e t", e=E)))
            do(vec.tensor_tensor_scan(out=before[:, :, :].rearrange("p e t -> p (e t)"), data0=tables["not_first"][:, :],
                                      data1=in_tile[:, :, :].rearrange("p e t -> p (e t)"), initial=0.0,
                                      op0=ALU.mult, op1=ALU.add))
            do(vec.tensor_tensor(full[:, :, :], before[:, :, NT - 1:NT].to_broadcast([P, E, NT]),
                                 tables["full_at"][:, :].unsqueeze(1).to_broadcast([P, E, NT]), ALU.is_gt))
            do(vec.tensor_reduce(tiles[:, :], full[:, :, :], AX.X, ALU.add))
            do(vec.tensor_tensor_scan(out=tile_end[:, :], data0=tiles[:, :], data1=zero8[:, :], initial=0.0,
                                      op0=ALU.add, op1=ALU.add))
            do(vec.tensor_tensor(first_slot[:, :], tile_end[:, :], tiles[:, :], ALU.subtract))
            do(vec.tensor_scalar(first_slot[:, :], first_slot[:, :], float(P), -1.0, ALU.mult, ALU.add))
            do(vec.tensor_tensor(before[:, :, :], before[:, :, :], in_tile[:, :, :], ALU.subtract))
            do(vec.tensor_tensor(before[:, :, :], before[:, :, :], first_slot[:, :].unsqueeze(2).to_broadcast([P, E, NT]), ALU.add))
            do(vec.tensor_tensor(slot[:, :, :], bank[2][:, 0:NT * E].rearrange("p (t e) -> p t e", e=E),
                                 before[:, :, :].rearrange("p e t -> p t e"), ALU.add))
            for k in range(K):
                sort.done(vec.tensor_tensor(slot_sel[:, :, k, :], onehot[:, :, k, :], slot[:, :, :], ALU.mult))
            sort.wait()
            do(vec.tensor_reduce(slot_f[:, :, :], slot_sel[:, :, :, :], AX.X, ALU.add))
            vec.tensor_copy(slot_i[:, :, :], slot_f[:, :, :].rearrange("p t k -> p k t")).then_inc(routed, 1)
            do(vec.tensor_tensor(past[:, :, :], tile_end[0:1, :].unsqueeze(1).to_broadcast([1, SLOT_TILES, E]),
                                 tables["tile_index"][0:1, :].unsqueeze(2).to_broadcast([1, SLOT_TILES, E]), ALU.is_le))
            do(vec.tensor_reduce(owner_f[:, :], past[:, :, :], AX.X, ALU.add))
            vec.tensor_scalar(owner[:, :], owner_f[:, :], float(E - 1), None, ALU.min).then_inc(routed, 1)
            sort.close()

            def step(n, s):
                if is_tile(n):
                    if last:
                        vec.wait_ge(gate_ready, n + 1)
                        wait_tiles(vec, h_ready, n - 1)
                        vec.tensor_scalar(clipped[:, s, :], bank[GATE[s]], -GATE_LIMIT, GATE_LIMIT, ALU.max,
                                          ALU.min).then_inc(gate_clipped, 1)
                    vec.wait_ge(gate_active, n + 1)
                    vec.wait_ge(up_ready, n + 1)
                    wait_tiles(vec, h_turned, n - 1)
                    vec.tensor_tensor(h[:, s, :], clipped[:, s, 0:width], bank[UP[s]][:, 0:width],
                                      ALU.mult).then_inc(h_ready, 1)
                if is_tile(n - 2):
                    vec.wait_ge(out_ready, n - 1)
                    if is_tile(n - 4):
                        vec.wait_ge(out_stored[s], 8 * (n - s) - 16)
                    vec.tensor_copy(y[:, s, :], bank[OUT][:, 0:D]).then_inc(out_copied, 1)

            stream_tiles(vec, SLOT_TILES, step)
            for t in range(NT):
                if t % PAIR == 0:
                    vec.wait_ge(gathered[t // PAIR], 16 * K * PAIR)
                for k in range(K):
                    if k:
                        vec.wait_ge(combined, K * t + k)
                    vec.scalar_tensor_tensor(out=x[:, t, :], in0=got[:, t, k, :], scalar=weight[:, t, k:k + 1],
                                             in1=x[:, t, :], op0=ALU.mult, op1=ALU.add).then_inc(combined, 1)

        @block.gpsimd
        def _(pool):
            pool.wait_ge(zero_filled, 16 * SLOT_TILES)
            pool.wait_ge(xn_kept, PAIRS)
            pool.wait_ge(routed, SLOTS_KNOWN)
            for t in range(NT):
                for k in range(K):
                    pool.indirect_dma_start(out=rows_d, out_offset=bass.IndirectOffsetOnAxis(ap=slot_i[:, k, t:t + 1], axis=0),
                                            in_=xn_all[:, t, :], in_offset=None).then_inc(rows_placed, 16)
            for s in range(2):
                pool.wait_ge(out_stored[s], 16 * (SLOT_TILES // 2))
            for t in range(NT):
                for k in range(K):
                    pool.indirect_dma_start(out=got[:, t, k, :], out_offset=None, in_=outputs_d,
                                            in_offset=bass.IndirectOffsetOnAxis(ap=slot_i[:, k, t:t + 1], axis=0)
                                            ).then_inc(gathered[t // PAIR], 16)


def first_expert_layer(core):
    expert_layer(core, 0)


def second_expert_layer(core):
    expert_layer(core, 1)


def load_x(core):
    with ExitStack() as ctx:
        block = ctx.enter_context(core.nc.Block())

        @block.sync
        def _(sp):
            for layer in LOAD_ORDER:
                for buffer, source in core.loads[layer]:
                    sp.dma_start(buffer, source).then_inc(core.loaded[layer], 16)
            for layer in core.loads:
                core.wait_loaded(sp, layer)


def store_x(core, out):
    with ExitStack() as ctx:
        stored = core.sem("stored")
        block = ctx.enter_context(core.nc.Block())

        @block.sync
        def _(sp):
            sp.dma_start(out.rearrange("(t p) d -> p t d", p=P), core.x[:, :, :]).then_inc(stored, 16)
            sp.wait_ge(stored, 16)


LAYERS = [retention_layer, depool_layer, first_expert_layer, conv_layer, cross_attention_layer,
          second_expert_layer]


def decoder_kernel(nc, arg, out, layers=6):
    with ExitStack() as ctx:
        core = Core(nc, ctx, arg)
        for n, layer in enumerate(LAYERS[:layers]):
            layer(core)
            if layer in (depool_layer, load_x):
                core.early.close()
        store_x(core, out)


def half_swapped(w):
    return w.reshape(RH, 2, RQK // 2, D)[:, ::-1].reshape(RH * RQK, D)


def constants():
    f64 = np.float64
    c = {"ident": np.eye(P, dtype=np.float32)}
    inv = 1.0 / 10000.0 ** (np.arange(0, RQK, 2, dtype=f64) / RQK)
    ang = (np.arange(S, dtype=np.float32)[None, :] * inv.astype(np.float32)[:, None]).astype(np.float32).astype(f64)
    decay = np.log1p(-np.exp2(-5.0 - np.arange(RH)))
    t = np.arange(S)
    rope = np.zeros((P, 4, S))
    for h in range(RH):
        r = slice(h * RQK, (h + 1) * RQK)
        cos, sin = np.tile(np.cos(ang), (2, 1)), np.concatenate([-np.sin(ang), np.sin(ang)])
        up, down = np.exp(decay[h] * t) * RQK ** -0.5, np.exp(-decay[h] * t)
        rope[r, 0], rope[r, 1], rope[r, 2], rope[r, 3] = cos * up, sin * up, cos * down, sin * down
    c["rope"] = rope.reshape(P, -1).astype(np.float32)
    tri = np.triu(np.ones((P, P)))
    c["causal"] = np.concatenate([tri, np.ones((P, P)), tri], 1).astype(np.float32)
    p = np.arange(P)
    c["index"] = np.stack([p, p + P, p + 1, p + 1 + P, np.where(p > 0, -1.0, 0.0), -np.ones(P)], 1).astype(np.float32)
    c["upto"] = np.concatenate([tri, np.ones((P, P))], 1).astype(np.float32)
    k, t = np.arange(S), np.arange(S)
    phase = 2 * np.pi * np.outer(t, k) / FFT
    dft = np.concatenate([np.cos(phase), -np.sin(phase)], 1)
    dft[:, S] = np.where(t % 2, -1.0, 1.0)
    idft = np.concatenate([2 * np.cos(phase).T, -2 * np.sin(phase).T], 0) / FFT
    idft[0] = 1.0 / FFT
    idft[S] = np.where(t % 2, -1.0, 1.0) / FFT
    c["dft"], c["idft"] = dft.astype(np.float32), idft.astype(np.float32)
    c["time"] = np.tile(np.arange(P, dtype=np.float32), (P, 1))
    c["half"] = np.stack([p < N_STATE, p >= N_STATE], 1).astype(np.float32)
    c["upto_tile"] = c["upto"][:, :P]
    c["expert"] = np.tile(np.arange(E, dtype=np.float32), (P, 1))
    c["not_first"] = np.tile((np.arange(E * NT) % NT > 0).astype(np.float32), (P, 1))
    c["full_at"] = np.tile(np.arange(NT, dtype=np.float32) * P, (P, 1))
    c["tile_index"] = np.tile(np.arange(SLOT_TILES, dtype=np.float32), (P, 1))
    row = p % HEAD_ROWS
    c["xat_rows"] = np.stack([np.where(row == MASK_ROW, MASKED, 0.0), row != MASK_ROW, row == MASK_ROW], 1).astype(np.float32)
    c["spread"] = (p[:, None] == HEAD_ROWS * (p[None, :] // HEAD_ROWS) + XD).astype(np.float32)
    c["packed"] = np.stack([p == 0, p > 0], 1).astype(np.float32)
    return c


def by_pair(w):
    return w.reshape(D // 2, 2 * N_STATE).T


def head_padded(w):
    out = np.zeros((w.shape[0], XH, HEAD_ROWS), w.dtype)
    out[:, :, :XD] = w.reshape(-1, XH, XD)
    return out.reshape(w.shape[0], XH * HEAD_ROWS)


def head_column(bias, one_row):
    out = np.zeros((XH, HEAD_ROWS), bias.dtype)
    out[:, :XD] = bias.reshape(XH, XD)
    out[:, one_row] = 1.0
    return out.reshape(2, P).T


def laid_out(inp):
    def cat(*a):
        return np.concatenate(a, 1)
    a = constants()
    a["x"] = inp["x"].reshape(B * S, D)
    wq, wk = inp["L0_attn_Wq"], inp["L0_attn_Wk"]
    a["wqk"] = cat(wq.T, half_swapped(wq).T, wk.T, half_swapped(wk).T)
    a["wvg"] = cat(inp["L0_attn_Wv"].T, inp["L0_attn_Wg"].T)
    a["wo"] = inp["L0_attn_Wo"].T
    a["gnorm"] = np.tile(inp["L0_attn_g_norm_w"], (P, RH))
    a["lens"] = inp["mask_BxS2_if0"]
    a["ctx"] = inp["ctx_2048"].reshape(B * S, DC)
    a["ginit"] = np.tile(inp["L0_xattn_g_init"][:D], (P, 1))
    a["gres"] = inp["L0_xattn_g_res"][:, None]
    a["dep_win"] = inp["L0_xattn_W_in"].T
    a["dep_bin"] = inp["L0_xattn_b_in"][None]
    for name, key in (("alog", "A_log"), ("b", "B"), ("c", "C")):
        a["conv_" + name] = by_pair(inp["L1_attn_" + key])
    a["conv_dt"] = by_pair(np.repeat(inp["L1_attn_dt"][:, None], N_STATE, 1))
    a["conv_skip"] = inp["L1_attn_Dp"][None]
    a["conv_win"], a["conv_wout"] = inp["L1_attn_Win"].T, inp["L1_attn_Wout"].T
    a["conv_bin"], a["conv_bout"] = inp["L1_attn_bin_"][None], inp["L1_attn_bout"][None]
    for name, layer, router, up, down, width, chunk in (
            ("ffn0", "L0_ffn_", "router_weight", "w1", "w2", F0, F0 // 2),
            ("ffn1", "L1_ffn_", "router_w", "gate_up_w", "down_w", F1, P)):
        a[name + "_router"] = inp[layer + router]
        a[name + "_up"] = inp[layer + up].transpose(1, 0, 2).reshape(D, E * 2 * width)
        a[name + "_down"] = inp[layer + down].reshape(E, width // chunk, chunk, D).transpose(2, 0, 1, 3).reshape(chunk, -1)
    a["ffn1_gamma"], a["ffn1_beta"] = inp["L1_ffn_ln_gamma"][:, None], inp["L1_ffn_ln_beta"][:, None]
    a["ffn1_shared_up"], a["ffn1_shared_down"] = inp["L1_ffn_shared_gate_up_w"], inp["L1_ffn_shared_down_w"]
    a["ctxT"] = inp["ctx_2048"].reshape(B * S, DC).T
    a["mask"] = inp["mask_BxS2_fk1"].reshape(1, B * S)
    wsrc, bsrc = inp["L1_xattn_W_src"].T, inp["L1_xattn_b_src"]
    a["xat_wk"], a["xat_wv"] = head_padded(wsrc[:, :D]), wsrc[:, D:]
    a["xat_wq"] = head_padded(inp["L1_xattn_W_tgt"].T)
    a["xat_kbias"] = head_column(bsrc[:D], MAX_ROW)
    a["xat_qbias"] = head_column(inp["L1_xattn_b_tgt"], MASK_ROW)
    a["xat_bv"] = np.tile(bsrc[D:], (P, 1))
    wout = inp["L1_xattn_W_out"].T
    a["xat_wout"] = np.concatenate([wout[:D], head_padded(wout[D:].T).T], 0)
    a["xat_bout"] = np.tile(inp["L1_xattn_b_out"], (P, 1))
    return {k: np.ascontiguousarray(v) for k, v in a.items()}


def build(nc, arrays, layers=6):
    arg = {k: nc.dram_tensor(f"in_{k}", v.shape, mybir.dt.from_np(v.dtype), kind="ExternalInput").ap()
           for k, v in arrays.items()}
    out = nc.dram_tensor("out_x", (B * S, D), F32, kind="ExternalOutput").ap()
    decoder_kernel(nc, arg, out, layers)


def kernel(**inputs):
    import concourse.bacc as bacc
    from concourse.bass_utils import run_bass_kernel_spmd

    arrays = laid_out({k: np.asarray(v) for k, v in inputs.items()})
    nc = bacc.Bacc("TRN2", target_bir_lowering=False, num_devices=1)
    build(nc, arrays)
    r = run_bass_kernel_spmd(nc, [{f"in_{k}": v for k, v in arrays.items()}], core_ids=[0])
    return r.results[0]["out_x"].reshape(B, S, D)
```

```python
from contextlib import ExitStack

import numpy as np

import concourse.bass as bass
from concourse import mybir

ALU = mybir.AluOpType
ACT = mybir.ActivationFunctionType
AX = mybir.AxisListType
F32 = mybir.dt.float32
BF16 = mybir.dt.bfloat16
I32 = mybir.dt.int32
U32 = mybir.dt.uint32

P = 128
B, S, D = 8, 256, 128
DC = 256
NT = B * S // P
PAIR = 4
PAIRS = NT // PAIR
WIDE = PAIR * P
LN_EPS = 1e-5
RSQRT_MAGIC = float(0x5F3759DF)

RH, RQK, RV = 4, 32, 64
CAUSAL = 384
DEPOOL_DT = float(-np.log(-np.expm1(np.float32(-0.001))))
DEPOOL_B = float(np.exp(np.float32(-0.001)))
E = 8
K = 2
SLOT_TILES = K * NT + E - 1
LANES = 4
GATE_LIMIT = 10.0
REGION = NT * P + P
SPARE = SLOT_TILES - 2 * NT
SLOTS = E * REGION + SPARE * P
BLANK = E + SPARE
ROW = D + 1
F0, F1, FS = 176, 512, 128
N_STATE = 64
FFT = 2 * S
XH, XD = 8, 16
MASKED = -1e30
HEAD_ROWS = 32
MASK_ROW, MAX_ROW = XD, XD + 1


LOAD_ORDER = ("x", "ret", "dep", "ffn0", "conv", "xat", "ffn1")


class Steps:

    def __init__(self, core, engine, i=0, per_body=0):
        self.core, self.engine, self.i, self.per_body, self.n = core, engine, i, per_body, 0
        self.sem, self.base = core.vector_steps, core.vector_base

    def done(self, ins):
        self.n += 1
        return ins.then_inc(self.sem, 1)

    def wait(self):
        self.engine.wait_ge(self.sem, self.i * self.per_body + (self.base + self.n))

    def close(self):
        self.core.vector_base += self.n


def rounds(engine, n, body):
    body(0)
    with engine.Fori(1, n) as i:
        body(i)


def turns(engine, n, body):
    body(0, True)
    with engine.Fori(1, n - 1) as i:
        body(i, True)
    body(n - 1, False)


def stream_tiles(engine, n_tiles, step):
    for n in range(LANES):
        step(n, n)
    full_rounds = (n_tiles - (LANES - 1)) // LANES
    with engine.Fori(1, full_rounds) as i:
        for s in range(LANES):
            step(LANES * i + s, s)
    for n in range(full_rounds * LANES, n_tiles + 2):
        step(n, n % LANES)


def lane_count(n, s):
    return (n - s) * (16 // LANES) + 16


def is_tile(n, n_tiles=SLOT_TILES):
    return not isinstance(n, int) or 0 <= n < n_tiles


def wait_tiles(engine, sem, count):
    if not isinstance(count, int) or count > 0:
        engine.wait_ge(sem, count)


def is_first(i):
    return isinstance(i, int) and i == 0


def wait_last_round(engine, sem, value):
    if not isinstance(value, int) or value > 0:
        engine.wait_ge(sem, value)


def rsqrt(vec, steps, out, v, tmp):
    steps.done(vec.tensor_scalar(tmp.bitcast(I32), v.bitcast(I32), 1, None, ALU.logical_shift_right))
    steps.wait()
    steps.done(vec.tensor_scalar(out.bitcast(I32), tmp.bitcast(I32), -1.0, RSQRT_MAGIC, ALU.mult, ALU.add))
    for _ in range(3):
        steps.wait()
        steps.done(vec.tensor_tensor(tmp, out, out, ALU.mult))
        steps.wait()
        steps.done(vec.scalar_tensor_tensor(out=tmp, in0=tmp, scalar=-0.5, in1=v, op0=ALU.mult, op1=ALU.mult))
        steps.wait()
        steps.done(vec.scalar_tensor_tensor(out=out, in0=tmp, scalar=1.5, in1=out, op0=ALU.add, op1=ALU.mult))


def tile_stats(core, vec, i):
    for j in range(PAIR):
        vec.bn_stats(core.raw[:, bass.ds(4 * i + j, 1), :].rearrange("p o n -> p (o n)"),
                     core.x[:, bass.ds(4 * i + j, 1), :].rearrange("p o n -> p (o n)")).then_inc(core.stats_ready, 1)


def moments(core, vec, st, twice):
    steps = Steps(core, vec)
    raw = core.raw
    mean, diff, v, r, tmp = (st[k] for k in ("mean", "diff", "v", "r", "tmp"))

    def do(ins):
        steps.done(ins)
        steps.wait()

    core.stats_counted += NT
    vec.wait_ge(core.stats_ready, core.stats_counted)
    steps.done(vec.tensor_tensor(mean[:, :], raw[:, :, 1], raw[:, :, 4], ALU.add))
    steps.done(vec.tensor_tensor(diff[:, :], raw[:, :, 1], raw[:, :, 4], ALU.subtract))
    do(vec.tensor_tensor(v[:, :], raw[:, :, 2], raw[:, :, 5], ALU.add))
    steps.done(vec.tensor_scalar(mean[:, :], mean[:, :], 0.5, None, ALU.mult))
    steps.done(vec.tensor_scalar(v[:, :], v[:, :], 1.0 / D, None, ALU.mult))
    do(vec.scalar_tensor_tensor(out=diff[:, :], in0=diff[:, :], scalar=0.25, in1=diff[:, :],
                                op0=ALU.mult, op1=ALU.mult))
    do(vec.tensor_tensor(diff[:, :], v[:, :], diff[:, :], ALU.add))
    do(vec.tensor_scalar(v[:, :], diff[:, :], LN_EPS, None, ALU.add))
    rsqrt(vec, steps, r[:, :], v[:, :], tmp[:, :])
    steps.wait()
    if twice:
        do(vec.tensor_tensor(diff[:, :], diff[:, :], r[:, :], ALU.mult))
        do(vec.tensor_tensor(diff[:, :], diff[:, :], r[:, :], ALU.mult))
        do(vec.tensor_scalar(v[:, :], diff[:, :], LN_EPS, None, ALU.add))
        rsqrt(vec, steps, st["r2"][:, :], v[:, :], tmp[:, :])
        steps.wait()
        do(vec.tensor_tensor(r[:, :], r[:, :], st["r2"][:, :], ALU.mult))
    steps.close()


def normalize(core, vec, st, i, xn):
    return [vec.tensor_scalar(xn[:, j, :], core.x[:, bass.ds(4 * i + j, 1), :], st["mean"][:, bass.ds(4 * i + j, 1)],
                              st["r"][:, bass.ds(4 * i + j, 1)], ALU.subtract, ALU.mult) for j in range(PAIR)]


class Core:

    def __init__(self, nc, ctx, arg):
        self.nc, self.ctx, self.arg = nc, ctx, arg
        self.used, self.to_clear = [], []
        self.sem_ctx, self.cleared_ctx = ExitStack(), ExitStack()
        self.loads = {}
        self.loaded = {}
        self.psum = ctx.enter_context(nc.psum_tensor("psum", [P, 8, 512], F32))
        self.vector_steps, self.vector_base = self.sem("vector_steps"), 0
        self.bank = [self.psum[:, i, :] for i in range(8)]
        self.raw = self.sb(ctx, "raw_stats", [P, NT, 6])
        self.stats_ready, self.stats_counted = self.sem("stats_ready"), 0

        self.x = self.preload("x", "x", [P, NT, D], arg["x"].rearrange("(t p) d -> p t d", p=P))
        self.ident = self.preload("ret", "ident", [P, P], arg["ident"])
        self.head_rows = self.preload("ret", "head_rows", [P, P // HEAD_ROWS], arg["head_rows"])
        self.ffn = []
        for name, width, chunk in (("ffn0", F0, F0 // 2), ("ffn1", F1, P)):
            chunks = width // chunk
            w = {
                "router": self.preload(name, "router", [P, E], arg[name + "_router"]),
                "up": self.preload(name, "up", [P, E * 2 * width], arg[name + "_up"]),
                "down": self.preload(name, "down", [chunk, E * chunks * D], arg[name + "_down"]),
            }
            if name == "ffn1":
                w["gamma"] = self.preload(name, "gamma", [P, 1], arg["ffn1_gamma"])
                w["beta"] = self.preload(name, "beta", [P, 1], arg["ffn1_beta"])
                w["shared_up"] = self.preload(name, "shared_up", [P, 2 * FS], arg["ffn1_shared_up"])
                w["shared_down"] = self.preload(name, "shared_down", [FS, D], arg["ffn1_shared_down"])
            self.ffn.append(w)
        self.moe_tables = {k: self.preload("ffn0", k, [P, n], arg[k]) for k, n in
                           (("order", E), ("upto_tile", P), ("not_first", E * PAIR), ("full_at", NT),
                            ("tile_index", SLOT_TILES), ("region_start", E))}
        self.output_rows = self.preload("ffn0", "output_rows", [P, K * NT], arg["output_rows"], U32)
        self.slots = [nc.dram_tensor(f"slot_rows{n}", (SLOTS, ROW), F32, kind="Internal").ap() for n in range(2)]
        self.outputs = [nc.dram_tensor(f"outputs{n}", ((K * NT + BLANK) * P, D), F32, kind="Internal").ap()
                        for n in range(2)]
        self.conv = {
            "alog": self.preload("conv", "alog", [P, D // 2], arg["conv_alog"]),
            "b": self.preload("conv", "b", [P, D // 2], arg["conv_b"]),
            "c": self.preload("conv", "c", [P, D // 2], arg["conv_c"]),
            "dt": self.preload("conv", "dt", [P, D // 2], arg["conv_dt"]),
            "skip": self.preload("conv", "skip", [1, D], arg["conv_skip"]),
            "half": self.preload("conv", "half", [P, 2], arg["half"]),
            "time": self.preload("conv", "time", [P, P], arg["time"]),
            "dft": self.preload("conv", "dft", [P, 2, FFT], arg["dft"].rearrange("(a p) n -> p a n", p=P)),
            "idft": self.preload("conv", "idft", [P, 4, S], arg["idft"].rearrange("(a p) n -> p a n", p=P)),
            "packed": self.preload("conv", "packed", [P, 2], arg["packed"]),
            "win": self.preload("conv", "win", [P, D], arg["conv_win"]),
            "bin": self.preload("conv", "bin", [P, D], arg["conv_bin"]),
            "wout": self.preload("conv", "wout", [P, D], arg["conv_wout"]),
            "bout": self.preload("conv", "bout", [P, D], arg["conv_bout"]),
        }
        self.kernel_spectrum = [self.sb(self.ctx, name, [P, 2, D]) for name in ("kre", "kim", "kre2")]
        self.xat = {
            "qmask": self.preload("xat", "qmask", [P, B * S], arg["mask"].to_broadcast([P, B * S])),
            "rows": self.preload("xat", "rows", [P, 3], arg["xat_rows"]),
            "spread": self.preload("xat", "spread", [P, P], arg["spread"]),
            "wk": self.preload("xat", "wk", [P, 2, 2 * P], arg["xat_wk"].rearrange("(a p) n -> p a n", p=P)),
            "wv": self.preload("xat", "wv", [P, 2, D], arg["xat_wv"].rearrange("(a p) n -> p a n", p=P)),
            "wq": self.preload("xat", "wq", [P, 2 * P], arg["xat_wq"]),
            "kbias": self.preload("xat", "kbias", [P, 2], arg["xat_kbias"]),
            "qbias": self.preload("xat", "qbias", [P, 2], arg["xat_qbias"]),
            "bv": self.preload("xat", "bv", [P, D], arg["xat_bv"]),
            "wout": self.preload("xat", "wout", [P, 3, D], arg["xat_wout"].rearrange("(a p) n -> p a n", p=P)),
            "bout": self.preload("xat", "bout", [P, D], arg["xat_bout"]),
        }
        self.early = ExitStack()
        self.ret = {
            "wqk": self.preload_early("ret", "wqk", [P, 4, P], arg["wqk"].rearrange("p (a n) -> p a n", a=4)),
            "rope": self.preload_early("ret", "rope", [P, 4, S], arg["rope"].rearrange("p (a n) -> p a n", a=4)),
            "wvg": self.preload_early("ret", "wvg", [P, 2 * RH * RV], arg["wvg"]),
            "causal": self.preload_early("ret", "causal", [P, CAUSAL], arg["causal"]),
            "wo": self.preload_early("ret", "wo", [P, 2, D], arg["wo"].rearrange("(a p) n -> p a n", p=P)),
            "gnorm": self.preload_early("ret", "gnorm", [P, RH * RV], arg["gnorm"]),
        }
        self.dep = {
            "lens": self.preload_early("dep", "lens", [P, B, S], arg["lens"].rearrange("(o b) s -> o b s", o=1).to_broadcast([P, B, S]), I32),
            "ctx": self.preload_early("dep", "ctx", [P, NT, DC], arg["ctx"].rearrange("(t p) d -> p t d", p=P)),
            "ginit": self.preload_early("dep", "ginit", [P, D], arg["ginit"]),
            "index": self.preload_early("dep", "index", [P, 6], arg["index"]),
            "upto": self.preload_early("dep", "upto", [P, S], arg["upto"]),
            "gres": self.preload_early("dep", "gres", [P, 1], arg["gres"]),
            "win": self.preload_early("dep", "win", [P, D], arg["dep_win"]),
            "bin": self.preload_early("dep", "bin", [1, D], arg["dep_bin"]),
        }

    def sb(self, ctx, name, shape, dt=F32):
        return ctx.enter_context(self.nc.sbuf_tensor(name, shape, dt))

    def preload_early(self, layer, name, shape, source, dt=F32):
        return self.preload(layer, name, shape, source, dt, self.early)

    def preload(self, layer, name, shape, source, dt=F32, ctx=None):
        buffer = self.sb(ctx or self.ctx, f"{layer}_{name}", shape, dt)
        if layer not in self.loads:
            self.loads[layer], self.loaded[layer] = [], self.sem(f"{layer}_loaded")
        self.loads[layer].append((buffer[tuple(slice(None) for _ in shape)], source))
        return buffer

    def wait_loaded(self, engine, layer):
        engine.wait_ge(self.loaded[layer], 16 * len(self.loads[layer]))

    def sem(self, name):
        return self.ctx.enter_context(self.nc.semaphore(name))

    def layer_sem(self, name):
        self.used.append(self.sem_ctx.enter_context(self.nc.semaphore(name)))
        return self.used[-1]

    def start_layer(self):
        self.cleared_ctx.close()
        self.to_clear, self.cleared_ctx = self.used, self.sem_ctx
        self.used, self.sem_ctx = [], ExitStack()

    def clear_last_layer(self, engine):
        for sem in self.to_clear:
            engine.sem_clear(sem)

    def ln_buffers(self, ctx, name):
        st = {k: self.sb(ctx, f"{name}_{k}", [P, NT]) for k in ("mean", "diff", "v", "r", "r2", "tmp")}
        return st


def transpose_tiles(pe, bank, tiles, ident, n=PAIR):
    for j in range(n):
        ins = pe.transpose(bank[:, j * P:(j + 1) * P], tiles(j), ident)
    return ins


def retention_layer(core):
    nc, arg, x, ident, bank = core.nc, core.arg, core.x, core.ident, core.bank
    with ExitStack() as ctx:
        def sb(name, shape, dt=F32):
            return core.sb(ctx, "ret_" + name, shape, dt)

        def sem(name):
            return core.layer_sem("ret_" + name)

        wqk, rope, wvg, causal, wo, gnorm = (core.ret[k] for k in ("wqk", "rope", "wvg", "causal", "wo", "gnorm"))
        st = core.ln_buffers(ctx, "ret_ln")
        xn = sb("xn", [P, PAIR, D])
        xnT = sb("xnT", [P, WIDE])
        rot = sb("rot", [P, 4, WIDE])
        qT = sb("qT", [P, WIDE])
        kT = sb("kT", [P, WIDE])
        kT_head = sb("kT_head", [P, RH, WIDE])
        v = sb("v", [P, PAIR, RH * RV])
        gate = sb("gate", [P, PAIR, RH * RV])
        gain = sb("gain", [P, PAIR, RH * RV])
        scores = sb("scores", [P, 2, RH, CAUSAL])
        osq = sb("osq", [P, PAIR, RH * RV])
        ms = sb("ms", [P, PAIR * RH])
        rms = sb("rms", [P, PAIR * RH])
        mtmp = sb("mtmp", [P, PAIR * RH])
        o = sb("o", [P, PAIR, RH * RV])
        oT = sb("oT", [P, 2, WIDE])

        xn_ready = sem("xn_ready")
        xn_turned = sem("xn_turned")
        xnT_ready = sem("xnT_ready")
        qk_ready = sem("qk_ready")
        rot_ready = sem("rot_ready")
        qk_rotated = sem("qk_rotated")
        k_parted = sem("k_parted")
        vg_ready = sem("vg_ready")
        vg_read = sem("vg_read")
        gain_ready = sem("gain_ready")
        scores_ready = sem("scores_ready")
        scores_masked = sem("scores_masked")
        o_ready = sem("o_ready")
        osq_ready = sem("osq_ready")
        o_scaled = sem("o_scaled")
        o_gated = sem("o_gated")
        o_turned = sem("o_turned")
        oT_ready = sem("oT_ready")
        y_ready = sem("y_ready")
        y_added = sem("y_added")
        vec_per = 1 + 1 + 11
        SCORES, QK, VG, O = ((1, 2, 3, 4), (6, 7, 0, 5)), (2, 3, 4, 7), (5, 0, 2, 3), (1, 6)
        OT, Y = (4, 7), 5
        block = ctx.enter_context(nc.Block())

        @block.sync
        def _(sp):
            for layer in LOAD_ORDER:
                for buffer, source in core.loads[layer]:
                    sp.dma_start(buffer, source).then_inc(core.loaded[layer], 16)

        @block.tensor
        def _(pe):
            core.wait_loaded(pe, "ret")

            def project(i):
                pe.wait_ge(xn_ready, 4 * i + 4)
                transpose_tiles(pe, bank[0], lambda j: xn[:, j, :], ident[:, :]).then_inc(xn_turned, 1)
                pe.wait_ge(xnT_ready, i + 1)
                for a in range(4):
                    pe.matmul(bank[QK[a]][:, :], wqk[:, a, :], xnT[:, :], start=True, stop=True).then_inc(qk_ready, 1)
                for j in range(PAIR):
                    if j >= 2:
                        pe.wait_ge(rot_ready, 4 * i + j - 1)
                    pe.matmul(bank[VG[j]][:, :], xnT[:, j * P:(j + 1) * P], wvg[:, :],
                              start=True, stop=True).then_inc(vg_ready, 1)

            project(0)

            def body(i, more):
                pe.wait_ge(qk_rotated, 2 * i + 2)
                pe.wait_ge(vg_read, 8 * i + 8)
                for s in range(2):
                    if s == 1:
                        wait_last_round(pe, y_added, i)
                    for h in range(RH):
                        if s == 0:
                            pe.wait_ge(k_parted, 4 * i + h + 1)
                        at, bk = s * S, bank[SCORES[s][h]]
                        pe.matmul(bk[:, 0:S], kT_head[:, h, at:at + P], qT[:, at:at + S], start=True, stop=True)
                        pe.matmul(bk[:, S:CAUSAL], kT_head[:, h, at + P:at + S], qT[:, at + P:at + S],
                                  start=True, stop=True).then_inc(scores_ready, 1)
                for s in range(2):
                    pe.wait_ge(scores_masked, 8 * i + 4 * s + 4)
                    bk = bank[O[s]]
                    for h in range(RH):
                        vh = slice(h * RV, (h + 1) * RV)
                        out0 = bk[:, h * RV:(h + 1) * RV]
                        out1 = bk[:, S + h * RV:S + (h + 1) * RV]
                        pe.matmul(out0, scores[:, s, h, 0:P], v[:, 2 * s, vh], start=True, stop=True)
                        pe.matmul(out1, scores[:, s, h, P:S], v[:, 2 * s, vh], start=True, stop=False)
                        mm = pe.matmul(out1, scores[:, s, h, S:CAUSAL], v[:, 2 * s + 1, vh], start=False, stop=True)
                    mm.then_inc(o_ready, 1)
                if more:
                    project(i + 1)
                    pe.wait_ge(rot_ready, 4 * i + 8)
                pe.wait_ge(o_gated, i + 1)
                for a in range(2):
                    transpose_tiles(pe, bank[OT[a]], lambda j: o[:, j, a * P:(a + 1) * P],
                                    ident[:, :]).then_inc(o_turned, 1)
                if more:
                    pe.wait_ge(vg_read, 8 * i + 10)
                pe.wait_ge(oT_ready, 2 * i + 2)
                for j in range(PAIR):
                    for a in range(2):
                        mm = pe.matmul(bank[Y][:, j * P:(j + 1) * P], oT[:, a, j * P:(j + 1) * P], wo[:, a, :],
                                       start=(a == 0), stop=(a == 1))
                mm.then_inc(y_ready, 1)
            turns(pe, PAIRS, body)

        @block.scalar
        def _(act):
            core.wait_loaded(act, "ret")
            act.preload_act_table(ACT.Silu)

            def copy_projections(i):
                act.wait_ge(xn_turned, i + 1)
                act.activation(xnT[:, :], bank[0][:, :], ACT.Copy).then_inc(xnT_ready, 1)
                for j in range(PAIR):
                    act.wait_ge(vg_ready, 4 * i + j + 1)
                    bk = bank[VG[j]]
                    if j == 0:
                        wait_last_round(act, gain_ready, i)
                    act.activation(v[:, j, :], bk[:, 0:RH * RV], ACT.Copy).then_inc(vg_read, 1)
                    act.activation(gate[:, j, :], bk[:, RH * RV:], ACT.Silu).then_inc(vg_read, 1)

            def part_k(i):
                wait_last_round(act, scores_ready, 8 * i)
                act.wait_ge(qk_rotated, 2 * i + 2)
                for h in range(RH):
                    act.activation(kT_head[:, h, :], kT[:, :], ACT.Copy, scale=core.head_rows[:, h:h + 1]).then_inc(k_parted, 1)

            copy_projections(0)
            part_k(0)

            def body(i, more):
                for s in range(2):
                    act.wait_ge(o_ready, 2 * i + s + 1)
                    act.activation(osq[:, 2 * s:2 * s + 2, :],
                                   bank[O[s]][:, :].rearrange("p (j n) -> p j n", j=2),
                                   ACT.Square).then_inc(osq_ready, 1)
                if more:
                    copy_projections(i + 1)
                for a in range(2):
                    act.wait_ge(o_turned, 2 * i + a + 1)
                    act.activation(oT[:, a, :], bank[OT[a]][:, :], ACT.Copy).then_inc(oT_ready, 1)
                if more:
                    part_k(i + 1)
            turns(act, PAIRS, body)

        @block.vector
        def _(vec):
            core.wait_loaded(vec, "x")
            for i in range(PAIRS):
                tile_stats(core, vec, i)
            moments(core, vec, st, False)
            core.wait_loaded(vec, "ret")

            def start(i):
                wait_last_round(vec, xn_turned, i)
                for ins in normalize(core, vec, st, i, xn):
                    ins.then_inc(xn_ready, 1)

            def rotate(i):
                for a in range(4):
                    vec.wait_ge(qk_ready, 4 * i + a + 1)
                    if a == 0:
                        wait_last_round(vec, qk_rotated, 2 * i)
                    vec.tensor_tensor(rot[:, a, :].rearrange("p (s t) -> p s t", s=2),
                                      bank[QK[a]][:, :].rearrange("p (s t) -> p s t", s=2),
                                      rope[:, a:a + 1, :].to_broadcast([P, 2, S]), ALU.mult).then_inc(rot_ready, 1)

            start(0)
            rotate(0)

            def body(i, more):
                steps = Steps(core, vec, i, vec_per)
                wait_last_round(vec, y_added, i)
                if more:
                    start(i + 1)
                for s in range(2):
                    for h in range(RH):
                        vec.wait_ge(scores_ready, 8 * i + 4 * s + h + 1)
                        vec.tensor_tensor(scores[:, s, h, :], bank[SCORES[s][h]][:, 0:CAUSAL], causal[:, :],
                                          ALU.mult).then_inc(scores_masked, 1)
                if not is_first(i):
                    tile_stats(core, vec, i - 1)
                vec.wait_ge(osq_ready, 2 * i + 2)
                steps.done(vec.tensor_reduce(ms[:, :], osq[:, :, :].rearrange("p j (h n) -> p (j h) n", h=RH),
                                             AX.X, ALU.add))
                steps.wait()
                steps.done(vec.tensor_scalar(ms[:, :], ms[:, :], 1.0 / RV, LN_EPS, ALU.mult, ALU.add))
                steps.wait()
                rsqrt(vec, steps, rms[:, :], ms[:, :], mtmp[:, :])
                steps.wait()
                for s in range(2):
                    if s == 0:
                        wait_last_round(vec, o_turned, 2 * i)
                    vec.tensor_tensor(
                        o[:, 2 * s:2 * s + 2, :].rearrange("p j (h n) -> p (j h) n", h=RH),
                        bank[O[s]][:, :].rearrange("p (g n) -> p g n", n=RV),
                        rms[:, 8 * s:8 * s + 8].unsqueeze(2).to_broadcast([P, 8, RV]), ALU.mult).then_inc(o_scaled, 1)
                if more:
                    rotate(i + 1)
                vec.wait_ge(y_ready, i + 1)
                vec.tensor_tensor(x[:, bass.ds(4 * i, PAIR), :], x[:, bass.ds(4 * i, PAIR), :],
                                  bank[Y][:, :].rearrange("p (j n) -> p j n", j=PAIR), ALU.add).then_inc(y_added, 1)
                assert steps.n == vec_per
            turns(vec, PAIRS, body)
            vec.wait_ge(y_added, PAIRS)
            tile_stats(core, vec, PAIRS - 1)
            core.vector_base += PAIRS * vec_per

        @block.gpsimd
        def _(pool):
            core.wait_loaded(pool, "ret")

            def add_up(i):
                for a, dst in enumerate((qT, kT)):
                    pool.wait_ge(rot_ready, 4 * i + 2 * a + 2)
                    if a == 0:
                        wait_last_round(pool, scores_ready, 8 * i)
                    pool.tensor_tensor(dst[:, :], rot[:, 2 * a, :], rot[:, 2 * a + 1, :],
                                       ALU.add).then_inc(qk_rotated, 1)

            add_up(0)

            def body(i, more):
                wait_last_round(pool, o_gated, i)
                pool.wait_ge(vg_read, 8 * i + 8)
                pool.tensor_tensor(gain[:, :, :], gate[:, :, :], gnorm[:, :].unsqueeze(1).to_broadcast([P, PAIR, RH * RV]),
                                   ALU.mult).then_inc(gain_ready, 1)
                pool.wait_ge(gain_ready, i + 1)
                pool.wait_ge(o_scaled, 2 * i + 2)
                pool.tensor_tensor(o[:, :, :], o[:, :, :], gain[:, :, :], ALU.mult).then_inc(o_gated, 1)
                if more:
                    add_up(i + 1)
            turns(pool, PAIRS, body)


def depool_layer(core):
    nc, x, ident, bank = core.nc, core.x, core.ident, core.bank
    with ExitStack() as ctx:
        def sb(name, shape, dt=F32):
            return core.sb(ctx, "dep_" + name, shape, dt)

        def sem(name):
            return core.layer_sem("dep_" + name)

        lens, cx, ginit, index, upto, gres, win, bin_ = (core.dep[k] for k in (
            "lens", "ctx", "ginit", "index", "upto", "gres", "win", "bin"))
        st = core.ln_buffers(ctx, "dep_ln")
        zeros = sb("zeros", [P, S])
        ones = sb("ones", [1, P])
        upto_b = sb("upto_b", [P, S], BF16)
        cum = sb("cum", [P, 2, S])
        wrap = sb("wrap", [P, 2, S])
        end_at = sb("end_at", [P, 2, S])
        same = sb("same", [P, 4, S])
        is_end = sb("is_end", [P, 4])
        is_end_b = sb("is_end_b", [P, 4, P], BF16)
        age = sb("age", [P, 2, CAUSAL])
        weight = sb("weight", [P, 2, CAUSAL])
        csq = sb("csq", [P, 2, DC])
        cms = sb("cms", [P, NT])
        crms = sb("crms", [P, NT])
        ctmp = sb("ctmp", [P, NT])
        u = sb("u", [P, PAIR, D])
        xn = sb("xn", [P, PAIR, D])
        xnT = sb("xnT", [P, WIDE])
        kernel = ConvKernel(core, ctx)

        set_up = sem("set_up")
        xn_ready = sem("xn_ready")
        xn_turned = sem("xn_turned")
        xnT_ready = sem("xnT_ready")
        ends_ready = sem("ends_ready")
        counts_ready = sem("counts_ready")
        ages_ready = sem("ages_ready")
        decays_ready = sem("decays_ready")
        weights_ready = sem("weights_ready")
        csq_ready = sem("csq_ready")
        crms_ready = sem("crms_ready")
        u_gained = sem("u_gained")
        u_ready = sem("u_ready")
        y_ready = sem("y_ready")
        y_added = sem("y_added")
        vec_per = 2 + 1 + 1 + 4
        block = ctx.enter_context(nc.Block())

        @block.sync
        def _(sp):
            core.clear_last_layer(sp)

        @block.tensor
        def _(pe):
            core.wait_loaded(pe, "dep")
            pe.wait_ge(set_up, 3)
            kernel.tensor(pe, range(kernel.EARLY))

            def count(i):
                pe.wait_ge(ends_ready, i + 1)
                for s in range(2):
                    pe.matmul(bank[2][:, s * S:(s + 1) * S], is_end_b[:, 2 * s, :], upto_b[:, :], start=True, stop=False)
                    mm = pe.matmul(bank[2][:, s * S + P:(s + 1) * S], is_end_b[:, 2 * s + 1, :], upto_b[:, 0:P],
                                   start=False, stop=True)
                mm.then_inc(counts_ready, 1)

            def turn_x(i):
                pe.wait_ge(xn_ready, 4 * i + 4)
                transpose_tiles(pe, bank[0], lambda j: xn[:, j, :], ident[:, :]).then_inc(xn_turned, 1)

            count(0)
            turn_x(0)

            def body(i, more):
                wait_last_round(pe, y_added, i)
                pe.wait_ge(xnT_ready, i + 1)
                pe.wait_ge(u_ready, i + 1)
                pe.wait_ge(weights_ready, i + 1)
                for s in range(2):
                    for t in range(2):
                        j = 2 * s + t
                        y = bank[1][:, j * P:(j + 1) * P]
                        pe.matmul(y, ones[:, :], bin_[:, :], start=True, stop=False)
                        pe.matmul(y, xnT[:, j * P:(j + 1) * P], win[:, :], start=False, stop=False)
                        mm = pe.matmul(y, weight[:, s, t * P:(t + 1) * P], u[:, 2 * s, :], start=False, stop=(t == 0))
                        if t == 1:
                            mm = pe.matmul(y, weight[:, s, S:CAUSAL], u[:, 2 * s + 1, :], start=False, stop=True)
                mm.then_inc(y_ready, 1)
                if more:
                    turn_x(i + 1)
                    count(i + 1)
            body(0, True)
            kernel.tensor(pe, range(kernel.EARLY, 5))
            with pe.Fori(1, PAIRS - 1) as i:
                body(i, True)
            kernel.tensor(pe, range(5, kernel.CUT))
            body(PAIRS - 1, False)

        @block.scalar
        def _(act):
            core.wait_loaded(act, "dep")
            act.preload_act_table(ACT.Exp)
            for t in range(NT):
                if t >= 2:
                    act.wait_ge(csq_ready, t - 1)
                act.activation(csq[:, t % 2, :], cx[:, t, :], ACT.Square, accum_out=cms[:, t:t + 1]).then_inc(csq_ready, 1)
            kernel.scalar(act)

            def body(i, more):
                wait_last_round(act, y_ready, i)
                act.wait_ge(xn_turned, i + 1)
                act.activation(xnT[:, :], bank[0][:, :], ACT.Copy, scale=gres[:, 0:1]).then_inc(xnT_ready, 1)
                act.wait_ge(ages_ready, 4 * i + 4)
                act.activation(weight[:, :, :], age[:, :, :], ACT.Exp, scale=-DEPOOL_DT).then_inc(decays_ready, 1)
            turns(act, PAIRS, body)

        @block.vector
        def _(vec):
            core.wait_loaded(vec, "dep")
            kernel.vector(vec)
            vec.memset(zeros[:, :], 0.0).then_inc(set_up, 1)
            vec.memset(ones[:, :], 1.0).then_inc(set_up, 1)
            vec.tensor_copy(upto_b[:, :], upto[:, :]).then_inc(set_up, 1)
            vec.wait_ge(set_up, 3)
            moments(core, vec, st, True)
            steps = Steps(core, vec)
            vec.wait_ge(csq_ready, NT)
            steps.done(vec.tensor_scalar(cms[:, :], cms[:, :], 1.0 / DC, LN_EPS, ALU.mult, ALU.add))
            steps.wait()
            rsqrt(vec, steps, crms[:, :], cms[:, :], ctmp[:, :])
            steps.wait()
            vec.tensor_scalar(crms[:, :], crms[:, :], DEPOOL_B, None, ALU.mult).then_inc(crms_ready, 1)
            steps.close()

            def find_ends(i):
                steps = Steps(core, vec, i, vec_per)
                for s in range(2):
                    steps.done(vec.tensor_tensor_scan(out=cum[:, s, :], data0=lens[:, bass.ds(2 * i + s, 1), :].rearrange("p o n -> p (o n)"), data1=zeros[:, :],
                                                      initial=0.0, op0=ALU.add, op1=ALU.add))
                steps.wait()
                steps.done(vec.tensor_scalar(wrap[:, :, :], cum[:, :, :], 1.0, float(S), ALU.is_lt, ALU.mult))
                steps.wait()
                steps.done(vec.scalar_tensor_tensor(out=end_at[:, :, :], in0=cum[:, :, :], scalar=-1.0,
                                                    in1=wrap[:, :, :], op0=ALU.add, op1=ALU.add))
                steps.wait()
                for s in range(2):
                    for t in range(2):
                        steps.done(vec.tensor_scalar(same[:, 2 * s + t, :], end_at[:, s, :], index[:, t:t + 1], None, ALU.is_equal,
                                                     ALU.max, accum_out=is_end[:, 2 * s + t:2 * s + t + 1]))
                steps.wait()
                wait_last_round(vec, counts_ready, i)
                vec.tensor_copy(is_end_b[:, :, :], is_end[:, :].unsqueeze(2).to_broadcast([P, 4, P])).then_inc(ends_ready, 1)
                assert steps.n == vec_per

            def start(i):
                wait_last_round(vec, xn_turned, i)
                for ins in normalize(core, vec, st, i, xn):
                    ins.then_inc(xn_ready, 1)

            find_ends(0)
            start(0)

            def body(i, more):
                vec.wait_ge(counts_ready, i + 1)
                wait_last_round(vec, weights_ready, i)
                for s in range(2):
                    vec.tensor_scalar(age[:, s, 0:S], bank[2][:, s * S:(s + 1) * S], index[:, 2:3], index[:, 4:5],
                                      ALU.subtract, ALU.max).then_inc(ages_ready, 1)
                    vec.tensor_scalar(age[:, s, S:CAUSAL], bank[2][:, s * S + P:(s + 1) * S], index[:, 3:4],
                                      index[:, 5:6], ALU.subtract, ALU.max).then_inc(ages_ready, 1)
                if more:
                    start(i + 1)
                vec.wait_ge(decays_ready, i + 1)
                vec.scalar_tensor_tensor(out=weight[:, :, :], in0=age[:, :, :], scalar=0.0, in1=weight[:, :, :],
                                         op0=ALU.is_ge, op1=ALU.mult).then_inc(weights_ready, 1)
                if more:
                    find_ends(i + 1)
                vec.wait_ge(y_ready, i + 1)
                vec.tensor_tensor(x[:, bass.ds(4 * i, PAIR), :], x[:, bass.ds(4 * i, PAIR), :],
                                  bank[1][:, :].rearrange("p (j n) -> p j n", j=PAIR), ALU.add).then_inc(y_added, 1)
            turns(vec, PAIRS, body)
            vec.wait_ge(y_added, PAIRS)
            for i in range(PAIRS):
                tile_stats(core, vec, i)
            core.vector_base += PAIRS * vec_per

        @block.gpsimd
        def _(pool):
            core.wait_loaded(pool, "dep")
            kernel.gpsimd(pool)
            pool.wait_ge(crms_ready, 1)

            def body(i):
                wait_last_round(pool, y_ready, i)
                pool.tensor_tensor(u[:, :, :], cx[:, bass.ds(4 * i, PAIR), 0:D],
                                   ginit[:, :].unsqueeze(1).to_broadcast([P, PAIR, D]), ALU.mult).then_inc(u_gained, 1)
                pool.wait_ge(u_gained, i + 1)
                pool.tensor_tensor(u[:, :, :], u[:, :, :], crms[:, bass.ds(4 * i, PAIR)].unsqueeze(2).to_broadcast([P, PAIR, D]),
                                   ALU.mult).then_inc(u_ready, 1)
            rounds(pool, PAIRS, body)


class ConvKernel:

    HALF = D // 2
    CUT = 8
    EARLY = 3
    BUFFERS = CUT - EARLY
    PART = HALF // CUT

    def __init__(self, core, ctx):
        self.core, self.w = core, core.conv
        HALF, PART = self.HALF, self.PART

        def sb(name, shape):
            return core.sb(ctx, "kernel_" + name, shape)

        def sem(name):
            return core.layer_sem("kernel_" + name)

        self.rate = sb("rate", [P, HALF])
        self.late = sb("late", [P, HALF])
        self.gain = sb("gain", [P, HALF])
        self.gains = sb("gains", [P, HALF, 4])
        self.angle = sb("angle", [P, 2, PART, P])
        self.power = sb("power", [P, self.BUFFERS, PART, P])
        self.signed = sem("signed")
        self.rates_ready = sem("rates_ready")
        self.gains_ready = sem("gains_ready")
        self.angles_ready = sem("angles_ready")
        self.powers_ready = sem("powers_ready")
        self.powers_used = sem("powers_used")

    def tensor(self, pe, parts):
        bank = self.core.bank
        pe.wait_ge(self.gains_ready, 2)
        for c in parts:
            pe.wait_ge(self.powers_ready, c + 1)
            for j in range(c * self.PART, (c + 1) * self.PART):
                mm = pe.matmul(bank[7][:, 4 * j:4 * j + 4], self.power[:, c % self.BUFFERS, j % self.PART, :],
                               self.gains[:, j, :], start=True, stop=True)
            mm.then_inc(self.powers_used, 1)

    def scalar(self, act):
        self.core.wait_loaded(act, "conv")
        act.activation(self.rate[:, :], self.w["alog"][:, :], ACT.Exp, scale=-1.0).then_inc(self.rates_ready, 1)
        act.wait_ge(self.signed, 1)
        act.activation(self.late[:, :], self.rate[:, :], ACT.Exp, scale=float(P)).then_inc(self.rates_ready, 1)
        for c in range(self.CUT):
            act.wait_ge(self.angles_ready, c + 1)
            if c >= self.BUFFERS:
                act.wait_ge(self.powers_used, c - self.BUFFERS + 1)
            act.activation(self.power[:, c % self.BUFFERS], self.angle[:, c % 2], ACT.Exp).then_inc(self.powers_ready, 1)

    def vector(self, vec):
        core, w = self.core, self.w
        rate, late, gain = self.rate, self.late, self.gain
        core.wait_loaded(vec, "conv")
        setup = Steps(core, vec)
        setup.done(vec.tensor_tensor(gain[:, :], w["b"][:, :], w["dt"][:, :], ALU.mult))
        setup.wait()
        setup.done(vec.tensor_tensor(gain[:, :], gain[:, :], w["c"][:, :], ALU.mult))
        vec.wait_ge(self.rates_ready, 1)
        vec.scalar_tensor_tensor(out=rate[:, :], in0=rate[:, :], scalar=-1.0, in1=w["dt"][:, :],
                                 op0=ALU.mult, op1=ALU.mult).then_inc(self.signed, 1)
        vec.wait_ge(self.rates_ready, 2)
        setup.wait()
        setup.done(vec.tensor_tensor(late[:, :], late[:, :], gain[:, :], ALU.mult))
        setup.wait()
        for h, g in enumerate((gain, late)):
            vec.tensor_tensor(self.gains[:, :, 2 * h:2 * h + 2], g[:, :].unsqueeze(2).to_broadcast([P, self.HALF, 2]),
                              w["half"][:, :].unsqueeze(1).to_broadcast([P, self.HALF, 2]),
                              ALU.mult).then_inc(self.gains_ready, 1)
        setup.close()

    def gpsimd(self, pool):
        self.core.wait_loaded(pool, "conv")
        pool.wait_ge(self.signed, 1)
        for c in range(self.CUT):
            part = slice(c * self.PART, (c + 1) * self.PART)
            if c >= 2:
                pool.wait_ge(self.powers_ready, c - 1)
            pool.tensor_tensor(self.angle[:, c % 2], self.w["time"][:, :].unsqueeze(1).to_broadcast([P, self.PART, P]),
                               self.rate[:, part].unsqueeze(2).to_broadcast([P, self.PART, P]), ALU.mult
                               ).then_inc(self.angles_ready, 1)


class KernelSpectrum:

    def __init__(self, core, ctx):
        self.core, self.w = core, core.conv
        self.kernel_t = core.sb(ctx, "kernel_t", [P, 2, D])
        self.packed = core.sb(ctx, "kernel_packed", [P, D])
        self.kernel_copied = core.layer_sem("kernel_copied")
        self.kspec_ready = core.layer_sem("kspec_ready")
        self.kspec_copied = core.layer_sem("kspec_copied")

    def tensor(self, pe):
        bank, dft = self.core.bank, self.w["dft"]
        pe.wait_ge(self.kernel_copied, 3)
        for m in range(4):
            for j in range(2):
                mm = pe.matmul(bank[6][:, m * D:(m + 1) * D], dft[:, j, m * P:(m + 1) * P], self.kernel_t[:, j, :],
                               start=(j == 0), stop=(j == 1))
        mm.then_inc(self.kspec_ready, 1)

    def copy_kernel(self, vec):
        kernel_t, bank = self.kernel_t, self.core.bank
        self.core.wait_loaded(vec, "conv")
        for h in range(2):
            vec.tensor_copy(kernel_t[:, h, :].rearrange("p (j c) -> p j c", c=2),
                            bank[7][:, 0:2 * D].rearrange("p (j h c) -> p h j c", h=2, c=2)[:, h]
                            ).then_inc(self.kernel_copied, 1)
        vec.wait_ge(self.kernel_copied, 2)
        vec.tensor_tensor(kernel_t[0:1, 0, :], kernel_t[0:1, 0, :], self.w["skip"][:, :], ALU.add).then_inc(self.kernel_copied, 1)

    def copy_spectrum(self, vec):
        w, packed, copied = self.w, self.packed, self.kspec_copied
        kre, kim, kre2 = self.core.kernel_spectrum
        vec.wait_ge(self.kspec_ready, 1)
        kbank = self.core.bank[6][:, :].rearrange("p (m d) -> p m d", m=4)
        vec.tensor_copy(kre[:, :, :], kbank[:, 0:2]).then_inc(copied, 1)
        vec.tensor_scalar(packed[:, :], kbank[:, 2], w["packed"][:, 0:1], None, ALU.mult).then_inc(copied, 1)
        vec.tensor_scalar(kim[:, 0, :], kbank[:, 2], w["packed"][:, 1:2], None, ALU.mult).then_inc(copied, 1)
        vec.tensor_copy(kim[:, 1, :], kbank[:, 3]).then_inc(copied, 1)
        vec.tensor_copy(kre2[:, 1, :], kbank[:, 1]).then_inc(copied, 1)
        vec.wait_ge(copied, 5)
        vec.scalar_tensor_tensor(out=kre2[:, 0, :], in0=kre[:, 0, :], scalar=w["packed"][:, 1:2], in1=packed[:, :],
                                 op0=ALU.mult, op1=ALU.add).then_inc(copied, 1)


def conv_layer(core):
    nc, x, ident, bank = core.nc, core.x, core.ident, core.bank
    w = core.conv
    with ExitStack() as ctx:
        def sb(name, shape, dt=F32):
            return core.sb(ctx, "conv_" + name, shape, dt)

        def sem(name):
            return core.layer_sem("conv_" + name)

        dft, idft, win, wout = (w[k] for k in ("dft", "idft", "win", "wout"))
        kre, kim, kre2 = core.kernel_spectrum
        st = core.ln_buffers(ctx, "conv_ln")
        xn = sb("xn", [P, PAIR, D])
        xnT = sb("xnT", [P, WIDE])
        u = sb("u", [P, PAIR, D])
        prod = sb("prod", [P, 4, 4, P])
        spec = sb("spec", [P, 4, 2, D])
        yT = sb("yT", [P, WIDE])

        xn_ready = sem("xn_ready")
        xn_turned = sem("xn_turned")
        xnT_ready = sem("xnT_ready")
        x_biased = sem("x_biased")
        u_ready = sem("u_ready")
        u_copied = sem("u_copied")
        uspec_ready = sem("uspec_ready")
        products_ready = sem("products_ready")
        spec_ready = sem("spec_ready")
        yT_ready = sem("yT_ready")
        yT_copied = sem("yT_copied")
        y_ready = sem("y_ready")
        y_added = sem("y_added")
        block = ctx.enter_context(nc.Block())

        @block.sync
        def _(sp):
            core.clear_last_layer(sp)

        @block.tensor
        def _(pe):
            core.wait_loaded(pe, "conv")

            def turn_x(i):
                pe.wait_ge(xn_ready, 4 * i + 4)
                transpose_tiles(pe, bank[0], lambda j: xn[:, j, :], ident[:, :]).then_inc(xn_turned, 1)

            def make_u(i):
                pe.wait_ge(xnT_ready, i + 1)
                for j in range(PAIR):
                    mm = pe.matmul(bank[1][:, j * P:(j + 1) * P], xnT[:, j * P:(j + 1) * P], win[:, :],
                                   start=True, stop=True)
                mm.then_inc(u_ready, 1)

            def transform(i):
                pe.wait_ge(u_copied, i + 1)
                for m in range(4):
                    for j in range(2):
                        mm = pe.matmul(bank[2 + m // 2][:, (m % 2) * S:(m % 2 + 1) * S].rearrange("p (s d) -> p s d", s=2),
                                       dft[:, j, m * P:(m + 1) * P],
                                       u[:, j:PAIR:2, :], start=(j == 0), stop=(j == 1))
                    if m % 2:
                        mm.then_inc(uspec_ready, 1)

            turn_x(0)
            make_u(0)
            transform(0)

            def body(i, more):
                if more:
                    turn_x(i + 1)
                    make_u(i + 1)
                pe.wait_ge(spec_ready, 2 * i + 2)
                for s in range(2):
                    for m in range(4):
                        mm = pe.matmul(bank[4][:, s * S:(s + 1) * S], spec[:, m, s, :], idft[:, m, :],
                                       start=(m == 0), stop=(m == 3))
                mm.then_inc(yT_ready, 1)
                if more:
                    transform(i + 1)
                pe.wait_ge(yT_copied, i + 1)
                wait_last_round(pe, y_added, i)
                for j in range(PAIR):
                    mm = pe.matmul(bank[5][:, j * P:(j + 1) * P], yT[:, j * P:(j + 1) * P], wout[:, :],
                                   start=True, stop=True)
                mm.then_inc(y_ready, 1)
            turns(pe, PAIRS, body)

        @block.scalar
        def _(act):
            def copy_x(i):
                act.wait_ge(xn_turned, i + 1)
                act.activation(xnT[:, :], bank[0][:, :], ACT.Copy).then_inc(xnT_ready, 1)
            copy_x(0)

            def body(i, more):
                if more:
                    copy_x(i + 1)
                act.wait_ge(yT_ready, i + 1)
                act.activation(yT[:, :], bank[4][:, :], ACT.Copy).then_inc(yT_copied, 1)
            turns(act, PAIRS, body)

        @block.vector
        def _(vec):
            core.wait_loaded(vec, "conv")
            moments(core, vec, st, False)

            def pair(i):
                return x[:, bass.ds(4 * i, PAIR), :]

            def start(i):
                wait_last_round(vec, xn_turned, i)
                for ins in normalize(core, vec, st, i, xn):
                    ins.then_inc(xn_ready, 1)
                vec.wait_ge(xn_ready, 4 * i + 4)
                vec.tensor_tensor(pair(i), pair(i), w["bout"][:, :].unsqueeze(1).to_broadcast([P, PAIR, D]),
                                  ALU.add).then_inc(x_biased, 1)

            def copy_u(i):
                vec.wait_ge(u_ready, i + 1)
                vec.tensor_tensor(u[:, :, :], bank[1][:, :].rearrange("p (j n) -> p j n", j=PAIR),
                                  w["bin"][:, :].unsqueeze(1).to_broadcast([P, PAIR, D]), ALU.add).then_inc(u_copied, 1)

            def add_y(i):
                vec.wait_ge(x_biased, i + 1)
                vec.wait_ge(y_ready, i + 1)
                vec.tensor_tensor(pair(i), pair(i), bank[5][:, :].rearrange("p (j n) -> p j n", j=PAIR),
                                  ALU.add).then_inc(y_added, 1)

            start(0)
            copy_u(0)

            def body(i, more):
                if more:
                    start(i + 1)
                if not is_first(i):
                    add_y(i - 1)
                vec.wait_ge(uspec_ready, 2 * i + 2)
                wait_last_round(vec, spec_ready, 2 * i)
                wait_last_round(vec, y_added, i)
                for q, (half, k) in enumerate(((0, kre), (1, kim), (0, kim), (1, kre2))):
                    vec.tensor_tensor(prod[:, q, :, :].rearrange("p (m s) d -> p m s d", m=2),
                                      bank[2 + half][:, :].rearrange("p (m s d) -> p m s d", m=2, s=2),
                                      k[:, :, :].unsqueeze(2).to_broadcast([P, 2, 2, D]),
                                      ALU.mult).then_inc(products_ready, 1)
                if more:
                    copy_u(i + 1)
                if not is_first(i):
                    tile_stats(core, vec, i - 1)
            turns(vec, PAIRS, body)
            add_y(PAIRS - 1)
            vec.wait_ge(y_added, PAIRS)
            tile_stats(core, vec, PAIRS - 1)

        @block.gpsimd
        def _(pool):
            def body(i):
                for half, op in ((0, ALU.subtract), (1, ALU.add)):
                    pool.wait_ge(products_ready, 4 * i + 2 * half + 2)
                    if half == 0:
                        wait_last_round(pool, yT_ready, i)
                    pool.tensor_tensor(spec[:, 2 * half:2 * half + 2, :, :].rearrange("p m s d -> p (m s) d"),
                                       prod[:, 2 * half, :, :], prod[:, 2 * half + 1, :, :], op).then_inc(spec_ready, 1)
            rounds(pool, PAIRS, body)


def cross_attention_layer(core):
    nc, x, ident, bank, psum = core.nc, core.x, core.ident, core.bank, core.psum
    w = core.xat
    with ExitStack() as ctx:
        def sb(name, shape, dt=F32):
            return core.sb(ctx, "xat_" + name, shape, dt)

        def sem(name):
            return core.layer_sem("xat_" + name)

        wk, wv, wq, bv, wout, qmask = (w[k] for k in ("wk", "wv", "wq", "bv", "wout", "qmask"))
        st = core.ln_buffers(ctx, "xat_ln")
        kmask = sb("kmask", [P, B * S])
        xn = sb("xn", [P, PAIR, D])
        xnT = sb("xnT", [P, WIDE])
        ctxT = sb("ctxT", [P, 2, WIDE])
        kT = sb("kT", [P, 2, WIDE])
        kT_head = sb("kT_head", [P, 4, 2, WIDE])
        qT = sb("qT", [P, 2, WIDE])
        qT_less = sb("qT_less", [P, 2, WIDE])
        v = sb("v", [P, PAIR, XH, HEAD_ROWS])
        top = sb("top", [P, PAIR, 2, P])
        prob = sb("prob", [P, 2, XH, 2, S])
        heads = sb("heads", [P, 2, 2 * S])
        updT = sb("updT", [P, 2, 2 * S])

        set_up = sem("set_up")
        xn_ready = sem("xn_ready")
        xn_turned = sem("xn_turned")
        xnT_ready = sem("xnT_ready")
        ctx_loaded = sem("ctx_loaded")
        x_biased = sem("x_biased")
        k_ready = sem("k_ready")
        k_copied = sem("k_copied")
        k_parted = sem("k_parted")
        q_ready = sem("q_ready")
        q_copied = sem("q_copied")
        v_ready = sem("v_ready")
        v_copied = sem("v_copied")
        scores_ready = sem("scores_ready")
        tops_ready = sem("tops_ready")
        tops_turned = sem("tops_turned")
        q_lessened = sem("q_lessened")
        shifted_ready = sem("shifted_ready")
        probs_ready = sem("probs_ready")
        heads_ready = sem("heads_ready")
        heads_copied = sem("heads_copied")
        sums_ready = sem("sums_ready")
        sums_inverted = sem("sums_inverted")
        updT_ready = sem("updT_ready")
        y_ready = sem("y_ready")
        y_added = sem("y_added")
        RING = (6, 7, 0, 1)
        block = ctx.enter_context(nc.Block())

        @block.sync
        def _(sp):
            core.clear_last_layer(sp)

            def body(i):
                wait_last_round(sp, v_ready, i)
                sp.dma_start(ctxT[:, :, :], core.arg["ctxT"].rearrange("(a p) t -> p a t", p=P)[:, :, bass.ds(i * WIDE, WIDE)]
                             ).then_inc(ctx_loaded, 16)
            rounds(sp, PAIRS, body)

        @block.tensor
        def _(pe):
            core.wait_loaded(pe, "xat")

            def turn_x(i):
                pe.wait_ge(xn_ready, 4 * i + 4)
                transpose_tiles(pe, bank[2], lambda j: xn[:, j, :], ident[:, :]).then_inc(xn_turned, 1)

            def make_k(i):
                pe.wait_ge(ctx_loaded, 16 * i + 16)
                for g in range(2):
                    for a in range(2):
                        mm = pe.matmul(bank[6 + g], wk[:, a, g * P:(g + 1) * P], ctxT[:, a, :], start=(a == 0), stop=(a == 1))
                    mm.then_inc(k_ready, 1)

            def make_v(i):
                pe.wait_ge(xnT_ready, i + 1)
                for j in range(PAIR):
                    for a in range(2):
                        mm = pe.matmul(bank[2][:, j * P:(j + 1) * P], ctxT[:, a, j * P:(j + 1) * P], wv[:, a, :],
                                       start=(a == 0), stop=(a == 1))
                mm.then_inc(v_ready, 1)

            def make_q(i):
                for g in range(2):
                    pe.matmul(bank[4 + g], wq[:, g * P:(g + 1) * P], xnT[:, :], start=True, stop=True).then_inc(q_ready, 1)

            def turn_tops(i, s):
                pe.wait_ge(tops_ready, 8 * i + 4 * s + 4)
                for g in range(2):
                    for t in range(2):
                        mm = pe.matmul(bank[2 + 3 * s][:, g * S + t * P:g * S + (t + 1) * P], top[:, 2 * s + t, g, :],
                                       ident[:, :], start=True, stop=True)
                mm.then_inc(tops_turned, 1)

            def spread_sums(i, s):
                pe.wait_ge(heads_copied, 2 * i + s + 1)
                pe.matmul(bank[s], w["spread"][:, :], heads[:, s, :], start=True, stop=True).then_inc(sums_ready, 1)

            turn_x(0)
            make_k(0)
            make_v(0)
            make_q(0)

            def body(i, more):
                pe.wait_ge(q_copied, 2 * i + 2)
                for j in range(PAIR):
                    for c in range(2):
                        n = 2 * j + c
                        if n >= 2:
                            pe.wait_ge(tops_ready, 8 * i + n - 1)
                        if j == 0:
                            pe.wait_ge(k_parted, 4 * i + 2 * c + 2)
                        for h in range(2 * c, 2 * c + 2):
                            at = (j // 2) * S
                            for g in range(2):
                                mm = pe.matmul(psum[:, (6, 0)[c] + h % 2, g * S:(g + 1) * S],
                                               qT[:, g, j * P:(j + 1) * P], kT_head[:, h, g, at:at + S],
                                               start=True, stop=True)
                        mm.then_inc(scores_ready, 1)
                pe.wait_ge(v_copied, i + 1)
                turn_tops(i, 0)
                wait_last_round(pe, y_added, i)
                for j in range(PAIR):
                    pe.matmul(bank[3][:, j * P:(j + 1) * P], xnT[:, j * P:(j + 1) * P], wout[:, 0, :], start=(j == 0),
                              stop=False)
                turn_tops(i, 1)
                for s in range(2):
                    pe.wait_ge(q_lessened, 2 * i + s + 1)
                    for h in range(XH):
                        n = XH * s + h
                        if n >= 4:
                            pe.wait_ge(probs_ready, 16 * i + n - 3)
                        g, at = h // 4, s * S
                        for t in range(2):
                            mm = pe.matmul(bank[RING[n % 4]][:, t * S:(t + 1) * S],
                                           kT_head[:, h % 4, g, at + t * P:at + (t + 1) * P], qT_less[:, g, at:at + S],
                                           start=True, stop=True)
                        mm.then_inc(shifted_ready, 1)
                for s in range(2):
                    pe.wait_ge(probs_ready, 16 * i + 8 * s + 8)
                    for g in range(2):
                        if (s, g) == (1, 1):
                            spread_sums(i, 0)
                        for h in range(4):
                            rows = slice(HEAD_ROWS * h, HEAD_ROWS * (h + 1))
                            for a in range(2):
                                mm = pe.matmul(bank[4 + s][rows, g * S:(g + 1) * S], v[:, 2 * s + a, 4 * g + h, :],
                                               prob[:, s, 4 * g + h, a, :], start=(a == 0), stop=(a == 1))
                    mm.then_inc(heads_ready, 1)
                if more:
                    turn_x(i + 1)
                    make_k(i + 1)
                spread_sums(i, 1)
                if more:
                    make_v(i + 1)
                    make_q(i + 1)
                pe.wait_ge(updT_ready, 2 * i + 2)
                for j in range(PAIR):
                    for g in range(2):
                        at = g * S + (j % 2) * P
                        mm = pe.matmul(bank[3][:, j * P:(j + 1) * P], updT[:, j // 2, at:at + P], wout[:, 1 + g, :],
                                       start=False, stop=(j == PAIR - 1 and g == 1))
                mm.then_inc(y_ready, 1)
            turns(pe, PAIRS, body)

        @block.scalar
        def _(act):
            act.preload_act_table(ACT.Exp)

            def front(i):
                act.wait_ge(xn_turned, i + 1)
                act.activation(xnT[:, :], bank[2], ACT.Copy).then_inc(xnT_ready, 1)
                act.wait_ge(k_copied, 2 * i + 2)
                wait_last_round(act, shifted_ready, 16 * i)
                for h in range(4):
                    act.activation(kT_head[:, h, :, :], kT[:, :, :], ACT.Copy, scale=core.head_rows[:, h:h + 1]).then_inc(k_parted, 1)
            front(0)

            def body(i, more):
                for s in range(2):
                    for h in range(XH):
                        n = XH * s + h
                        act.wait_ge(shifted_ready, 16 * i + n + 1)
                        act.activation(prob[:, s, h, :, :], bank[RING[n % 4]].rearrange("p (a t) -> p a t", a=2), ACT.Exp,
                                       scale=XD ** -0.5).then_inc(probs_ready, 1)
                for s in range(2):
                    act.wait_ge(heads_ready, 2 * i + s + 1)
                    act.activation(heads[:, s, :], bank[4 + s], ACT.Copy).then_inc(heads_copied, 1)
                if more:
                    front(i + 1)
            turns(act, PAIRS, body)

        @block.vector
        def _(vec):
            core.wait_loaded(vec, "xat")
            moments(core, vec, st, False)

            def front(i):
                for ins in normalize(core, vec, st, i, xn):
                    ins.then_inc(xn_ready, 1)
                vec.wait_ge(xn_ready, 4 * i + 4)
                vec.tensor_tensor(x[:, bass.ds(4 * i, PAIR), :], x[:, bass.ds(4 * i, PAIR), :],
                                  w["bout"][:, :].unsqueeze(1).to_broadcast([P, PAIR, D]), ALU.add).then_inc(x_biased, 1)

            def copy_k(i):
                for g in range(2):
                    vec.wait_ge(k_ready, 2 * i + g + 1)
                    vec.scalar_tensor_tensor(out=kT[:, g, :], in0=bank[6 + g], scalar=w["kbias"][:, g:g + 1],
                                             in1=kmask[:, bass.ds(i * WIDE, WIDE)], op0=ALU.add, op1=ALU.add
                                             ).then_inc(k_copied, 1)

            def copy_qv(i):
                for g in range(2):
                    vec.wait_ge(q_ready, 2 * i + g + 1)
                    vec.scalar_tensor_tensor(out=qT[:, g, :], in0=bank[4 + g], scalar=w["qbias"][:, g:g + 1],
                                             in1=qmask[:, bass.ds(i * WIDE, WIDE)], op0=ALU.add, op1=ALU.mult
                                             ).then_inc(q_copied, 1)
                vec.wait_ge(v_ready, i + 1)
                vec.tensor_tensor(v[:, :, :, 0:XD], bank[2].rearrange("p (j h n) -> p j h n", j=PAIR, h=XH),
                                  bv[:, :].rearrange("p (h n) -> p h n", h=XH).unsqueeze(1).to_broadcast([P, PAIR, XH, XD]),
                                  ALU.add).then_inc(v_copied, 1)

            front(0)
            vec.wait_ge(set_up, 4)
            copy_k(0)
            copy_qv(0)

            def body(i, more):
                wait_last_round(vec, y_added, i)
                for j in range(PAIR):
                    for c in range(2):
                        n = 2 * j + c
                        vec.wait_ge(scores_ready, 8 * i + n + 1)
                        first = (6, 0)[c]
                        vec.tensor_reduce(top[:, j, :, MAX_ROW + 2 * c * HEAD_ROWS:MAX_ROW + (2 * c + 1) * HEAD_ROWS + 1:HEAD_ROWS]
                                          .rearrange("p g h -> p h g"),
                                          psum[:, first:first + 2, :].rearrange("p h (g n) -> p h g n", g=2),
                                          AX.X, ALU.max, negate=True).then_inc(tops_ready, 1)
                for s in range(2):
                    vec.wait_ge(tops_turned, 2 * i + s + 1)
                    at = slice(s * S, (s + 1) * S)
                    vec.tensor_tensor(qT_less[:, :, at], bank[2 + 3 * s].rearrange("p (g t) -> p g t", g=2), qT[:, :, at],
                                      ALU.add).then_inc(q_lessened, 1)
                if more:
                    front(i + 1)
                if not is_first(i):
                    tile_stats(core, vec, i - 1)
                for s in range(2):
                    vec.wait_ge(sums_ready, 2 * i + s + 1)
                    vec.reciprocal(updT[:, s, :], bank[s]).then_inc(sums_inverted, 1)
                    vec.wait_ge(sums_inverted, 2 * i + s + 1)
                    vec.tensor_tensor(updT[:, s, :], heads[:, s, :], updT[:, s, :], ALU.mult).then_inc(updT_ready, 1)
                    if s == 0 and more:
                        copy_k(i + 1)
                if more:
                    copy_qv(i + 1)
                vec.wait_ge(x_biased, i + 1)
                vec.wait_ge(y_ready, i + 1)
                vec.tensor_tensor(x[:, bass.ds(4 * i, PAIR), :], x[:, bass.ds(4 * i, PAIR), :],
                                  bank[3].rearrange("p (j n) -> p j n", j=PAIR), ALU.add).then_inc(y_added, 1)
            turns(vec, PAIRS, body)
            vec.wait_ge(y_added, PAIRS)
            tile_stats(core, vec, PAIRS - 1)

        @block.gpsimd
        def _(pool):
            core.wait_loaded(pool, "xat")
            pool.memset(top[:, :, :, :], 0.0).then_inc(set_up, 1)
            pool.memset(v[:, :, :, :], 1.0).then_inc(set_up, 1)
            pool.tensor_scalar(kmask[:, :], qmask[:, :], 0.0, w["rows"][:, 0:1], ALU.is_equal, ALU.mult).then_inc(set_up, 1)
            pool.wait_ge(set_up, 3)
            pool.tensor_scalar(qmask[:, :], qmask[:, :], w["rows"][:, 1:2], w["rows"][:, 2:3], ALU.mult,
                              ALU.add).then_inc(set_up, 1)
            pool.wait_ge(set_up, 4)


def expert_layer(core, number):
    nc, x, ident, bank = core.nc, core.x, core.ident, core.bank
    w, tables = core.ffn[number], core.moe_tables
    rows_d, outputs_d = core.slots[number], core.outputs[number]
    last = number == 1
    name = f"ffn{number}"
    width, chunk = (F1, P) if last else (F0, F0 // 2)
    chunks = width // chunk
    with ExitStack() as ctx:
        def sb(n, shape, dt=F32):
            return core.sb(ctx, f"{name}_{n}", shape, dt)

        def sem(n):
            return core.layer_sem(f"{name}_{n}")

        st = core.ln_buffers(ctx, f"{name}_ln")
        xn = sb("xn", [P, PAIR, D])
        xnT = sb("xnT", [P, WIDE])
        xn_all = sb("xn_all", [P, K, NT, ROW])
        blank = sb("blank", [P, BLANK, ROW], U32)
        clipped = sb("clipped", [P, 2, WIDE])
        hidden = sb("hidden", [P, 2, WIDE])
        logits = sb("logits", [P, NT, E])
        best = sb("best", [P, NT, K])
        lesser = sb("lesser", [P, PAIR, E])
        equal = sb("equal", [P, PAIR, E])
        first = sb("first", [P, PAIR])
        onehot = sb("onehot", [P, PAIR, K, E])
        picked_b = sb("picked_b", [P, PAIR, E], BF16)
        upto_b = sb("upto_b", [P, P], BF16)
        ones_b = sb("ones_b", [P, P], BF16)
        soft = sb("soft", [P, NT, E + 1])
        denom = sb("denom", [P, NT])
        weight = sb("weight", [P, NT, K])
        in_tile = sb("in_tile", [P, E, PAIR])
        upto = sb("upto", [P, E, PAIR])
        before = sb("before", [P, E, PAIR])
        reached = sb("reached", [P, E])
        slot = sb("slot", [P, PAIR, E])
        slot_sel = sb("slot_sel", [P, PAIR, K, E])
        slot_f = sb("slot_f", [P, PAIR, K])
        slot_i = sb("slot_i", [P, K, NT], U32)
        count = sb("count", [P, E])
        full = sb("full", [P, E, NT])
        tiles = sb("tiles", [P, E])
        tile_end = sb("tile_end", [P, E])
        skipped = sb("skipped", [P, E])
        zero8 = sb("zero8", [P, E])
        past = sb("past", [1, SLOT_TILES, E])
        skips = sb("skips", [1, SLOT_TILES, E])
        owner_f = sb("owner_f", [1, SLOT_TILES])
        column_at = sb("column_at", [1, 2 * (SLOT_TILES + 2 + LANES)], I32)
        row_at_f = sb("row_at_f", [1, SLOT_TILES])
        row_at = sb("row_at", [1, SLOT_TILES], I32)
        pad_at = sb("pad_at", [1, E], I32)
        row = sb("row", [P, LANES, ROW])
        to_row = sb("to_row", [P, LANES], U32)
        rowT = sb("rowT", [P, 2, P])
        h = sb("h", [P, 2, width])
        hT = sb("hT", [chunk, 2, chunks * P])
        zero = sb("zero", [P, 1], U32)
        waited = sb("waited", [P, 1], U32)
        y = sb("y", [P, LANES, D])
        got = sb("got", [P, NT, K, D])

        set_up = sem("set_up")
        rows_named = sem("rows_named")
        xn_ready = sem("xn_ready")
        xn_turned = sem("xn_turned")
        xnT_ready = sem("xnT_ready")
        xn_kept = sem("xn_kept")
        logits_ready = sem("logits_ready")
        logits_kept = sem("logits_kept")
        picks_ready = sem("picks_ready")
        ranks_ready = sem("ranks_ready")
        slots_ready = sem("slots_ready")
        tables_ready = sem("tables_ready")
        gaps_ready = sem("gaps_ready")
        soft_ready = sem("soft_ready")
        rows_placed = sem("rows_placed")
        blank_loaded = sem("blank_loaded")
        blanks_placed = sem("blanks_placed")
        row_loaded = [sem(f"row_loaded{s}") for s in range(LANES)]
        to_row_kept = sem("to_row_kept")
        row_turned = sem("row_turned")
        rowT_ready = sem("rowT_ready")
        gate_ready = sem("gate_ready")
        up_ready = sem("up_ready")
        gate_active = sem("gate_active")
        h_ready = sem("h_ready")
        h_turned = sem("h_turned")
        hT_ready = sem("hT_ready")
        out_ready = sem("out_ready")
        out_copied = sem("out_copied")
        out_stored = [sem(f"out_stored{s}") for s in range(LANES)]
        waits_carried = sem("waits_carried")
        got_loaded = [sem(f"got_loaded{q}") for q in range(PAIRS)]
        combined = sem("combined")
        if last:
            shared_ready = sem("shared_ready")
            shared_clipped = sem("shared_clipped")
            shared_gated = sem("shared_gated")
            shared_hidden = sem("shared_hidden")
            shared_y_ready = sem("shared_y_ready")
            shared_y_added = sem("shared_y_added")
            gate_clipped = sem("gate_clipped")
            x_stored = sem("x_stored")
        spectrum = None if last else KernelSpectrum(core, ctx)
        GATE, UP, HT, TURN, OUT = (0, 1), (2, 3), 4, 5, 6
        block = ctx.enter_context(nc.Block())

        def load_outputs(engine, k):
            for s in range(LANES):
                engine.wait_ge(out_stored[s], 16 * len(range(s, SLOT_TILES, LANES)))
            for q in range(PAIRS):
                at = (k * NT + q * PAIR) * P
                engine.dma_start(got[:, q * PAIR:(q + 1) * PAIR, k, :],
                                 outputs_d[at:at + WIDE, :].rearrange("(t p) d -> p t d", p=P)).then_inc(got_loaded[q], 16)

        def place_blanks(engine, experts):
            engine.wait_ge(tables_ready, 1)
            for e in experts:
                at = engine.value_load(pad_at[0:1, e:e + 1], min_val=e * REGION, max_val=(e + 1) * REGION - P)
                engine.dma_start(rows_d[bass.ds(at, P), :], blank[:, e, :].bitcast(F32)).then_inc(blanks_placed, 16)

        @block.sync
        def _(sp):
            core.clear_last_layer(sp)
            core.wait_loaded(sp, "ffn0")
            sp.dma_start(blank[:, :, :], core.arg["blank"].rearrange("p (n c) -> p n c", c=ROW)).then_inc(blank_loaded, 16)
            sp.wait_ge(blank_loaded, 16)
            sp.dma_start(rows_d[E * REGION:SLOTS, :].rearrange("(n p) c -> p n c", p=P),
                         blank[:, E:BLANK, :].bitcast(F32)).then_inc(blanks_placed, 16)
            place_blanks(sp, range(E // 2))
            sp.wait_ge(blanks_placed, 16 * (E + 1))
            sp.wait_ge(rows_placed, 16 * NT * K)

            def load(n, s):
                wait_tiles(sp, row_turned, n - LANES + 1)
                wait_tiles(sp, to_row_kept, n - LANES + 1)
                at = sp.value_load(row_at[0:1, bass.ds(n, 1)], min_val=0, max_val=SLOTS - P)
                sp.dma_start(row[:, s, :], rows_d[bass.ds(at, P), :]).then_inc(row_loaded[s], 16)

            def step(n, s):
                if is_tile(n + 3):
                    load(n + 3, (s + 3) % LANES)

            for n in range(3):
                load(n, n)
            stream_tiles(sp, SLOT_TILES, step)
            load_outputs(sp, 0)
            if last:
                for q in range(PAIRS):
                    sp.wait_ge(combined, K * PAIR * (q + 1))
                    sp.dma_start(core.out[q * WIDE:(q + 1) * WIDE, :].rearrange("(t p) d -> p t d", p=P),
                                 x[:, q * PAIR:(q + 1) * PAIR, :]).then_inc(x_stored, 16)
                sp.wait_ge(x_stored, 16 * PAIRS)

        @block.tensor
        def _(pe):
            core.wait_loaded(pe, name)
            pe.wait_ge(set_up, 5)

            def turn_x(i):
                wait_last_round(pe, xnT_ready, i)
                pe.wait_ge(xn_ready, 4 * i + 4)
                transpose_tiles(pe, bank[0], lambda j: xn[:, j, :], ident[:, :]).then_inc(xn_turned, 1)

            if spectrum:
                spectrum.tensor(pe)
            turn_x(0)

            def body(i, more):
                pe.wait_ge(xnT_ready, i + 1)
                wait_last_round(pe, logits_kept, i)
                for j in range(PAIR):
                    mm = pe.matmul(bank[1][:, j * E:(j + 1) * E], xnT[:, j * P:(j + 1) * P], w["router"][:, :],
                                   start=True, stop=True)
                mm.then_inc(logits_ready, 1)
                if last:
                    for a in range(2):
                        pe.matmul(bank[2 + a], w["shared_up"][:, a * FS:(a + 1) * FS], xnT[:, :],
                                  start=True, stop=True).then_inc(shared_ready, 1)
                pe.wait_ge(picks_ready, i + 1)
                picks = picked_b[:, :, :].rearrange("p t e -> p (t e)")
                pe.matmul(bank[5][:, 0:PAIR * E], upto_b[:, :], picks, start=True, stop=True)
                pe.matmul(bank[5][:, PAIR * E:2 * PAIR * E], ones_b[:, :], picks, start=True, stop=True).then_inc(ranks_ready, 1)
                if more:
                    turn_x(i + 1)
                if last:
                    pe.wait_ge(shared_hidden, i + 1)
                    wait_last_round(pe, shared_y_added, i)
                    for j in range(PAIR):
                        mm = pe.matmul(bank[4][:, j * P:(j + 1) * P], hidden[:, 0, j * P:(j + 1) * P],
                                       w["shared_down"][:, :], start=True, stop=True)
                    mm.then_inc(shared_y_ready, 1)
            turns(pe, PAIRS, body)
            pe.wait_ge(tables_ready, 1)

            columns = [pe.alloc_register(f"{name}_column{c}") for c in range(2 * LANES)]

            def turn_row(n, s):
                pe.wait_ge(row_loaded[s], lane_count(n, s))
                wait_tiles(pe, rowT_ready, n)
                pe.transpose(bank[TURN][:, 0:P], row[:, s, 0:D], ident[:, :]).then_inc(row_turned, 1)

            def gate_and_up(n, s, at):
                pe.wait_ge(rowT_ready, n + 1)
                wait_tiles(pe, h_ready, n - 1)
                pe.matmul(bank[GATE[s]][:, 0:width], rowT[:, s, :], w["up"][:, bass.ds(at, width)],
                          start=True, stop=True).then_inc(gate_ready, 1)
                pe.matmul(bank[UP[s]][:, 0:width], rowT[:, s, :], w["up"][:, bass.ds(at + width, width)],
                          start=True, stop=True).then_inc(up_ready, 1)

            def turn_h(n, s):
                pe.wait_ge(h_ready, n + 1)
                wait_tiles(pe, hT_ready, n)
                for c in range(chunks):
                    mm = pe.transpose(bank[HT][0:chunk, c * P:(c + 1) * P], h[:, s, c * chunk:(c + 1) * chunk], ident[:, :])
                mm.then_inc(h_turned, 1)

            def down(n, s, at):
                pe.wait_ge(hT_ready, n + 1)
                wait_tiles(pe, out_copied, n)
                for c in range(chunks):
                    mm = pe.matmul(bank[OUT][:, 0:D], hT[:, s, c * P:(c + 1) * P],
                                   w["down"][:, bass.ds(at + c * D, D)],
                                   start=(c == 0), stop=(c == chunks - 1))
                mm.then_inc(out_ready, 1)

            def step(n, s):
                if s == 0:
                    pe.reg_load(columns, column_at[0:1, bass.ds(2 * n, 2 * LANES)])
                if is_tile(n + 1):
                    turn_row(n + 1, (s + 1) % LANES)
                if is_tile(n):
                    gate_and_up(n, s % 2, pe.snap(columns[2 * s], min_val=0, max_val=(E - 1) * 2 * width))
                if is_tile(n - 1):
                    turn_h(n - 1, (s + 1) % 2)
                if is_tile(n - 2):
                    down(n - 2, s % 2, pe.snap(columns[2 * s + 1], min_val=0, max_val=(E - 1) * chunks * D))

            turn_row(0, 0)
            stream_tiles(pe, SLOT_TILES, step)

        @block.scalar
        def _(act):
            core.wait_loaded(act, name)
            core.wait_loaded(act, "ffn0")

            def turned_copy(out, in_):
                if last:
                    return act.activation(out, in_, ACT.Identity, bias=w["beta"][:, 0:1], scale=w["gamma"][:, 0:1])
                return act.activation(out, in_, ACT.Copy)

            act.preload_act_table(ACT.Silu)

            def copy_x(i):
                act.wait_ge(xn_turned, i + 1)
                turned_copy(xnT[:, :], bank[0]).then_inc(xnT_ready, 1)
                for k in range(K):
                    act.activation(xn_all[:, k, bass.ds(4 * i, PAIR), 0:D], xn[:, :, :], ACT.Copy).then_inc(xn_kept, 1)

            copy_x(0)

            def body(i, more):
                if last:
                    act.wait_ge(shared_clipped, i + 1)
                    act.activation(hidden[:, 1, :], clipped[:, 0, :], ACT.Silu).then_inc(shared_gated, 1)
                if more:
                    act.wait_ge(shared_ready if last else logits_ready, 2 * i + 2 if last else i + 1)
                    copy_x(i + 1)
            turns(act, PAIRS, body)
            act.wait_ge(blank_loaded, 16)
            place_blanks(act, range(E // 2, E))
            act.wait_ge(gaps_ready, 1)
            act.activation(soft[:, :, :], soft[:, :, :], ACT.Exp).then_inc(soft_ready, 1)
            act.preload_act_table(ACT.Silu)

            def copy_row(n, s):
                act.wait_ge(row_turned, n + 1)
                wait_tiles(act, up_ready, n - 1)
                turned_copy(rowT[:, s, :], bank[TURN][:, 0:P]).then_inc(rowT_ready, 1)

            def activate(n, s):
                if last:
                    act.wait_ge(gate_clipped, n + 1)
                    act.activation(clipped[:, s, 0:width], clipped[:, s, 0:width], ACT.Silu).then_inc(gate_active, 1)
                else:
                    act.wait_ge(gate_ready, n + 1)
                    wait_tiles(act, h_ready, n - 1)
                    act.activation(clipped[:, s, 0:width], bank[GATE[s]][:, 0:width], ACT.Silu).then_inc(gate_active, 1)

            def copy_h(n, s):
                act.wait_ge(h_turned, n + 1)
                wait_tiles(act, out_ready, n - 1)
                act.activation(hT[:, s, :], bank[HT][0:chunk, 0:chunks * P], ACT.Copy).then_inc(hT_ready, 1)

            def step(n, s):
                if is_tile(n + 1):
                    copy_row(n + 1, (s + 1) % 2)
                if is_tile(n):
                    activate(n, s % 2)
                if is_tile(n - 1):
                    copy_h(n - 1, (s + 1) % 2)

            copy_row(0, 0)
            stream_tiles(act, SLOT_TILES, step)
            load_outputs(act, 1)

        @block.vector
        def _(vec):
            core.wait_loaded(vec, name)
            core.wait_loaded(vec, "ffn0")
            vec.tensor_copy(upto_b[:, :], tables["upto_tile"][:, :]).then_inc(set_up, 1)
            vec.memset(ones_b[:, :], 1.0).then_inc(set_up, 1)
            vec.memset(zero8[:, :], 0.0).then_inc(set_up, 1)
            vec.memset(column_at[:, :], 0).then_inc(set_up, 1)
            vec.tensor_copy(reached[:, :], tables["region_start"][:, :]).then_inc(set_up, 1)
            vec.wait_ge(set_up, 5)
            if spectrum:
                spectrum.copy_kernel(vec)
            moments(core, vec, st, last)
            vec_per = 20

            def start(i):
                wait_last_round(vec, xn_turned, i)
                wait_last_round(vec, xn_kept, K * i)
                for ins in normalize(core, vec, st, i, xn):
                    ins.then_inc(xn_ready, 1)

            start(0)
            if spectrum:
                spectrum.copy_spectrum(vec)

            def body(i, more):
                steps = Steps(core, vec, i, vec_per)

                def do(ins):
                    steps.done(ins)
                    steps.wait()

                tokens = bass.ds(4 * i, PAIR)
                vec.wait_ge(logits_ready, i + 1)
                vec.tensor_copy(logits[:, tokens, :], bank[1][:, 0:PAIR * E].rearrange("p (j e) -> p j e", e=E)
                                ).then_inc(logits_kept, 1)
                vec.wait_ge(logits_kept, i + 1)
                order = tables["order"][:, :].unsqueeze(1).to_broadcast([P, PAIR, E])
                for k, among in enumerate((logits[:, tokens, :], lesser[:, :, :])):
                    do(vec.tensor_reduce(best[:, tokens, k], among, AX.X, ALU.max))
                    do(vec.tensor_tensor(equal[:, :, :], among, best[:, tokens, k:k + 1].to_broadcast([P, PAIR, E]), ALU.is_equal))
                    do(vec.tensor_tensor(equal[:, :, :], equal[:, :, :], order, ALU.mult))
                    do(vec.tensor_reduce(first[:, :], equal[:, :, :], AX.X, ALU.max))
                    do(vec.tensor_tensor(onehot[:, :, k, :], order, first[:, :].unsqueeze(2).to_broadcast([P, PAIR, E]), ALU.is_equal))
                    if k == 0:
                        do(vec.scalar_tensor_tensor(out=lesser[:, :, :], in0=onehot[:, :, 0, :], scalar=-3e38,
                                                    in1=among, op0=ALU.mult, op1=ALU.add))
                vec.tensor_tensor(picked_b[:, :, :], onehot[:, :, 0, :], onehot[:, :, 1, :], ALU.add).then_inc(picks_ready, 1)
                if last:
                    vec.wait_ge(shared_ready, 2 * i + 2)
                    vec.tensor_scalar(clipped[:, 0, :], bank[2], -GATE_LIMIT, GATE_LIMIT, ALU.max,
                                      ALU.min).then_inc(shared_clipped, 1)
                if more:
                    start(i + 1)
                vec.wait_ge(ranks_ready, i + 1)
                do(vec.tensor_copy(in_tile[:, :, :], bank[5][:, PAIR * E:2 * PAIR * E].rearrange("p (t e) -> p e t", e=E)))
                do(vec.tensor_tensor_scan(out=upto[:, :, :].rearrange("p e t -> p (e t)"), data0=tables["not_first"][:, :],
                                          data1=in_tile[:, :, :].rearrange("p e t -> p (e t)"), initial=0.0,
                                          op0=ALU.mult, op1=ALU.add))
                do(vec.tensor_tensor(before[:, :, :], upto[:, :, :], in_tile[:, :, :], ALU.subtract))
                do(vec.tensor_tensor(before[:, :, :], before[:, :, :], reached[:, :].unsqueeze(2).to_broadcast([P, E, PAIR]), ALU.add))
                steps.done(vec.tensor_tensor(reached[:, :], reached[:, :], upto[:, :, PAIR - 1], ALU.add))
                do(vec.tensor_tensor(slot[:, :, :], bank[5][:, 0:PAIR * E].rearrange("p (t e) -> p t e", e=E),
                                     before[:, :, :].rearrange("p e t -> p t e"), ALU.add))
                steps.done(vec.tensor_tensor(slot_sel[:, :, 0, :], onehot[:, :, 0, :], slot[:, :, :], ALU.mult))
                do(vec.tensor_tensor(slot_sel[:, :, 1, :], onehot[:, :, 1, :], slot[:, :, :], ALU.mult))
                do(vec.tensor_reduce(slot_f[:, :, :], slot_sel[:, :, :, :], AX.X, ALU.add))
                vec.tensor_copy(slot_i[:, :, tokens], slot_f[:, :, :].rearrange("p t k -> p k t")).then_inc(slots_ready, 1)
                assert steps.n == vec_per, steps.n
                if last:
                    vec.wait_ge(shared_gated, i + 1)
                    vec.tensor_tensor(hidden[:, 0, :], hidden[:, 1, :], bank[3], ALU.mult).then_inc(shared_hidden, 1)
                    vec.wait_ge(shared_y_ready, i + 1)
                    vec.tensor_tensor(x[:, tokens, :], x[:, tokens, :],
                                      bank[4].rearrange("p (j n) -> p j n", j=PAIR), ALU.add).then_inc(shared_y_added, 1)
            turns(vec, PAIRS, body)
            core.vector_base += PAIRS * vec_per

            sort = Steps(core, vec)

            def do(ins):
                sort.done(ins)
                sort.wait()

            do(vec.tensor_tensor(count[:, :], reached[:, :], tables["region_start"][:, :], ALU.subtract))
            do(vec.tensor_tensor(full[:, :, :], count[:, :].unsqueeze(2).to_broadcast([P, E, NT]),
                                 tables["full_at"][:, :].unsqueeze(1).to_broadcast([P, E, NT]), ALU.is_gt))
            do(vec.tensor_reduce(tiles[:, :], full[:, :, :], AX.X, ALU.add))
            sort.done(vec.tensor_scalar(pad_at[:, :], reached[0:1, :], 1.0, None, ALU.add))
            sort.done(vec.tensor_scalar(skipped[:, :], tiles[:, :], float(-P), float(REGION), ALU.mult, ALU.add))
            do(vec.tensor_tensor_scan(out=tile_end[:, :], data0=tiles[:, :], data1=zero8[:, :], initial=0.0,
                                      op0=ALU.add, op1=ALU.add))
            do(vec.tensor_tensor(past[:, :, :], tile_end[0:1, :].unsqueeze(1).to_broadcast([1, SLOT_TILES, E]),
                                 tables["tile_index"][0:1, :].unsqueeze(2).to_broadcast([1, SLOT_TILES, E]), ALU.is_le))
            sort.done(vec.tensor_tensor(skips[:, :, :], past[:, :, :],
                                        skipped[0:1, :].unsqueeze(1).to_broadcast([1, SLOT_TILES, E]), ALU.mult))
            do(vec.tensor_reduce(owner_f[:, :], past[:, :, :], AX.X, ALU.add))
            steps_at = column_at[:, :].rearrange("o (n c) -> o n c", c=2)
            for c, columns in enumerate((2 * width, chunks * D)):
                sort.done(vec.tensor_scalar(steps_at[:, 2 * c:2 * c + SLOT_TILES, c], owner_f[:, :], float(E - 1),
                                            float(columns), ALU.min, ALU.mult))
            do(vec.tensor_reduce(row_at_f[:, :], skips[:, :, :], AX.X, ALU.add))
            vec.scalar_tensor_tensor(out=row_at[:, :], in0=tables["tile_index"][0:1, :], scalar=float(P), in1=row_at_f[:, :],
                                     op0=ALU.mult, op1=ALU.add).then_inc(tables_ready, 1)
            sort.done(vec.tensor_tensor(soft[:, :, 0:E], logits[:, :, :], best[:, :, 0:1].to_broadcast([P, NT, E]), ALU.subtract))
            sort.wait()
            vec.tensor_tensor(soft[:, :, E:E + 1], best[:, :, 1:2], best[:, :, 0:1], ALU.subtract).then_inc(gaps_ready, 1)
            vec.wait_ge(soft_ready, 1)
            if last:
                do(vec.tensor_scalar(denom[:, :], soft[:, :, E], 1.0, None, ALU.add))
            else:
                do(vec.tensor_reduce(denom[:, :], soft[:, :, 0:E], AX.X, ALU.add))
            do(vec.reciprocal(weight[:, :, 0], denom[:, :]))
            do(vec.tensor_tensor(weight[:, :, 1], soft[:, :, E], weight[:, :, 0], ALU.mult))
            sort.close()

            def step(n, s):
                lane, s = (s + 2) % LANES, s % 2
                if is_tile(n):
                    if last:
                        vec.wait_ge(gate_ready, n + 1)
                        wait_tiles(vec, h_ready, n - 1)
                        vec.tensor_scalar(clipped[:, s, :], bank[GATE[s]], -GATE_LIMIT, GATE_LIMIT, ALU.max,
                                          ALU.min).then_inc(gate_clipped, 1)
                    vec.wait_ge(gate_active, n + 1)
                    vec.wait_ge(up_ready, n + 1)
                    wait_tiles(vec, h_turned, n - 1)
                    vec.tensor_tensor(h[:, s, :], clipped[:, s, 0:width], bank[UP[s]][:, 0:width],
                                      ALU.mult).then_inc(h_ready, 1)
                if is_tile(n - 2):
                    vec.wait_ge(out_ready, n - 1)
                    if is_tile(n - 2 - LANES):
                        vec.wait_ge(out_stored[lane], lane_count(n - 2 - LANES, lane))
                    vec.tensor_copy(y[:, lane, :], bank[OUT][:, 0:D]).then_inc(out_copied, 1)

            stream_tiles(vec, SLOT_TILES, step)
            for t in range(NT):
                if t % PAIR == 0:
                    vec.wait_ge(got_loaded[t // PAIR], 16 * K)
                for k in range(K):
                    if k:
                        vec.wait_ge(combined, K * t + k)
                    vec.scalar_tensor_tensor(out=x[:, t, :], in0=got[:, t, k, :], scalar=weight[:, t, k:k + 1],
                                             in1=x[:, t, :], op0=ALU.mult, op1=ALU.add).then_inc(combined, 1)
                if t % PAIR == PAIR - 1 and not last:
                    vec.wait_ge(combined, K * (t + 1))
                    tile_stats(core, vec, t // PAIR)

        @block.gpsimd
        def _(pool):
            core.wait_loaded(pool, "ffn0")
            pool.tensor_copy(xn_all[:, :, :, D].bitcast(U32), core.output_rows[:, :].rearrange("p (k t) -> p k t", k=K)
                             ).then_inc(rows_named, 1)
            pool.memset(zero[:, :], 0).then_inc(rows_named, 1)
            pool.wait_ge(rows_named, 2)
            for t in range(NT):
                if t % PAIR == 0:
                    i = t // PAIR
                    pool.wait_ge(xn_kept, K * (i + 1))
                    pool.wait_ge(slots_ready, i + 1)
                for k in range(K):
                    pool.indirect_dma_start(out=rows_d, out_offset=bass.IndirectOffsetOnAxis(ap=slot_i[:, k, t:t + 1], axis=0),
                                            in_=xn_all[:, k, t, :], in_offset=None).then_inc(rows_placed, 16)

            def step(n, s):
                if is_tile(n):
                    pool.wait_ge(row_loaded[s], lane_count(n, s))
                    if is_tile(n - LANES):
                        pool.wait_ge(out_stored[s], lane_count(n - LANES, s))
                    pool.tensor_tensor(to_row[:, s:s + 1], row[:, s, D:D + 1].bitcast(U32), zero[:, :], ALU.add
                                       ).then_inc(to_row_kept, 1)
                if is_tile(n - 2):
                    lane = (s + 2) % LANES
                    pool.wait_ge(to_row_kept, n - 1)
                    pool.wait_ge(out_copied, n - 1)
                    wait_tiles(pool, waits_carried, n - 2)
                    pool.tensor_tensor(waited[:, :], zero[:, :], zero[:, :], ALU.add).then_inc(waits_carried, 1)
                    pool.indirect_dma_start(out=outputs_d, out_offset=bass.IndirectOffsetOnAxis(ap=to_row[:, lane:lane + 1], axis=0),
                                            in_=y[:, lane, :], in_offset=None).then_inc(out_stored[lane], 16)

            stream_tiles(pool, SLOT_TILES, step)


def first_expert_layer(core):
    expert_layer(core, 0)


def second_expert_layer(core):
    expert_layer(core, 1)


def load_x(core):
    with ExitStack() as ctx:
        block = ctx.enter_context(core.nc.Block())

        @block.sync
        def _(sp):
            for layer in LOAD_ORDER:
                for buffer, source in core.loads[layer]:
                    sp.dma_start(buffer, source).then_inc(core.loaded[layer], 16)
            for layer in core.loads:
                core.wait_loaded(sp, layer)


def store_x(core, out):
    with ExitStack() as ctx:
        stored = core.sem("stored")
        block = ctx.enter_context(core.nc.Block())

        @block.sync
        def _(sp):
            sp.dma_start(out.rearrange("(t p) d -> p t d", p=P), core.x[:, :, :]).then_inc(stored, 16)
            sp.wait_ge(stored, 16)


LAYERS = [retention_layer, depool_layer, first_expert_layer, conv_layer, cross_attention_layer,
          second_expert_layer]


def decoder_kernel(nc, arg, out, layers=6):
    with ExitStack() as ctx:
        core = Core(nc, ctx, arg)
        core.out = out
        for n, layer in enumerate(LAYERS[:layers]):
            core.start_layer()
            layer(core)
            if layer in (depool_layer, load_x):
                core.early.close()
        if layers < len(LAYERS) or LAYERS[-1] is not second_expert_layer:
            store_x(core, out)


def half_swapped(w):
    return w.reshape(RH, 2, RQK // 2, D)[:, ::-1].reshape(RH * RQK, D)


def constants():
    f64 = np.float64
    c = {"ident": np.eye(P, dtype=np.float32)}
    inv = 1.0 / 10000.0 ** (np.arange(0, RQK, 2, dtype=f64) / RQK)
    ang = (np.arange(S, dtype=np.float32)[None, :] * inv.astype(np.float32)[:, None]).astype(np.float32).astype(f64)
    decay = np.log1p(-np.exp2(-5.0 - np.arange(RH)))
    t = np.arange(S)
    rope = np.zeros((P, 4, S))
    for h in range(RH):
        r = slice(h * RQK, (h + 1) * RQK)
        cos, sin = np.tile(np.cos(ang), (2, 1)), np.concatenate([-np.sin(ang), np.sin(ang)])
        up, down = np.exp(decay[h] * t) * RQK ** -0.5, np.exp(-decay[h] * t)
        rope[r, 0], rope[r, 1], rope[r, 2], rope[r, 3] = cos * up, sin * up, cos * down, sin * down
    c["rope"] = rope.reshape(P, -1).astype(np.float32)
    tri = np.triu(np.ones((P, P)))
    c["causal"] = np.concatenate([tri, np.ones((P, P)), tri], 1).astype(np.float32)
    p = np.arange(P)
    c["index"] = np.stack([p, p + P, p + 1, p + 1 + P, np.where(p > 0, -1.0, 0.0), -np.ones(P)], 1).astype(np.float32)
    c["upto"] = np.concatenate([tri, np.ones((P, P))], 1).astype(np.float32)
    k, t = np.arange(S), np.arange(S)
    phase = 2 * np.pi * np.outer(t, k) / FFT
    dft = np.concatenate([np.cos(phase), -np.sin(phase)], 1)
    dft[:, S] = np.where(t % 2, -1.0, 1.0)
    idft = np.concatenate([2 * np.cos(phase).T, -2 * np.sin(phase).T], 0) / FFT
    idft[0] = 1.0 / FFT
    idft[S] = np.where(t % 2, -1.0, 1.0) / FFT
    c["dft"], c["idft"] = dft.astype(np.float32), idft.astype(np.float32)
    c["time"] = np.tile(np.arange(P, dtype=np.float32), (P, 1))
    c["half"] = np.stack([p < N_STATE, p >= N_STATE], 1).astype(np.float32)
    c["upto_tile"] = c["upto"][:, :P]
    c["order"] = np.tile(E - np.arange(E, dtype=np.float32), (P, 1))
    c["not_first"] = np.tile((np.arange(E * PAIR) % PAIR > 0).astype(np.float32), (P, 1))
    c["full_at"] = np.tile(np.arange(NT, dtype=np.float32) * P, (P, 1))
    c["tile_index"] = np.tile(np.arange(SLOT_TILES, dtype=np.float32), (P, 1))
    c["region_start"] = np.tile(np.arange(E, dtype=np.float32) * REGION - 1, (P, 1))
    c["output_rows"] = (np.arange(K * NT)[None, :] * P + p[:, None]).astype(np.uint32)
    blank = np.zeros((P, BLANK, ROW), np.uint32)
    blank[:, :, D] = (K * NT + np.arange(BLANK)[None, :]) * P + p[:, None]
    c["blank"] = blank.reshape(P, -1)
    c["head_rows"] = (p[:, None] // HEAD_ROWS == np.arange(P // HEAD_ROWS)[None, :]).astype(np.float32)
    row = p % HEAD_ROWS
    c["xat_rows"] = np.stack([np.where(row == MASK_ROW, MASKED, 0.0), row != MASK_ROW, row == MASK_ROW], 1).astype(np.float32)
    c["spread"] = (p[:, None] == HEAD_ROWS * (p[None, :] // HEAD_ROWS) + XD).astype(np.float32)
    c["packed"] = np.stack([p == 0, p > 0], 1).astype(np.float32)
    return c


def by_pair(w):
    return w.reshape(D // 2, 2 * N_STATE).T


def head_padded(w):
    out = np.zeros((w.shape[0], XH, HEAD_ROWS), w.dtype)
    out[:, :, :XD] = w.reshape(-1, XH, XD)
    return out.reshape(w.shape[0], XH * HEAD_ROWS)


def head_column(bias, one_row):
    out = np.zeros((XH, HEAD_ROWS), bias.dtype)
    out[:, :XD] = bias.reshape(XH, XD)
    out[:, one_row] = 1.0
    return out.reshape(2, P).T


def laid_out(inp):
    def cat(*a):
        return np.concatenate(a, 1)
    a = constants()
    a["x"] = inp["x"].reshape(B * S, D)
    wq, wk = inp["L0_attn_Wq"], inp["L0_attn_Wk"]
    a["wqk"] = cat(wq.T, half_swapped(wq).T, wk.T, half_swapped(wk).T)
    a["wvg"] = cat(inp["L0_attn_Wv"].T, inp["L0_attn_Wg"].T)
    a["wo"] = inp["L0_attn_Wo"].T
    a["gnorm"] = np.tile(inp["L0_attn_g_norm_w"], (P, RH))
    a["lens"] = inp["mask_BxS2_if0"]
    a["ctx"] = inp["ctx_2048"].reshape(B * S, DC)
    a["ginit"] = np.tile(inp["L0_xattn_g_init"][:D], (P, 1))
    a["gres"] = inp["L0_xattn_g_res"][:, None]
    a["dep_win"] = inp["L0_xattn_W_in"].T
    a["dep_bin"] = inp["L0_xattn_b_in"][None]
    for name, key in (("alog", "A_log"), ("b", "B"), ("c", "C")):
        a["conv_" + name] = by_pair(inp["L1_attn_" + key])
    a["conv_dt"] = by_pair(np.repeat(inp["L1_attn_dt"][:, None], N_STATE, 1))
    a["conv_skip"] = inp["L1_attn_Dp"][None]
    a["conv_win"], a["conv_wout"] = inp["L1_attn_Win"].T, inp["L1_attn_Wout"].T
    a["conv_bin"], a["conv_bout"] = np.tile(inp["L1_attn_bin_"], (P, 1)), np.tile(inp["L1_attn_bout"], (P, 1))
    for name, layer, router, up, down, width, chunk in (
            ("ffn0", "L0_ffn_", "router_weight", "w1", "w2", F0, F0 // 2),
            ("ffn1", "L1_ffn_", "router_w", "gate_up_w", "down_w", F1, P)):
        a[name + "_router"] = inp[layer + router]
        a[name + "_up"] = inp[layer + up].transpose(1, 0, 2).reshape(D, E * 2 * width)
        a[name + "_down"] = inp[layer + down].reshape(E, width // chunk, chunk, D).transpose(2, 0, 1, 3).reshape(chunk, -1)
    a["ffn1_gamma"], a["ffn1_beta"] = inp["L1_ffn_ln_gamma"][:, None], inp["L1_ffn_ln_beta"][:, None]
    a["ffn1_shared_up"], a["ffn1_shared_down"] = inp["L1_ffn_shared_gate_up_w"], inp["L1_ffn_shared_down_w"]
    a["ctxT"] = inp["ctx_2048"].reshape(B * S, DC).T
    a["mask"] = inp["mask_BxS2_fk1"].reshape(1, B * S)
    wsrc, bsrc = inp["L1_xattn_W_src"].T, inp["L1_xattn_b_src"]
    a["xat_wk"], a["xat_wv"] = head_padded(wsrc[:, :D]), wsrc[:, D:]
    a["xat_wq"] = head_padded(inp["L1_xattn_W_tgt"].T)
    a["xat_kbias"] = head_column(bsrc[:D], MAX_ROW)
    a["xat_qbias"] = head_column(inp["L1_xattn_b_tgt"], MASK_ROW)
    a["xat_bv"] = np.tile(bsrc[D:], (P, 1))
    wout = inp["L1_xattn_W_out"].T
    a["xat_wout"] = np.concatenate([wout[:D], head_padded(wout[D:].T).T], 0)
    a["xat_bout"] = np.tile(inp["L1_xattn_b_out"], (P, 1))
    return {k: np.ascontiguousarray(v) for k, v in a.items()}


def build(nc, arrays, layers=6):
    arg = {k: nc.dram_tensor(f"in_{k}", v.shape, mybir.dt.from_np(v.dtype), kind="ExternalInput").ap()
           for k, v in arrays.items()}
    out = nc.dram_tensor("out_x", (B * S, D), F32, kind="ExternalOutput").ap()
    decoder_kernel(nc, arg, out, layers)


def kernel(**inputs):
    import concourse.bacc as bacc
    from concourse.bass_utils import run_bass_kernel_spmd

    arrays = laid_out({k: np.asarray(v) for k, v in inputs.items()})
    nc = bacc.Bacc("TRN2", target_bir_lowering=False, num_devices=1)
    build(nc, arrays)
    r = run_bass_kernel_spmd(nc, [{f"in_{k}": v for k, v in arrays.items()}], core_ids=[0])
    return r.results[0]["out_x"].reshape(B, S, D)
```
